# Optimizing a Trainium2 kernel written in Bass

```python
import numpy as np
import jax
import jax.numpy as jnp

def _softmax(x, axis=-1):
    return jax.nn.softmax(x, axis=axis)

def _gelu(x):
    return jax.nn.gelu(x, approximate=True)

def _silu(x):
    return jax.nn.silu(x)

def _sigmoid(x):
    return jax.nn.sigmoid(x)

def _layernorm(x, axis=-1, eps=1e-05):
    m = jnp.mean(x, axis=axis, keepdims=True)
    v = jnp.var(x, axis=axis, keepdims=True)
    return (x - m) / jnp.sqrt(v + eps)

def _scatter_add(tgt, idx, src, axis=0):
    return tgt.at[idx].add(src)

def _segment_sum(src, seg, n):
    return jax.ops.segment_sum(src, seg, n)
kernel_name = 'mk_prb_d2_jaxref_r8_e4c36c'

def setup_inputs(seed: int=0):
    np.random.seed(seed)
    _w = jnp.asarray

    def _L0_attn_setup():
        import jax, jax.numpy as jnp
        import numpy as np
        D_MODEL = 128
        D_FF = 512
        FFN_H = int(2 * D_FF / 3)
        B, S = (4, 512)
        LN_EPS = 1e-05
        ATTN_EPS = 1e-06

        def layer_norm(x, g, b):
            mu = jnp.mean(x, axis=-1, keepdims=True)
            var = jnp.mean(jnp.square(x - mu), axis=-1, keepdims=True)
            return (x - mu) * jax.lax.rsqrt(var + LN_EPS) * g + b
        key = jax.random.key(seed)
        ks = jax.random.split(key, 16)
        s = 0.02
        return {'x': jax.random.normal(ks[0], (B, S, D_MODEL), dtype=jnp.float32), 'Wqkv': jax.random.normal(ks[1], (D_MODEL, 3 * D_MODEL), dtype=jnp.float32) * s, 'bqkv': jnp.zeros((3 * D_MODEL,), jnp.float32), 'Wg': jax.random.normal(ks[2], (D_MODEL, FFN_H), dtype=jnp.float32) * s, 'bg': jnp.zeros((FFN_H,), jnp.float32), 'Wu': jax.random.normal(ks[3], (D_MODEL, FFN_H), dtype=jnp.float32) * s, 'bu': jnp.zeros((FFN_H,), jnp.float32), 'Wd': jax.random.normal(ks[4], (FFN_H, D_MODEL), dtype=jnp.float32) * s, 'bd': jnp.zeros((D_MODEL,), jnp.float32), 'g1': jnp.ones((D_MODEL,), jnp.float32), 'b1': jnp.zeros((D_MODEL,), jnp.float32), 'g2': jnp.ones((D_MODEL,), jnp.float32), 'b2': jnp.zeros((D_MODEL,), jnp.float32)}
    _L0_attn_in = _L0_attn_setup()

    def _L0_ffn_setup():
        import jax, jax.numpy as jnp
        import numpy as np
        NUM_EXPERTS = 8
        HIDDEN = 128
        FFN = 512
        BATCH = 2
        SEQ = 256
        key = jax.random.key(seed)
        k_x, k_g, k_u, k_d = jax.random.split(key, 4)
        scale_in = 1.0 / np.sqrt(HIDDEN)
        scale_mid = 1.0 / np.sqrt(FFN)
        return {'hidden_states': jax.random.normal(k_x, (BATCH, SEQ, HIDDEN), dtype=jnp.float32), 'Wg': jax.random.normal(k_g, (NUM_EXPERTS, HIDDEN, FFN), dtype=jnp.float32) * scale_in, 'Wu': jax.random.normal(k_u, (NUM_EXPERTS, HIDDEN, FFN), dtype=jnp.float32) * scale_in, 'Wd': jax.random.normal(k_d, (NUM_EXPERTS, FFN, HIDDEN), dtype=jnp.float32) * scale_mid}
    _L0_ffn_in = _L0_ffn_setup()

    def _L1_attn_setup():
        import jax, jax.numpy as jnp
        import numpy as np
        L, E, H = (4, 128, 16)
        HD = E // H
        EPS_LN = 1e-05

        def _layernorm(x, w, b):
            m = jnp.mean(x, axis=-1, keepdims=True)
            v = jnp.mean((x - m) ** 2, axis=-1, keepdims=True)
            return (x - m) / jnp.sqrt(v + EPS_LN) * w + b

        def _to_quaternion(x):
            p1 = jnp.diff(x, axis=1, prepend=x[:, :1])
            p2 = jnp.roll(x, 1, axis=2)
            p3 = jnp.cos(x)
            return jnp.stack([x, p1, p2, p3], axis=-1)

        def _hamilton(a, b):
            a0, a1, a2, a3 = (a[..., 0], a[..., 1], a[..., 2], a[..., 3])
            b0, b1, b2, b3 = (b[..., 0], b[..., 1], b[..., 2], b[..., 3])
            return jnp.stack([a0 * b0 - a1 * b1 - a2 * b2 - a3 * b3, a0 * b1 + a1 * b0 + a2 * b3 - a3 * b2, a0 * b2 - a1 * b3 + a2 * b0 + a3 * b1, a0 * b3 + a1 * b2 - a2 * b1 + a3 * b0], axis=-1)

        def _spectral_filter(S):
            ks = jnp.fft.fftfreq(S).astype(jnp.float32)[:, None, None]
            kh = jnp.fft.fftfreq(H).astype(jnp.float32)[None, :, None]
            kd = jnp.fft.fftfreq(HD).astype(jnp.float32)[None, None, :]
            km = jnp.sqrt(ks ** 2 + kh ** 2 + kd ** 2 + 1e-10)
            f = jnp.exp(1j * jnp.arctan(jnp.log(km + 1e-10)))
            return f[None, :, :, :, None].astype(jnp.complex64)

        def _modulation(S):
            lam = jnp.arange(S, dtype=jnp.float32) / S
            t = jnp.arange(S, dtype=jnp.float32) * 0.1
            probe = jnp.sin(t + lam)
            phase = t - 2.0 * lam + 0.5 * lam ** 2
            return (probe * jnp.cos(phase))[None, :, None, None]

        def _attention(x, aw, ab, pw, pb):
            B, S, _ = x.shape
            qkv = (x @ aw + ab).reshape(B, S, H, 3 * HD)
            q, k, v = jnp.split(qkv, 3, axis=-1)
            qk = _hamilton(_to_quaternion(q), _to_quaternion(k))
            qkv_p = _hamilton(qk, _to_quaternion(v))
            f = jnp.fft.fftn(qkv_p.astype(jnp.complex64), axes=(-3, -2))
            out = jnp.fft.ifftn(f * _spectral_filter(S), axes=(-3, -2)).real
            a = out[..., 0] * (1.0 + 0.1 * _modulation(S))
            return a.reshape(B, S, E) @ pw + pb

        def _layer(x, p):
            ln1w, ln1b, aw, ab, pw, pb, ln2w, ln2b, fw, fb, mw, mb = p
            x = x + _attention(_layernorm(x, ln1w, ln1b), aw, ab, pw, pb)
            h = _layernorm(x, ln2w, ln2b)
            h = jax.nn.gelu(h @ fw + fb, approximate=False) @ mw + mb
            return x + h
        key = jax.random.key(seed)
        ks = jax.random.split(key, 6)
        s = 0.02
        return {'x': jax.random.normal(ks[0], (2, 256, E), jnp.float32), 'ln1_w': jnp.ones((L, E), jnp.float32), 'ln1_b': jnp.zeros((L, E), jnp.float32), 'attn_w': jax.random.normal(ks[1], (L, E, 3 * E), jnp.float32) * s, 'attn_b': jnp.zeros((L, 3 * E), jnp.float32), 'aproj_w': jax.random.normal(ks[2], (L, E, E), jnp.float32) * s, 'aproj_b': jnp.zeros((L, E), jnp.float32), 'ln2_w': jnp.ones((L, E), jnp.float32), 'ln2_b': jnp.zeros((L, E), jnp.float32), 'fc_w': jax.random.normal(ks[3], (L, E, 4 * E), jnp.float32) * s, 'fc_b': jnp.zeros((L, 4 * E), jnp.float32), 'mproj_w': jax.random.normal(ks[4], (L, 4 * E, E), jnp.float32) * s, 'mproj_b': jnp.zeros((L, E), jnp.float32)}
    _L1_attn_in = _L1_attn_setup()

    def _L1_ffn_setup():
        import jax, jax.numpy as jnp
        import numpy as np
        E, K = (8, 2)
        key = jax.random.key(seed)
        ks = jax.random.split(key, 5)
        B, S, H, I = (2, 128, 128, 512)
        scale_h = 1.0 / np.sqrt(H)
        scale_i = 1.0 / np.sqrt(I)
        return {'hidden_states': jax.random.normal(ks[0], (B, S, H), jnp.float32), 'conf_w': jax.random.normal(ks[1], (E, H), jnp.float32) * 0.1 * scale_h, 'conf_b': jnp.zeros((E,), jnp.float32), 'gate_w': jax.random.normal(ks[2], (E, I, H), jnp.float32) * scale_h, 'up_w': jax.random.normal(ks[3], (E, I, H), jnp.float32) * scale_h, 'down_w': jax.random.normal(ks[4], (E, H, I), jnp.float32) * scale_i, 'wealth': jnp.ones((E,), jnp.float32)}
    _L1_ffn_in = _L1_ffn_setup()
    _d = {'L0_attn_x': _L0_attn_in['x'], 'L0_attn_Wqkv': _L0_attn_in['Wqkv'], 'L0_attn_bqkv': _L0_attn_in['bqkv'], 'L0_attn_Wg': _L0_attn_in['Wg'], 'L0_attn_bg': _L0_attn_in['bg'], 'L0_attn_Wu': _L0_attn_in['Wu'], 'L0_attn_bu': _L0_attn_in['bu'], 'L0_attn_Wd': _L0_attn_in['Wd'], 'L0_attn_bd': _L0_attn_in['bd'], 'L0_attn_g1': _L0_attn_in['g1'], 'L0_attn_b1': _L0_attn_in['b1'], 'L0_attn_g2': _L0_attn_in['g2'], 'L0_attn_b2': _L0_attn_in['b2'], 'L0_ffn_Wg': _L0_ffn_in['Wg'], 'L0_ffn_Wu': _L0_ffn_in['Wu'], 'L0_ffn_Wd': _L0_ffn_in['Wd'], 'L1_attn_ln1_w': _L1_attn_in['ln1_w'], 'L1_attn_ln1_b': _L1_attn_in['ln1_b'], 'L1_attn_attn_w': _L1_attn_in['attn_w'], 'L1_attn_attn_b': _L1_attn_in['attn_b'], 'L1_attn_aproj_w': _L1_attn_in['aproj_w'], 'L1_attn_aproj_b': _L1_attn_in['aproj_b'], 'L1_attn_ln2_w': _L1_attn_in['ln2_w'], 'L1_attn_ln2_b': _L1_attn_in['ln2_b'], 'L1_attn_fc_w': _L1_attn_in['fc_w'], 'L1_attn_fc_b': _L1_attn_in['fc_b'], 'L1_attn_mproj_w': _L1_attn_in['mproj_w'], 'L1_attn_mproj_b': _L1_attn_in['mproj_b'], 'L1_ffn_conf_w': _L1_ffn_in['conf_w'], 'L1_ffn_conf_b': _L1_ffn_in['conf_b'], 'L1_ffn_gate_w': _L1_ffn_in['gate_w'], 'L1_ffn_up_w': _L1_ffn_in['up_w'], 'L1_ffn_down_w': _L1_ffn_in['down_w'], 'L1_ffn_wealth': _L1_ffn_in['wealth']}
    _x0 = _d['L0_attn_x']
    _d['L0_attn_x'] = jax.random.normal(jax.random.fold_in(jax.random.key(seed), 1), (4, 1024, 128), dtype=_x0.dtype)
    del _x0
    return _d

def reference(L0_attn_x, L0_attn_Wqkv, L0_attn_bqkv, L0_attn_Wg, L0_attn_bg, L0_attn_Wu, L0_attn_bu, L0_attn_Wd, L0_attn_bd, L0_attn_g1, L0_attn_b1, L0_attn_g2, L0_attn_b2, L0_ffn_Wg, L0_ffn_Wu, L0_ffn_Wd, L1_attn_ln1_w, L1_attn_ln1_b, L1_attn_attn_w, L1_attn_attn_b, L1_attn_aproj_w, L1_attn_aproj_b, L1_attn_ln2_w, L1_attn_ln2_b, L1_attn_fc_w, L1_attn_fc_b, L1_attn_mproj_w, L1_attn_mproj_b, L1_ffn_conf_w, L1_ffn_conf_b, L1_ffn_gate_w, L1_ffn_up_w, L1_ffn_down_w, L1_ffn_wealth):

    def _L0_attn_ref(x, Wqkv, bqkv, Wg, bg, Wu, bu, Wd, bd, g1, b1, g2, b2):
        import jax, jax.numpy as jnp
        import numpy as np
        D_MODEL = 128
        D_FF = 512
        FFN_H = int(2 * D_FF / 3)
        B, S = (4, 512)
        LN_EPS = 1e-05
        ATTN_EPS = 1e-06

        def layer_norm(x, g, b):
            mu = jnp.mean(x, axis=-1, keepdims=True)
            var = jnp.mean(jnp.square(x - mu), axis=-1, keepdims=True)
            return (x - mu) * jax.lax.rsqrt(var + LN_EPS) * g + b
        qkv = jnp.einsum('bsd,de->bse', x, Wqkv) + bqkv
        q, k, v = jnp.split(qkv, 3, axis=-1)
        qp = jax.nn.elu(q) + 1.0
        kp = jax.nn.elu(k) + 1.0
        kv = jnp.einsum('bsd,bse->bde', kp, v)
        num = jnp.einsum('bsd,bde->bse', qp, kv)
        k_sum = jnp.sum(kp, axis=1)
        den = jnp.einsum('bsd,bd->bs', qp, k_sum)[..., None]
        attn = num / (den + ATTN_EPS)
        x = layer_norm(x + attn, g1, b1)
        gate = jnp.einsum('bsd,dh->bsh', x, Wg) + bg
        up = jnp.einsum('bsd,dh->bsh', x, Wu) + bu
        ffn = jnp.einsum('bsh,hd->bsd', jax.nn.silu(gate) * up, Wd) + bd
        return layer_norm(x + ffn, g2, b2)

    def _L0_ffn_ref(hidden_states, Wg, Wu, Wd):
        import jax, jax.numpy as jnp
        import numpy as np
        NUM_EXPERTS = 8
        HIDDEN = 128
        FFN = 512
        BATCH = 2
        SEQ = 256
        B, S, H = hidden_states.shape
        x = hidden_states.reshape(-1, H)

        def expert_step(acc, w):
            wg, wu, wd = w
            h = jax.nn.silu(x @ wg) * (x @ wu)
            return (acc + h @ wd, None)
        acc, _ = jax.lax.scan(expert_step, jnp.zeros_like(x), (Wg, Wu, Wd))
        return acc.reshape(B, S, H)

    def _L1_attn_ref(x, ln1_w, ln1_b, attn_w, attn_b, aproj_w, aproj_b, ln2_w, ln2_b, fc_w, fc_b, mproj_w, mproj_b):
        import jax, jax.numpy as jnp
        import numpy as np
        L, E, H = (4, 128, 16)
        HD = E // H
        EPS_LN = 1e-05

        def _layernorm(x, w, b):
            m = jnp.mean(x, axis=-1, keepdims=True)
            v = jnp.mean((x - m) ** 2, axis=-1, keepdims=True)
            return (x - m) / jnp.sqrt(v + EPS_LN) * w + b

        def _to_quaternion(x):
            p1 = jnp.diff(x, axis=1, prepend=x[:, :1])
            p2 = jnp.roll(x, 1, axis=2)
            p3 = jnp.cos(x)
            return jnp.stack([x, p1, p2, p3], axis=-1)

        def _hamilton(a, b):
            a0, a1, a2, a3 = (a[..., 0], a[..., 1], a[..., 2], a[..., 3])
            b0, b1, b2, b3 = (b[..., 0], b[..., 1], b[..., 2], b[..., 3])
            return jnp.stack([a0 * b0 - a1 * b1 - a2 * b2 - a3 * b3, a0 * b1 + a1 * b0 + a2 * b3 - a3 * b2, a0 * b2 - a1 * b3 + a2 * b0 + a3 * b1, a0 * b3 + a1 * b2 - a2 * b1 + a3 * b0], axis=-1)

        def _spectral_filter(S):
            ks = jnp.fft.fftfreq(S).astype(jnp.float32)[:, None, None]
            kh = jnp.fft.fftfreq(H).astype(jnp.float32)[None, :, None]
            kd = jnp.fft.fftfreq(HD).astype(jnp.float32)[None, None, :]
            km = jnp.sqrt(ks ** 2 + kh ** 2 + kd ** 2 + 1e-10)
            f = jnp.exp(1j * jnp.arctan(jnp.log(km + 1e-10)))
            return f[None, :, :, :, None].astype(jnp.complex64)

        def _modulation(S):
            lam = jnp.arange(S, dtype=jnp.float32) / S
            t = jnp.arange(S, dtype=jnp.float32) * 0.1
            probe = jnp.sin(t + lam)
            phase = t - 2.0 * lam + 0.5 * lam ** 2
            return (probe * jnp.cos(phase))[None, :, None, None]

        def _attention(x, aw, ab, pw, pb):
            B, S, _ = x.shape
            qkv = (x @ aw + ab).reshape(B, S, H, 3 * HD)
            q, k, v = jnp.split(qkv, 3, axis=-1)
            qk = _hamilton(_to_quaternion(q), _to_quaternion(k))
            qkv_p = _hamilton(qk, _to_quaternion(v))
            f = jnp.fft.fftn(qkv_p.astype(jnp.complex64), axes=(-3, -2))
            out = jnp.fft.ifftn(f * _spectral_filter(S), axes=(-3, -2)).real
            a = out[..., 0] * (1.0 + 0.1 * _modulation(S))
            return a.reshape(B, S, E) @ pw + pb

        def _layer(x, p):
            ln1w, ln1b, aw, ab, pw, pb, ln2w, ln2b, fw, fb, mw, mb = p
            x = x + _attention(_layernorm(x, ln1w, ln1b), aw, ab, pw, pb)
            h = _layernorm(x, ln2w, ln2b)
            h = jax.nn.gelu(h @ fw + fb, approximate=False) @ mw + mb
            return x + h
        for i in range(L):
            x = _layer(x, (ln1_w[i], ln1_b[i], attn_w[i], attn_b[i], aproj_w[i], aproj_b[i], ln2_w[i], ln2_b[i], fc_w[i], fc_b[i], mproj_w[i], mproj_b[i]))
        return x

    def _L1_ffn_ref(hidden_states, conf_w, conf_b, gate_w, up_w, down_w, wealth):
        import jax, jax.numpy as jnp
        import numpy as np
        E, K = (8, 2)
        x = hidden_states
        confidences = jax.nn.sigmoid(jnp.einsum('bsh,eh->bse', x, conf_w) + conf_b)
        bids = confidences * wealth
        top_bids, selected_experts = jax.lax.top_k(bids, K)
        sorted_bids = -jnp.sort(-bids, axis=-1)
        payments = jnp.broadcast_to(sorted_bids[..., K:K + 1], top_bids.shape)
        routing_weights = jax.nn.softmax(top_bids, axis=-1)
        combine = jnp.sum(jax.nn.one_hot(selected_experts, E, dtype=x.dtype) * routing_weights[..., None], axis=2)

        def ffn(gw, uw, dw):
            g = jnp.einsum('bsh,ih->bsi', x, gw)
            u = jnp.einsum('bsh,ih->bsi', x, uw)
            return jnp.einsum('bsi,hi->bsh', jax.nn.silu(g) * u, dw)
        expert_out = jax.vmap(ffn)(gate_w, up_w, down_w)
        output = jnp.einsum('ebsh,bse->bsh', expert_out, combine)
        return output
    x = L0_attn_x
    xn = _layernorm(x, axis=-1)
    x = x + _L0_attn_ref(xn, L0_attn_Wqkv, L0_attn_bqkv, L0_attn_Wg, L0_attn_bg, L0_attn_Wu, L0_attn_bu, L0_attn_Wd, L0_attn_bd, L0_attn_g1, L0_attn_b1, L0_attn_g2, L0_attn_b2) + _L0_ffn_ref(xn, L0_ffn_Wg, L0_ffn_Wu, L0_ffn_Wd)
    xn = _layernorm(x, axis=-1)
    x = x + _L1_attn_ref(xn, L1_attn_ln1_w, L1_attn_ln1_b, L1_attn_attn_w, L1_attn_attn_b, L1_attn_aproj_w, L1_attn_aproj_b, L1_attn_ln2_w, L1_attn_ln2_b, L1_attn_fc_w, L1_attn_fc_b, L1_attn_mproj_w, L1_attn_mproj_b) + _L1_ffn_ref(xn, L1_ffn_conf_w, L1_ffn_conf_b, L1_ffn_gate_w, L1_ffn_up_w, L1_ffn_down_w, L1_ffn_wealth)
    return x

_drawn_inputs = setup_inputs


def setup_inputs(seed=0):
    import zlib

    import numpy as np

    out = dict(_drawn_inputs(seed))
    spreads = {'L0_attn_bqkv': (0.0, 0.1),
     'L0_attn_bg': (0.0, 0.8),
     'L0_attn_bu': (0.0, 0.8),
     'L0_attn_bd': (0.0, 0.8),
     'L0_attn_g1': (1.0, 0.2),
     'L0_attn_b1': (0.0, 0.1),
     'L0_attn_g2': (1.0, 0.2),
     'L0_attn_b2': (0.0, 0.1),
     'L1_attn_ln1_w': (1.0, 0.6),
     'L1_attn_ln1_b': (0.0, 0.8),
     'L1_attn_attn_b': (0.0, 0.449),
     'L1_attn_aproj_b': (0.0, 0.1),
     'L1_attn_ln2_w': (1.0, 0.6),
     'L1_attn_ln2_b': (0.0, 0.8),
     'L1_attn_fc_b': (0.0, 0.562),
     'L1_attn_mproj_b': (0.0, 0.1),
     'L1_ffn_conf_b': (0.0, 0.1),
     'L1_ffn_wealth': (1.0, 0.2)}
    factors = {'L0_attn_Wqkv': 8.0, 'L0_attn_Wg': 8.0, 'L0_attn_Wu': 8.0, 'L0_attn_Wd': 8.0}
    for name, (base, spread) in spreads.items():
        noise = np.random.default_rng([zlib.crc32(name.encode()), seed]).standard_normal(out[name].shape)
        drawn = base * np.exp(spread * noise) if base else spread * noise
        out[name] = jnp.asarray(drawn.astype(out[name].dtype))
    for name, factor in factors.items():
        out[name] = (out[name] * factor).astype(out[name].dtype)
    return out
```

```python
from contextlib import ExitStack

import numpy as np

import concourse.bass as bass
from concourse import mybir

F32 = mybir.dt.float32
F32R = mybir.dt.float32r
ALU = mybir.AluOpType
ACT = mybir.ActivationFunctionType
AX = mybir.AxisListType

P = 128
TOK = 4096
TILE = 512
GROUPS = TILE // P
SEQ = 1024
BATCHES = TOK // SEQ
HALVES = SEQ // TILE
TILES = TOK // TILE
EXPERTS = 8
FF = 512
CHUNKS = FF // P
H0 = 341
H0_ROWS = [min(P, H0 - P * c) for c in range(3)]
LAYERS = 4
PER_LAYER = EXPERTS // LAYERS
EPS = 1e-5
ATTN_EPS = 1e-6
ROUND = 12582912.0
TURN = 6.283185


def kernel_program(nc, A):
    with ExitStack() as whole:
        def sem_of(ctx):
            return lambda name: ctx.enter_context(nc.semaphore(name))

        def sb_of(ctx):
            return lambda name, shape, dt=F32: ctx.enter_context(nc.sbuf_tensor(name, shape, dt))

        sb = sb_of(whole)
        X = sb("X", [P, TOK])
        ident = sb("ident", [P, P])
        centre = sb("centre", [P, P])
        mean_col = sb("mean_col", [P, 1])
        pick = sb("pick", [2 * GROUPS, GROUPS, P], F32R)
        power_half = sb("power_half", [P, GROUPS])
        power_one = sb("power_one", [P, GROUPS])
        ones = sb("ones", [P, GROUPS])
        eps_col = sb("eps_col", [P, 1])
        attn_eps_col = sb("attn_eps_col", [P, 1])
        banks = [whole.enter_context(nc.psum_tensor(f"bank{i}", [P, TILE], F32)) for i in range(8)]

        XC = sb("XC", [P, TILE])
        SQ = sb("SQ", [P, TILE])
        XS = sb("XS", [P, TILE])
        HI = sb("HI", [P, TILE], F32R)
        LO = sb("LO", [P, TILE], F32R)
        VAR = sb("VAR", [P, GROUPS])
        RSTD = sb("RSTD", [P, GROUPS])
        RHL = sb("RHL", [P, 2 * GROUPS])
        RT = sb("RT", [2 * GROUPS, P], F32R)
        S = sb("S", [P, 2, TILE])
        H = sb("H", [P, 2, TILE])

        LNB = banks[5]

        def split3(pe, out, w_hi, w_lo, x_hi, x_lo):
            pe.matmul(out, w_hi, x_hi, start=True, stop=False)
            pe.matmul(out, w_lo, x_hi, start=False, stop=False)
            return pe.matmul(out, w_hi, x_lo, start=False, stop=True)

        class PerToken:

            def __init__(self, sem, per_pass):
                self.per = per_pass
                self.source_done = sem("source_done")
                self.copied = sem("copied")
                self.sums_done = sem("sums_done")
                self.var_copied = sem("var_copied")
                self.power_step = sem("power_step")
                self.turned = sem("turned")
                self.rows_copied = sem("rows_copied")
                self.spread = sem("spread")
                self.scaled = sem("scaled")
                self.hi_done = sem("hi_done")
                self.lo_done = sem("lo_done")

            def at(self, it, n, each=1):
                return it * (self.per * each) + n * each

        def pe_sums(pe, ps, it, n, lhs, col):
            pe.wait_ge(ps.copied, ps.at(it, n + 1))
            for g in range(GROUPS):
                mm = pe.matmul(LNB[:, g:g + 1], lhs[:, g * P:(g + 1) * P], col, start=True, stop=True)
            mm.then_inc(ps.sums_done, 1)

        def act_var(act, ps, it, n, eps_col):
            act.wait_ge(ps.sums_done, ps.at(it, n + 1))
            act.wait_ge(ps.power_step, ps.at(it, n, 3))
            act.activation(VAR[:], LNB[:, 0:GROUPS], ACT.Identity, bias=eps_col).then_inc(ps.var_copied, 1)

        def pool_power(pool, ps, it, n, power):
            pool.wait_ge(ps.var_copied, ps.at(it, n + 1))
            pool.wait_ge(ps.turned, ps.at(it, n))
            pool.wait_ge(ps.power_step, ps.at(it, n, 3))
            pool.tensor_tensor(RSTD[:], VAR[:], power[:], ALU.pow).then_inc(ps.power_step, 1)
            pool.wait_ge(ps.power_step, ps.at(it, n, 3) + 1)
            pool.tensor_tensor(RHL[:, 0:GROUPS].bitcast(F32R), RSTD[:], ones[:], ALU.mult).then_inc(ps.power_step, 1)
            pool.wait_ge(ps.power_step, ps.at(it, n, 3) + 2)
            pool.tensor_tensor(RHL[:, GROUPS:].bitcast(F32R), RSTD[:], RHL[:, 0:GROUPS],
                               ALU.subtract).then_inc(ps.power_step, 1)

        def pe_turn(pe, ps, it, n):
            pe.wait_ge(ps.power_step, ps.at(it, n + 1, 3))
            pe.transpose(LNB[0:2 * GROUPS, P:2 * P], RHL[:], ident[:]).then_inc(ps.turned, 1)

        def act_rows(act, ps, it, n):
            act.wait_ge(ps.turned, ps.at(it, n + 1))
            act.wait_ge(ps.spread, ps.at(it, n))
            act.activation(RT[:], LNB[0:2 * GROUPS, P:2 * P], ACT.Copy).then_inc(ps.rows_copied, 1)

        def pe_spread(pe, ps, it, n):
            pe.wait_ge(ps.rows_copied, ps.at(it, n + 1))
            for g in range(GROUPS):
                mm = pe.matmul(LNB[:, g * P:(g + 1) * P], pick[:, g, :], RT[:], start=True, stop=True)
            mm.then_inc(ps.spread, 1)

        def act_centred(act, ps, it, n):
            act.wait_ge(ps.source_done, ps.at(it, n + 1))
            act.wait_ge(ps.scaled, ps.at(it, n))
            act.activation(XC[:], LNB[:], ACT.Copy)
            act.wait_ge(ps.sums_done, ps.at(it, n))
            act.activation(SQ[:], LNB[:], ACT.Square).then_inc(ps.copied, 1)

        def setup(sem, pick_raw, block):
            loaded, made = sem("const_loaded"), sem("const_made")

            @block.sync
            def _(sp):
                for dst, src in ((ident, A["c_ident"]), (centre, A["c_centre"]), (pick_raw, A["c_pick"])):
                    sp.dma_start(dst[:], src).then_inc(loaded, 16)
                sp.dma_start(X[:], A["xT"]).then_inc(loaded, 16)
                sp.wait_ge(loaded, 64)

            @block.vector
            def _(dve):
                dve.memset(mean_col[:], 1.0 / P)
                dve.memset(ones[:], 1.0)
                dve.memset(eps_col[:], EPS)
                dve.memset(attn_eps_col[:], ATTN_EPS)
                dve.memset(power_half[:], -0.5)
                dve.memset(power_one[:], -1.0).then_inc(made, 1)
                dve.wait_ge(loaded, 64)
                dve.tensor_copy(pick[:], pick_raw[:]).then_inc(made, 1)
                dve.wait_ge(made, 2)

        with ExitStack() as ctx:
            setup(sem_of(ctx), sb_of(ctx)("pick_raw", [2 * GROUPS, GROUPS, P]), ctx.enter_context(nc.Block()))

        with ExitStack() as ctx:
            sem, sb = sem_of(ctx), sb_of(ctx)
            first_layer(nc, A, sem, sb, ctx, locals())

        Z = whole.enter_context(nc.sbuf_tensor("Z", [P, TOK], F32))
        XH = whole.enter_context(nc.sbuf_tensor("XH", [P, TOK], F32R))
        XL = whole.enter_context(nc.sbuf_tensor("XL", [P, TOK], F32R))
        combine = nc.dram_tensor("combine", (EXPERTS, TOK), F32, kind="Internal").ap()
        with ExitStack() as ctx:
            sem, sb = sem_of(ctx), sb_of(ctx)
            routing(nc, A, sem, sb, ctx, locals())
        with ExitStack() as ctx:
            sem, sb = sem_of(ctx), sb_of(ctx)
            second_layer(nc, A, sem, sb, ctx, locals())


def first_layer(nc, A, sem, sb, ctx, g):
    X, ident, centre, mean_col = g["X"], g["ident"], g["centre"], g["mean_col"]
    banks, LNB, XC, SQ, XS, HI, LO, S, H = (g[k] for k in ("banks", "LNB", "XC", "SQ", "XS", "HI", "LO", "S", "H"))
    split3, PerToken = g["split3"], g["PerToken"]
    pe_sums, act_var, pool_power, pe_turn, act_rows, pe_spread, act_centred = (
        g[k] for k in ("pe_sums", "act_var", "pool_power", "pe_turn", "act_rows", "pe_spread", "act_centred"))
    power_half, power_one, eps_col, attn_eps_col = (
        g[k] for k in ("power_half", "power_one", "eps_col", "attn_eps_col"))

    GUH = sb("GUH", [P, EXPERTS, 2 * FF], F32R)
    GUL = sb("GUL", [P, EXPERTS, 2 * FF], F32R)
    WD = sb("WD", [P, EXPERTS, CHUNKS, P])
    raw = sb("raw0", [P, 2, 2 * FF])
    AW = 3 * P + 2 * H0
    attn_raw = sb("attn_raw", [P, AW])
    AH = sb("AH", [P, AW], F32R)
    AL = sb("AL", [P, AW], F32R)
    WDA = sb("WDA", [P, 3, P])
    kv_bias = sb("kv_bias", [P, 2 * P])
    cols = sb("cols0", [P, 16])
    BQ, BG, BU, BD, G1, B1, G2, B2 = 0, 1, 4, 7, 8, 9, 10, 11
    XN = sb("XN", [P, HALVES, TILE])
    NH = sb("NH", [P, HALVES, TILE], F32R)
    NL = sb("NL", [P, HALVES, TILE], F32R)
    KV = sb("KV", [P, HALVES * GROUPS, 2 * P + 2])
    KE = sb("KE", [P, GROUPS, P])
    KVS = sb("KVS", [P, P + 2])
    QB = sb("QB", [P, TILE])
    QE = sb("QE", [P, TILE])
    QP = sb("QP", [P, TILE])
    Y = sb("Y", [P, TILE])
    X1 = sb("X1", [P, TILE])
    S2 = sb("S2", [P, TILE])
    H2 = sb("H2", [P, 3, TILE])
    GX = sb("GX", [P, HALVES, TILE])

    STEPS = HALVES * EXPERTS * CHUNKS
    PT = 4 * HALVES
    ps = PerToken(sem, PT)
    small_loaded, wd_loaded = sem("small_loaded"), sem("wd_loaded")
    raw_loaded = [sem(f"raw_loaded{i}") for i in range(2)]
    hi_split, lo_split, attn_hi, attn_lo = sem("hi_split"), sem("lo_split"), sem("attn_hi"), sem("attn_lo")
    ones_set = sem("ones_set")
    gu_done, silu_done, h_ready, down_done = sem("gu_done"), sem("silu_done"), sem("h_ready"), sem("down_done")
    o_added = sem("o_added")
    kv_done, kv_biased, k_min, k_exp, k_ready = (sem(n) for n in ("kv_done", "kv_biased", "k_min", "k_exp", "k_ready"))
    kvs_done, kvs_copied = sem("kvs_done"), sem("kvs_copied")
    q_done, q_copied, q_min, q_exp, q_ready = (sem(n) for n in ("q_done", "q_copied", "q_min", "q_exp", "q_ready"))
    y_ready, x1_ready = sem("y_ready"), sem("x1_ready")
    gu2_done, silu2_done, h2_ready, down2_done = (sem(n) for n in ("gu2_done", "silu2_done", "h2_ready", "down2_done"))
    x_ready, xs_kept = sem("x_ready"), sem("xs_kept")

    def schedule():
        out = []
        ffn = iter(range(STEPS))

        def f(n=1):
            for _ in range(n):
                s = next(ffn, None)
                if s is not None:
                    out.append(("expert", s))

        def scaling(n, last, gaps=(1, 2, 1)):
            out.append(("centre", n))
            f(gaps[0])
            out.append(("sums", n))
            f(gaps[1])
            out.append(("turn", n))
            f(gaps[2])
            out.append(("spread", n))
            out.append((last, n))

        n = iter(range(PT))
        for h in range(HALVES):
            scaling((next(n), h, "norm0"), "end_norm0", (1, 2, 1) if h else (0, 0, 0))
        f(1)
        for h in range(HALVES):
            out.append(("keys", h))
            f(3)
        out.append(("kv_sum", 0))
        f(2)
        for h in range(HALVES):
            out.append(("query", h))
            f(3)
            scaling((next(n), h, "attn"), "end_attn")
            f(1)
            scaling((next(n), h, "norm1"), "end_norm1")
            f(1)
            out.append(("ffn2", h))
            f(1)
            scaling((next(n), h, "norm2"), "end_norm2")
            f(1)
        f(STEPS)
        out.append(("expert_end", STEPS))
        return out

    SCHEDULE = schedule()
    MARKS = {(k[2], k[1]): k[0] for name, k in SCHEDULE if name == "centre"}

    def x_tile(b, h):
        return X[:, bass.ds(b * SEQ + h * TILE, TILE)]

    def attn_cols(part, lo):
        w = AL if lo else AH
        return w[:, part * P:(part + 1) * P]

    def ffn2_cols(up, c, lo):
        w = AL if lo else AH
        a = 3 * P + up * H0 + c * P
        return w[:, a:a + H0_ROWS[c]]

    block = ctx.enter_context(nc.Block())

    @block.sync
    def _(sp):
        loads = [(attn_raw[:], A["w0_attn"]), (kv_bias[:], A["kv_bias"].broadcast_to([P, 2 * P])),
                 (cols[:, 0:12], A["cols0"]), (WDA[:, 0:2, :], A["w0_down"][0:2 * P, :].rearrange("(c p) n -> p c n", p=P)),
                 (WDA[0:H0_ROWS[2], 2, :], A["w0_down"][2 * P:H0, :])]
        for dst, src in loads:
            sp.dma_start(dst, src).then_inc(small_loaded, 16)
        for e in range(EXPERTS):
            if e >= 2:
                sp.wait_ge(lo_split, e - 1)
            sp.dma_start(raw[:, e % 2, :], A["w0_gu"][e]).then_inc(raw_loaded[e % 2], 16)
        sp.dma_start(WD[:], A["w0_d"]).then_inc(wd_loaded, 16)
        sp.wait_ge(x_ready, BATCHES * HALVES)

    @block.scalar
    def _(act):
        act.wait_ge(small_loaded, 16 * 5)
        act.activation(AH[:], attn_raw[:], ACT.Copy).then_inc(attn_hi, 1)
        for e in range(EXPERTS):
            act.wait_ge(raw_loaded[e % 2], 16 * (e // 2 + 1))
            act.activation(GUH[:, e, :], raw[:, e % 2, :], ACT.Copy).then_inc(hi_split, 1)

        def body(b):
            for name, k in SCHEDULE:
                if name == "expert":
                    act.wait_ge(gu_done, b * STEPS + k + 1)
                    act.wait_ge(h_ready, b * STEPS + max(k - 1, 0))
                    act.activation(S[:, k % 2, :], banks[k % 2][:], ACT.Silu).then_inc(silu_done, 1)
                elif name == "centre":
                    n, h, kind = k
                    if kind == "attn":
                        act.wait_ge(ps.source_done, ps.at(b, n + 1))
                        act.wait_ge(ps.scaled, ps.at(b, n))
                        act.activation(XC[:], LNB[:], ACT.Copy).then_inc(ps.copied, 1)
                    else:
                        act_centred(act, ps, b, n)
                elif name == "sums":
                    act_var(act, ps, b, k[0], attn_eps_col[:] if k[2] == "attn" else eps_col[:])
                elif name == "turn":
                    act_rows(act, ps, b, k[0])
                elif name == "end_norm0":
                    n, h, _ = k
                    act.wait_ge(ps.scaled, ps.at(b, n + 1))
                    act.wait_ge(gu_done, b * STEPS)
                    act.wait_ge(q_done, b * HALVES)
                    act.activation(NH[:, h, :], XN[:, h, :], ACT.Copy).then_inc(ps.hi_done, 1)
                elif name == "keys":
                    act.wait_ge(kv_biased, (b * HALVES + k) * 2 + 2)
                    act.wait_ge(k_ready, b * HALVES + k)
                    act.activation(KE[:], KV[:, k * GROUPS:(k + 1) * GROUPS, 0:P], ACT.Relu, scale=-1.0).then_inc(k_min, 1)
                    act.wait_ge(k_min, b * HALVES + k + 1)
                    act.activation(KE[:], KE[:], ACT.Exp, scale=-1.0).then_inc(k_exp, 1)
                elif name == "kv_sum":
                    act.wait_ge(kvs_done, b + 1)
                    act.wait_ge(ps.sums_done, ps.at(b, 0))
                    act.activation(KVS[:], banks[6][:, 0:P + 2], ACT.Copy).then_inc(kvs_copied, 1)
                elif name == "query":
                    act.wait_ge(q_done, b * HALVES + k + 1)
                    act.wait_ge(q_ready, b * HALVES + k)
                    act.activation(QB[:], banks[7][:], ACT.Identity, bias=cols[:, BQ:BQ + 1]).then_inc(q_copied, 1)
                    act.wait_ge(q_copied, b * HALVES + k + 1)
                    act.activation(QE[:], QB[:], ACT.Relu, scale=-1.0).then_inc(q_min, 1)
                    act.wait_ge(q_min, b * HALVES + k + 1)
                    act.activation(QE[:], QE[:], ACT.Exp, scale=-1.0).then_inc(q_exp, 1)
                elif name == "end_norm1":
                    n, h, _ = k
                    act.wait_ge(ps.scaled, ps.at(b, n + 1))
                    act.wait_ge(y_ready, b * 2 * HALVES + 2 * h)
                    act.activation(X1[:], XS[:], ACT.Identity, bias=cols[:, B1:B1 + 1],
                                   scale=cols[:, G1:G1 + 1]).then_inc(x1_ready, 1)
                    act.wait_ge(x1_ready, b * HALVES + h + 1)
                    act.wait_ge(gu2_done, (b * HALVES + h) * 3)
                    act.activation(HI[:], X1[:], ACT.Copy).then_inc(ps.hi_done, 1)
                elif name == "ffn2":
                    for c in range(3):
                        m = H0_ROWS[c]
                        act.wait_ge(gu2_done, (b * HALVES + k) * 3 + c + 1)
                        act.wait_ge(h2_ready, (b * HALVES + k) * 3 + c)
                        act.activation(S2[0:m, :], banks[6][0:m, :], ACT.Silu,
                                       bias=cols[0:m, BG + c:BG + c + 1]).then_inc(silu2_done, 1)

        with act.Fori(0, BATCHES) as b:
            body(b)

    @block.gpsimd
    def _(pool):
        pool.memset(KV[:, :, 2 * P:], 1.0).then_inc(ones_set, 1)

        def body(b):
            for name, k in SCHEDULE:
                if name == "sums":
                    pool_power(pool, ps, b, k[0], power_one if k[2] == "attn" else power_half)
                elif name == "end_norm0":
                    n, h, _ = k
                    pool.wait_ge(ps.hi_done, 2 * HALVES * b + h + 1)
                    pool.tensor_tensor(NL[:, h, :], XN[:, h, :], NH[:, h, :].bitcast(F32),
                                       ALU.subtract).then_inc(ps.lo_done, 1)
                elif name == "end_norm1":
                    n, h, _ = k
                    pool.wait_ge(ps.hi_done, 2 * HALVES * b + HALVES + h + 1)
                    pool.wait_ge(gu2_done, (b * HALVES + h) * 3)
                    pool.tensor_tensor(LO[:], X1[:], HI[:].bitcast(F32), ALU.subtract).then_inc(ps.lo_done, 1)

        with pool.Fori(0, BATCHES) as b:
            body(b)

    @block.vector
    def _(dve):
        dve.wait_ge(attn_hi, 1)
        dve.tensor_tensor(AL[:], attn_raw[:], AH[:].bitcast(F32), ALU.subtract).then_inc(attn_lo, 1)
        for e in range(EXPERTS):
            dve.wait_ge(hi_split, e + 1)
            dve.tensor_tensor(GUL[:, e, :], raw[:, e % 2, :], GUH[:, e, :].bitcast(F32),
                              ALU.subtract).then_inc(lo_split, 1)

        def add_experts(b, h):
            dve.wait_ge(down_done, b * STEPS + (h + 1) * EXPERTS * CHUNKS)
            dve.scalar_tensor_tensor(x_tile(b, h), banks[4][:], cols[:, B2:B2 + 1], x_tile(b, h),
                                     ALU.add, ALU.add).then_inc(o_added, 1)

        def body(b):
            for name, k in SCHEDULE:
                if name == "expert":
                    if k > 0 and k % (EXPERTS * CHUNKS) == 1:
                        if k > EXPERTS * CHUNKS:
                            add_experts(b, k // (EXPERTS * CHUNKS) - 1)
                    dve.wait_ge(silu_done, b * STEPS + k + 1)
                    dve.wait_ge(down_done, b * STEPS + max(k - 1, 0))
                    dve.tensor_tensor(H[:, k % 2, :], S[:, k % 2, :], banks[2 + k % 2][:],
                                      ALU.mult).then_inc(h_ready, 1)
                elif name == "expert_end":
                    add_experts(b, HALVES - 1)
                    for h in range(HALVES):
                        dve.wait_ge(o_added, b * HALVES + h + 1)
                        dve.wait_ge(ps.scaled, ps.at(b, MARKS["norm2", h] + 1))
                        dve.tensor_tensor(x_tile(b, h), x_tile(b, h), GX[:, h, :], ALU.add).then_inc(x_ready, 1)
                elif name == "spread":
                    n, h, kind = k
                    dve.wait_ge(ps.spread, ps.at(b, n + 1))
                    if kind == "norm0":
                        dve.wait_ge(y_ready, b * 2 * HALVES)
                        dve.wait_ge(ps.lo_done, 2 * HALVES * b)
                        dve.tensor_tensor(XN[:, h, :], XC[:], LNB[:], ALU.mult).then_inc(ps.scaled, 1)
                    else:
                        dve.wait_ge(x1_ready, b * HALVES + (h if kind != "norm2" else h + 1))
                        dve.wait_ge(y_ready, b * 2 * HALVES + 2 * h + (0 if kind == "attn" else 1 if kind == "norm1" else 2))
                        dve.wait_ge(xs_kept, b * HALVES + h)
                        dve.tensor_tensor(XS[:], XC[:], LNB[:], ALU.mult).then_inc(ps.scaled, 1)
                elif name == "keys":
                    for half in range(2):
                        dve.wait_ge(kv_done, (b * HALVES + k) * 2 + half + 1)
                        if half == 0 and k == 0:
                            dve.wait_ge(kvs_done, b)
                            dve.wait_ge(small_loaded, 16 * 5)
                        i = k * GROUPS + 2 * half
                        dve.tensor_tensor(KV[:, i:i + 2, 0:2 * P],
                                          banks[6 + half][:].rearrange("p (a n) -> p a n", a=2),
                                          kv_bias[:].unsqueeze(1).broadcast_to([P, 2, 2 * P]),
                                          ALU.add).then_inc(kv_biased, 1)
                    dve.wait_ge(k_exp, b * HALVES + k + 1)
                    kk = KV[:, k * GROUPS:(k + 1) * GROUPS, 0:P]
                    dve.scalar_tensor_tensor(kk, kk, 0.0, KE[:], ALU.max, ALU.add).then_inc(k_ready, 1)
                elif name == "query":
                    dve.wait_ge(q_exp, b * HALVES + k + 1)
                    if k == 0:
                        dve.wait_ge(ps.sums_done, ps.at(b, 0))
                    else:
                        dve.wait_ge(ps.sums_done, ps.at(b, MARKS["attn", k - 1] + 1))
                    dve.scalar_tensor_tensor(QP[:], QB[:], 0.0, QE[:], ALU.max, ALU.add).then_inc(q_ready, 1)
                elif name == "end_attn":
                    n, h, _ = k
                    dve.wait_ge(ps.scaled, ps.at(b, n + 1))
                    dve.wait_ge(ps.source_done, ps.at(b, n))
                    dve.tensor_tensor(Y[:], XS[:], XN[:, h, :], ALU.add).then_inc(y_ready, 1)
                elif name == "ffn2":
                    for c in range(3):
                        m = H0_ROWS[c]
                        dve.wait_ge(silu2_done, (b * HALVES + k) * 3 + c + 1)
                        dve.wait_ge(down2_done, b * HALVES + k)
                        dve.scalar_tensor_tensor(H2[0:m, c, :], banks[7][0:m, :], cols[0:m, BU + c:BU + c + 1],
                                                 S2[0:m, :], ALU.add, ALU.mult).then_inc(h2_ready, 1)
                    dve.wait_ge(down2_done, b * HALVES + k + 1)
                    dve.scalar_tensor_tensor(Y[:], LNB[:], cols[:, BD:BD + 1], X1[:],
                                             ALU.add, ALU.add).then_inc(y_ready, 1)
                elif name == "end_norm2":
                    n, h, _ = k
                    dve.wait_ge(ps.scaled, ps.at(b, n + 1))
                    dve.wait_ge(x_ready, b * HALVES)
                    dve.tensor_scalar(GX[:, h, :], XS[:], cols[:, G2:G2 + 1], None, ALU.mult).then_inc(xs_kept, 1)

        with dve.Fori(0, BATCHES) as b:
            body(b)

    @block.tensor
    def _(pe):
        pe.wait_ge(attn_lo, 1)
        pe.wait_ge(lo_split, EXPERTS)
        pe.wait_ge(wd_loaded, 16)
        pe.wait_ge(small_loaded, 16 * 5)
        pe.wait_ge(ones_set, 1)

        def down(b, s):
            e, c = s // CHUNKS % EXPERTS, s % CHUNKS
            first, last = s % (EXPERTS * CHUNKS) == 0, s % (EXPERTS * CHUNKS) == EXPERTS * CHUNKS - 1
            pe.wait_ge(h_ready, b * STEPS + s + 1)
            if first:
                pe.wait_ge(o_added, b * HALVES + s // (EXPERTS * CHUNKS))
            mm = pe.matmul(banks[4][:], WD[:, e, c, :], H[:, s % 2, :], start=first, stop=last)
            mm.then_inc(down_done, 1)

        def body(b):
            for name, k in SCHEDULE:
                if name == "expert":
                    e, c, h = k // CHUNKS % EXPERTS, k % CHUNKS, k // (CHUNKS * EXPERTS)
                    pe.wait_ge(h_ready, b * STEPS + max(k - 1, 0))
                    if k % (EXPERTS * CHUNKS) == 0:
                        pe.wait_ge(ps.lo_done, 2 * HALVES * b + h + 1)
                    for up in range(2):
                        a = up * FF + c * P
                        mm = split3(pe, banks[2 * up + k % 2][:], GUH[:, e, a:a + P], GUL[:, e, a:a + P],
                                    NH[:, h, :], NL[:, h, :])
                    mm.then_inc(gu_done, 1)
                    if k > 0:
                        down(b, k - 1)
                elif name == "expert_end":
                    down(b, STEPS - 1)
                elif name == "centre":
                    n, h, kind = k
                    pe.wait_ge(ps.scaled, ps.at(b, n))
                    pe.wait_ge(y_ready, b * 2 * HALVES + (0 if kind == "norm0" else 2 * h + (0 if kind == "attn" else 1 if kind == "norm1" else 2)))
                    if kind == "attn":
                        pe.wait_ge(q_ready, b * HALVES + h + 1)
                        pe.matmul(LNB[:], KVS[:, 0:P], QP[:], start=True, stop=True).then_inc(ps.source_done, 1)
                    elif kind == "norm0":
                        pe.matmul(LNB[:], centre[:], x_tile(b, h), start=True, stop=True).then_inc(ps.source_done, 1)
                    else:
                        pe.matmul(LNB[:], centre[:], Y[:], start=True, stop=True).then_inc(ps.source_done, 1)
                elif name == "sums":
                    if k[2] == "attn":
                        pe_sums(pe, ps, b, k[0], QP, KVS[:, P:P + 1])
                    else:
                        pe_sums(pe, ps, b, k[0], SQ, mean_col[:])
                elif name == "turn":
                    pe_turn(pe, ps, b, k[0])
                elif name == "spread":
                    pe_spread(pe, ps, b, k[0])
                elif name == "keys":
                    h = k
                    pe.wait_ge(ps.lo_done, 2 * HALVES * b + h + 1)
                    for half in range(2):
                        if h > 0:
                            pe.wait_ge(kv_biased, (b * HALVES + h) * 2 - 1 + half)
                        else:
                            pe.wait_ge(kv_biased, b * HALVES * 2)
                            pe.wait_ge(h2_ready, b * HALVES * 3)
                        for i in range(2):
                            t = slice((2 * half + i) * P, (2 * half + i + 1) * P)
                            mm = split3(pe, banks[6 + half][:, i * 2 * P:(i + 1) * 2 * P],
                                        NH[:, h, t], NL[:, h, t], AH[:, P:3 * P], AL[:, P:3 * P])
                        mm.then_inc(kv_done, 1)
                elif name == "kv_sum":
                    pe.wait_ge(k_ready, (b + 1) * HALVES)
                    n = HALVES * GROUPS
                    for i in range(n):
                        mm = pe.matmul(banks[6][:, 0:P + 2], KV[:, i, 0:P], KV[:, i, P:2 * P + 2],
                                       start=(i == 0), stop=(i == n - 1))
                    mm.then_inc(kvs_done, 1)
                elif name == "query":
                    if k > 0:
                        pe.wait_ge(h2_ready, (b * HALVES + k) * 3)
                    pe.wait_ge(kv_biased, (b + 1) * 2 * HALVES)
                    split3(pe, banks[7][:], attn_cols(0, 0), attn_cols(0, 1), NH[:, k, :], NL[:, k, :]).then_inc(q_done, 1)
                    pe.wait_ge(kvs_copied, b + 1)
                elif name == "ffn2":
                    pe.wait_ge(ps.lo_done, 2 * HALVES * b + HALVES + k + 1)
                    pe.wait_ge(ps.scaled, ps.at(b, MARKS["norm1", k] + 1))
                    for c in range(3):
                        m = H0_ROWS[c]
                        pe.wait_ge(h2_ready, (b * HALVES + k) * 3 + c)
                        for up in range(2):
                            mm = split3(pe, banks[6 + up][0:m, :], ffn2_cols(up, c, 0), ffn2_cols(up, c, 1), HI[:], LO[:])
                        mm.then_inc(gu2_done, 1)
                    for c in range(3):
                        m = H0_ROWS[c]
                        pe.wait_ge(h2_ready, (b * HALVES + k) * 3 + c + 1)
                        mm = pe.matmul(LNB[:], WDA[0:m, c, :], H2[0:m, c, :], start=(c == 0), stop=(c == 2))
                    mm.then_inc(down2_done, 1)

        with pe.Fori(0, BATCHES) as b:
            body(b)


def routing(nc, A, sem, sb, ctx, g):
    X, Z, XH, XL, combine, ident, centre, mean_col = (
        g[k] for k in ("X", "Z", "XH", "XL", "combine", "ident", "centre", "mean_col"))
    banks, LNB, XC, SQ, XS = (g[k] for k in ("banks", "LNB", "XC", "SQ", "XS"))
    pe_sums, act_var, pool_power, pe_turn, act_rows, pe_spread, act_centred = (
        g[k] for k in ("pe_sums", "act_var", "pool_power", "pe_turn", "act_rows", "pe_spread", "act_centred"))
    ps = g["PerToken"](sem, 1)
    NG = TOK // P
    WIDE = [P, NG, EXPERTS]

    conf = sb("conf", [P, EXPERTS])
    rows = sb("rows", [P, 3, EXPERTS])
    LG = sb("LG", WIDE)
    TH = sb("TH", WIDE)
    BID = sb("BID", WIDE)
    LEFT = sb("LEFT", WIDE)
    EQ = sb("EQ", WIDE)
    ONE1 = sb("ONE1", WIDE)
    ONE2 = sb("ONE2", WIDE)
    CW = sb("CW", [P, EXPERTS, NG])
    M1, M2, F1, F2, DIF, EX, SUM, W1, W2 = (sb(n, [P, NG]) for n in ("M1", "M2", "F1", "F2", "DIF", "EX", "SUM", "W1", "W2"))
    CT = sb("CT", [P, 2, P])

    rows_loaded = sem("rows_loaded")
    logits_done, logits_copied, z_done, xh_done, xl_done = (
        sem(n) for n in ("logits_done", "logits_copied", "z_done", "xh_done", "xl_done"))
    biased, tanh_done, dif_done, exp_done, cw_done, cw_turned, ct_copied, stored, chain = (
        sem(n) for n in ("biased", "tanh_done", "dif_done", "exp_done", "cw_done", "cw_turned", "ct_copied", "stored", "chain"))

    block = ctx.enter_context(nc.Block())

    @block.sync
    def _(sp):
        sp.dma_start(conf[:], A["conf_w"]).then_inc(rows_loaded, 16)
        for i, name in enumerate(("conf_b", "wealth", "c_rank")):
            sp.dma_start(rows[:, i, :], A[name].broadcast_to([P, EXPERTS])).then_inc(rows_loaded, 16)
        sp.wait_ge(ct_copied, 2)
        sp.dma_start(combine.rearrange("e (j k) -> (e j) k", k=P).rearrange("(a r) k -> r a k", a=2),
                     CT[:]).then_inc(stored, 16)
        sp.wait_ge(stored, 16)

    @block.scalar
    def _(act):
        with act.Fori(0, TILES) as t:
            act_centred(act, ps, t, 0)
            act_var(act, ps, t, 0, g["eps_col"][:])
            act_rows(act, ps, t, 0)
            act.wait_ge(ps.scaled, t + 1)
            act.activation(Z[:, bass.ds(t * TILE, TILE)], XS[:], ACT.Copy).then_inc(z_done, 1)
            act.activation(XH[:, bass.ds(t * TILE, TILE)], XS[:], ACT.Copy).then_inc(xh_done, 1)
            act.wait_ge(logits_done, t + 1)
            act.activation(LG[:, bass.ds(t * GROUPS, GROUPS), :],
                           banks[6][:, 0:GROUPS * EXPERTS].rearrange("p (g e) -> p g e", e=EXPERTS),
                           ACT.Copy).then_inc(logits_copied, 1)
        act.wait_ge(biased, 1)
        act.activation(TH[:], LG[:], ACT.Tanh, scale=0.5).then_inc(tanh_done, 1)
        act.wait_ge(dif_done, 1)
        act.activation(EX[:], DIF[:], ACT.Exp).then_inc(exp_done, 1)
        for i in range(2):
            act.wait_ge(cw_turned, i + 1)
            act.activation(CT[:, i, :], banks[6 + i][:, 0:P], ACT.Copy).then_inc(ct_copied, 1)

    @block.gpsimd
    def _(pool):
        with pool.Fori(0, TILES) as t:
            pool_power(pool, ps, t, 0, g["power_half"])

    @block.vector
    def _(dve):
        with dve.Fori(0, TILES) as t:
            dve.wait_ge(ps.spread, t + 1)
            dve.wait_ge(logits_done, t)
            dve.wait_ge(xl_done, t)
            dve.tensor_tensor(XS[:], XC[:], LNB[:], ALU.mult).then_inc(ps.scaled, 1)
            dve.wait_ge(xh_done, t + 1)
            dve.tensor_tensor(XL[:, bass.ds(t * TILE, TILE)], XS[:], XH[:, bass.ds(t * TILE, TILE)].bitcast(F32),
                              ALU.subtract).then_inc(xl_done, 1)

        count = [0]

        def link(ins):
            count[0] += 1
            ins.then_inc(chain, 1)
            dve.wait_ge(chain, count[0])

        def wide(ap):
            return ap.unsqueeze(1).broadcast_to(WIDE)

        def deep(ap):
            return ap.unsqueeze(2).broadcast_to(WIDE)

        dve.wait_ge(logits_copied, TILES)
        dve.wait_ge(rows_loaded, 64)
        dve.tensor_tensor(LG[:], LG[:], wide(rows[:, 0, :]), ALU.add).then_inc(biased, 1)
        dve.wait_ge(tanh_done, 1)
        link(dve.tensor_scalar(TH[:], TH[:], 0.5, 0.5, ALU.mult, ALU.add))
        link(dve.tensor_tensor(BID[:], TH[:], wide(rows[:, 1, :]), ALU.mult))
        link(dve.tensor_reduce(M1[:], BID[:], AX.X, ALU.max))
        link(dve.tensor_tensor(EQ[:], BID[:], deep(M1[:]), ALU.is_equal))
        link(dve.tensor_tensor(EQ[:], EQ[:], wide(rows[:, 2, :]), ALU.mult))
        link(dve.tensor_reduce(F1[:], EQ[:], AX.X, ALU.max))
        link(dve.tensor_tensor(ONE1[:], deep(F1[:]), wide(rows[:, 2, :]), ALU.is_equal))
        link(dve.scalar_tensor_tensor(LEFT[:], ONE1[:], -3.0e38, BID[:], ALU.mult, ALU.add))
        link(dve.tensor_reduce(M2[:], LEFT[:], AX.X, ALU.max))
        link(dve.tensor_tensor(EQ[:], LEFT[:], deep(M2[:]), ALU.is_equal))
        link(dve.tensor_tensor(EQ[:], EQ[:], wide(rows[:, 2, :]), ALU.mult))
        link(dve.tensor_reduce(F2[:], EQ[:], AX.X, ALU.max))
        link(dve.tensor_tensor(ONE2[:], deep(F2[:]), wide(rows[:, 2, :]), ALU.is_equal))
        dve.tensor_tensor(DIF[:], M2[:], M1[:], ALU.subtract).then_inc(dif_done, 1)
        dve.wait_ge(exp_done, 1)
        link(dve.tensor_scalar(SUM[:], EX[:], 1.0, None, ALU.add))
        link(dve.reciprocal(W1[:], SUM[:]))
        link(dve.tensor_tensor(W2[:], EX[:], W1[:], ALU.mult))
        link(dve.tensor_tensor(ONE1[:], ONE1[:], deep(W1[:]), ALU.mult))
        link(dve.tensor_tensor(ONE2[:], ONE2[:], deep(W2[:]), ALU.mult))
        dve.tensor_tensor(CW[:].rearrange("p e j -> p j e"), ONE1[:], ONE2[:], ALU.add).then_inc(cw_done, 1)

    @block.tensor
    def _(pe):
        pe.wait_ge(rows_loaded, 64)
        with pe.Fori(0, TILES) as t:
            pe.wait_ge(ps.scaled, t)
            pe.matmul(LNB[:], centre[:], X[:, bass.ds(t * TILE, TILE)], start=True, stop=True).then_inc(ps.source_done, 1)
            pe_sums(pe, ps, t, 0, SQ, mean_col[:])
            pe_turn(pe, ps, t, 0)
            pe_spread(pe, ps, t, 0)
            pe.wait_ge(ps.scaled, t + 1)
            pe.wait_ge(logits_copied, t)
            for j in range(GROUPS):
                mm = pe.matmul(banks[6][:, j * EXPERTS:(j + 1) * EXPERTS], XS[:, j * P:(j + 1) * P], conf[:],
                               start=True, stop=True)
            mm.then_inc(logits_done, 1)
        pe.wait_ge(cw_done, 1)
        pe.wait_ge(logits_copied, TILES)
        for i in range(2):
            pe.transpose(banks[6 + i][:, 0:P], CW[:].rearrange("p e j -> p (e j)")[:, i * P:(i + 1) * P],
                         ident[:]).then_inc(cw_turned, 1)


def second_layer(nc, A, sem, sb, ctx, g):
    X, Z, XH, XL, combine, ident, centre, mean_col = (
        g[k] for k in ("X", "Z", "XH", "XL", "combine", "ident", "centre", "mean_col"))
    banks, LNB, XC, SQ, XS, HI, LO, S, H = (g[k] for k in ("banks", "LNB", "XC", "SQ", "XS", "HI", "LO", "S", "H"))
    split3 = g["split3"]
    pe_sums, act_var, pool_power, pe_turn, act_rows, pe_spread, act_centred = (
        g[k] for k in ("pe_sums", "act_var", "pool_power", "pe_turn", "act_rows", "pe_spread", "act_centred"))

    W = TILE + 2
    VIEWS = 6
    GUH = sb("GUH2", [P, PER_LAYER, 2 * FF], F32R)
    GUL = sb("GUL2", [P, PER_LAYER, 2 * FF], F32R)
    WD = sb("WD2", [P, PER_LAYER, CHUNKS, P])
    raw = sb("raw2", [P, 2 * FF])
    QRAW = sb("QRAW", [P, VIEWS * P])
    FRAW = sb("FRAW", [P, 4 * P])
    PRAW = sb("PRAW", [P, P])
    LC = sb("LC", [P, 16])
    LU = sb("LU", [P, 16])
    BIAS = sb("BIAS", [P, 10])
    PB, MB, G1, B1, G2, B2 = 14, 15, 10, 11, 12, 13
    WQH = sb("WQH", [P, VIEWS * P], F32R)
    WQL = sb("WQL", [P, VIEWS * P], F32R)
    FCH = sb("FCH", [P, 4 * P], F32R)
    FCL = sb("FCL", [P, 4 * P], F32R)
    WP = sb("WP", [P, P])
    MP = sb("MP", [P, 4, P])
    hartley = sb("hartley", [P, P])
    GAIN = sb("GAIN", [P, SEQ])
    quarter = sb("quarter", [P, 1])
    rounder = sb("rounder", [P, 1])
    unrounder = sb("unrounder", [P, 1])
    QK = sb("QK", [P, 2, 4, W])
    V = sb("V", [P, 2, 4, W])
    TURNS = sb("TURNS", [P, 3, TILE])
    AM = sb("AM", [P, 4, TILE])
    TA = sb("TA", [P, 4, TILE])
    TB = sb("TB", [P, 4, TILE])
    XG = sb("XG", [P, TILE])
    GE = sb("GE", [P, 2, TILE])
    CB = sb("CB", [P, 2, TILE])
    CO = sb("CO", [P, TILE])

    STEPS = PER_LAYER * TILES * CHUNKS
    UNITS = PER_LAYER * TILES
    ps = g["PerToken"](sem, 2 * TILES)
    consts_loaded, const_set, const_copied = sem("consts_loaded"), sem("const_set"), sem("const_copied")
    attn_loaded, mp_loaded, gu_loaded, wd_loaded = (
        sem(n) for n in ("attn_loaded", "mp_loaded", "gu_loaded", "wd2_loaded"))
    cb_loaded = [sem(f"cb_loaded{i}") for i in range(2)]
    bias_products, fold_done, bias_done, hi_ready, lo_ready, fold_copied = (
        sem(n) for n in ("bias_products", "fold_done", "bias_done", "hi_ready", "lo_ready", "fold_copied"))
    egu_hi, egu_lo = sem("egu_hi"), sem("egu_lo")
    z_ready, out_ready, out_stored = sem("z_ready"), sem("out_ready"), sem("out_stored")
    gu_done, silu_done, h_ready, down_done = (sem(n) for n in ("gu_done2", "silu_done2", "h_ready2", "down_done2"))
    o_read, x_added = sem("o_read"), sem("x_added")
    view_done, view_read, edge_done, turns_done, rounded, reduced, cos_done, diff_done = (
        sem(n) for n in ("view_done", "view_read", "edge_done", "turns_done", "rounded", "reduced", "cos_done", "diff_done"))
    ham, fold_step = sem("ham"), sem("fold_step")
    freq_done, gained, proj_done = sem("freq_done"), sem("gained"), sem("proj_done")
    fc_done, gelu_done, mp_step = sem("fc_done"), sem("gelu_done"), sem("mp_step")
    HAM, FOLD = 13, 3

    def schedule():
        out = []
        ffn = iter(range(STEPS))
        n = iter(range(2 * TILES))

        def f(k=1):
            for _ in range(k):
                s = next(ffn, None)
                if s is not None:
                    out.append(("expert", s))

        out.append(("prep", 0))
        out.append(("prep_expert", 0))
        a = (next(n), 0, "A")
        f(2)
        out.append(("centre", a))
        f(1)
        out.append(("sums", a))
        f(2)
        out.append(("turn", a))
        f(1)
        out.append(("spread", a))
        f(1)
        out.append(("views", 0))
        f(1)
        out.append(("cosines", 0))
        for t in range(TILES + 1):
            B, C, nxt = t < TILES, t > 0, t + 1 < TILES
            a = (next(n), t + 1, "A") if nxt else None
            c = (next(n), t - 1, "C") if C else None
            ham_ops = iter(range(HAM))

            def hams(k):
                for _ in range(k):
                    i = next(ham_ops, None)
                    if B and i is not None:
                        out.append(("ham", (t, i)))

            if C:
                out.append(("freq", t - 1))
            hams(2)
            f(1)
            if C:
                out.append(("proj", t - 1))
            if nxt:
                out.append(("centre", a))
            hams(2)
            f(1)
            if nxt:
                out.append(("sums", a))
            hams(3)
            f(1)
            if t == 0:
                out.append(("prep_expert", 1))
            if nxt:
                out.append(("turn", a))
            hams(2)
            f(1)
            if nxt:
                out.append(("spread", a))
            if C:
                out.append(("centre", c))
            hams(2)
            f(1)
            if nxt:
                out.append(("views", t + 1))
            if C:
                out.append(("sums", c))
            hams(2)
            f(1)
            if nxt:
                out.append(("cosines", t + 1))
            if C:
                out.append(("turn", c))
            hams(HAM)
            if B:
                out.append(("fold", t))
            f(1)
            if C:
                out.append(("spread", c))
                f(1 if not B else 0)
                out.append(("mlp", t - 1))
        f(STEPS)
        out.append(("expert_end", STEPS))
        return out

    SCHEDULE = schedule()
    MARKS = {(k[2], k[1]): k[0] for name, k in SCHEDULE if name == "centre"}

    Z_MARK = {x: i + 1 for i, x in enumerate(x for x in SCHEDULE if x[0] in ("proj", "mlp"))}

    def hi_lo_used(engine, l, n):
        kinds = {i: (kind, t) for (kind, t), i in MARKS.items()}
        kind, t = kinds[n - 1] if n else ("C", -1)
        if kind == "A":
            engine.wait_ge(view_done, (l * TILES + t + 1) * VIEWS)
        else:
            engine.wait_ge(fc_done, (l * TILES + t + 1) * 4)

    def tile(ap, t):
        return ap[:, t * TILE:(t + 1) * TILE]

    def own(ap):
        return ap[..., 1:TILE + 1]

    block = ctx.enter_context(nc.Block())

    @block.sync
    def _(sp):
        sp.dma_start(hartley[:], A["c_hartley"]).then_inc(consts_loaded, 16)
        sp.dma_start(GAIN[:], A["c_gain"]).then_inc(consts_loaded, 16)

        def one(l):
            return bass.ds(l, 1)

        def attention(l):
            for dst, name in ((QRAW, "w1_qkv"), (FRAW, "w1_fc"), (PRAW, "w1_proj"), (LC, "cols1")):
                sp.dma_start(dst[:], A[name][one(l)].rearrange("a p n -> p (a n)")).then_inc(attn_loaded, 16)

        def expert_up(l, e):
            sp.dma_start(raw[:], A["w1_gu"][one(l * PER_LAYER + e)].rearrange("a p n -> p (a n)")).then_inc(gu_loaded, 16)

        def expert_down(l, e):
            sp.dma_start(WD[:, e, :, :], A["w1_d"][one(l * PER_LAYER + e)].rearrange("a p c n -> p (a c) n")).then_inc(wd_loaded, 16)

        def mproj(l):
            sp.dma_start(MP[:], A["w1_mproj"][one(l)].rearrange("a p c n -> p (a c) n")).then_inc(mp_loaded, 16)

        with sp.Fori(0, LAYERS) as l:
            sp.wait_ge(lo_ready, 2 * l)
            attention(l)
            for e in range(PER_LAYER):
                sp.wait_ge(egu_lo, PER_LAYER * l + e)
                expert_up(l, e)
            sp.wait_ge(down_done, STEPS * l)
            for e in range(PER_LAYER):
                expert_down(l, e)
            sp.wait_ge(mp_step, 4 * TILES * l)
            mproj(l)
        for t in range(TILES):
            sp.wait_ge(out_ready, t + 1)
            sp.dma_start(A["outT"][:, t * TILE:(t + 1) * TILE], tile(X, t)).then_inc(out_stored, 16)
        sp.wait_ge(out_stored, 16 * TILES)

    @block.scalar
    def _(act):
        act.wait_ge(const_set, 1)

        def body(l):
            for name, k in SCHEDULE:
                if name == "prep":
                    act.wait_ge(attn_loaded, 64 * l + 64)
                    act.wait_ge(view_done, VIEWS * TILES * l)
                    act.activation(WQH[:], QRAW[:], ACT.Copy, scale=LC[:, G1:G1 + 1]).then_inc(hi_ready, 1)
                    act.wait_ge(fc_done, 4 * TILES * l)
                    act.activation(FCH[:], FRAW[:], ACT.Copy, scale=LC[:, G2:G2 + 1]).then_inc(hi_ready, 1)
                    act.wait_ge(fold_done, l + 1)
                    act.wait_ge(proj_done, TILES * l)
                    act.activation(WP[:], banks[7][:, 0:P], ACT.Copy, scale=1.0 / P).then_inc(fold_copied, 1)
                elif name == "prep_expert":
                    act.wait_ge(gu_loaded, (PER_LAYER * l + k + 1) * 16)
                    act.wait_ge(gu_done, STEPS * l)
                    act.activation(GUH[:, k, :], raw[:], ACT.Copy).then_inc(egu_hi, 1)
                elif name == "expert":
                    if k % CHUNKS == 0:
                        u = k // CHUNKS
                        e, t = u // TILES, u % TILES
                        act.wait_ge(o_read, UNITS * l + max(u - 1, 0))
                        act.dma_start(CB[:, u % 2, :],
                                      combine[bass.ds(l * PER_LAYER + e, 1),
                                              t * TILE:(t + 1) * TILE].broadcast_to([P, TILE])).then_inc(cb_loaded[u % 2], 16)
                    act.wait_ge(gu_done, l * STEPS + k + 1)
                    act.wait_ge(h_ready, l * STEPS + max(k - 1, 0))
                    act.activation(S[:, k % 2, :], banks[k % 2][:], ACT.Silu).then_inc(silu_done, 1)
                elif name == "centre":
                    act_centred(act, ps, l, k[0])
                elif name == "sums":
                    act_var(act, ps, l, k[0], g["eps_col"][:])
                elif name == "turn":
                    act_rows(act, ps, l, k[0])
                elif name == "spread":
                    act.wait_ge(ps.scaled, ps.at(l, k[0] + 1))
                    hi_lo_used(act, l, k[0])
                    act.activation(HI[:], XS[:], ACT.Copy).then_inc(ps.hi_done, 1)
                elif name == "views":
                    t = k
                    first = t % HALVES == 0
                    act.wait_ge(ham, (l * TILES + t - 1) * HAM + 6 if t else l * TILES * HAM)
                    if not first:
                        act.wait_ge(view_read, (l * TILES + t) * VIEWS)
                        act.activation(QK[:, :, 0, 0:1], QK[:, :, 0, TILE:TILE + 1], ACT.Copy)
                        act.activation(V[:, t % 2, 0, 0:1], V[:, (t - 1) % 2, 0, TILE:TILE + 1], ACT.Copy).then_inc(edge_done, 1)
                        act.wait_ge(edge_done, l * TILES + t + 1)
                    act.wait_ge(bias_done, l + 1)
                    outs = [QK[:, 0, 0, :], QK[:, 1, 0, :], V[:, t % 2, 0, :],
                            QK[:, 0, 2, :], QK[:, 1, 2, :], V[:, t % 2, 2, :]]
                    for i in range(VIEWS):
                        act.wait_ge(view_done, (l * TILES + t) * VIEWS + i + 1)
                        act.activation(own(outs[i]), banks[6 + i % 2][:], ACT.Identity,
                                       bias=BIAS[:, i:i + 1]).then_inc(view_read, 1)
                    if first:
                        act.wait_ge(view_read, (l * TILES + t + 1) * VIEWS)
                        act.activation(QK[:, :, 0, 0:1], QK[:, :, 0, 1:2], ACT.Copy)
                        act.activation(V[:, t % 2, 0, 0:1], V[:, t % 2, 0, 1:2], ACT.Copy).then_inc(edge_done, 1)
                elif name == "cosines":
                    t = k
                    act.wait_ge(view_read, (l * TILES + t + 1) * VIEWS)
                    act.activation(own(QK[:, :, 3, :]), own(QK[:, :, 0, :]), ACT.Identity, bias=quarter[:],
                                   scale=1.0 / (2 * np.pi))
                    act.activation(own(V[:, t % 2, 3, :]), own(V[:, t % 2, 0, :]), ACT.Identity, bias=quarter[:],
                                   scale=1.0 / (2 * np.pi)).then_inc(turns_done, 1)
                    act.wait_ge(turns_done, l * TILES + t + 1)
                    act.wait_ge(cos_done, l * TILES + t)
                    act.activation(TURNS[:, 0:2, :], own(QK[:, :, 3, :]), ACT.Identity, bias=rounder[:])
                    act.activation(TURNS[:, 2, :], own(V[:, t % 2, 3, :]), ACT.Identity, bias=rounder[:]).then_inc(rounded, 1)
                    act.wait_ge(rounded, 2 * (l * TILES + t) + 1)
                    act.activation(TURNS[:], TURNS[:], ACT.Identity, bias=unrounder[:]).then_inc(rounded, 1)
                    act.wait_ge(reduced, l * TILES + t + 1)
                    act.activation(own(QK[:, :, 3, :]), TURNS[:, 0:2, :], ACT.Sin, scale=-TURN)
                    act.activation(own(V[:, t % 2, 3, :]), TURNS[:, 2, :], ACT.Sin, scale=-TURN).then_inc(cos_done, 1)
                elif name == "mlp":
                    for c in range(4):
                        act.wait_ge(fc_done, (l * TILES + k) * 4 + c + 1)
                        act.wait_ge(mp_step, (l * TILES + k) * 4 + max(c - 1, 0))
                        act.activation(GE[:, c % 2, :], banks[6 + c % 2][:], ACT.Gelu,
                                       bias=BIAS[:, VIEWS + c:VIEWS + c + 1]).then_inc(gelu_done, 1)

        with act.Fori(0, LAYERS) as l:
            body(l)

    @block.gpsimd
    def _(pool):
        def body(l):
            for name, k in SCHEDULE:
                if name == "prep_expert":
                    pool.wait_ge(egu_hi, PER_LAYER * l + k + 1)
                    pool.tensor_tensor(GUL[:, k, :], raw[:], GUH[:, k, :].bitcast(F32),
                                       ALU.subtract).then_inc(egu_lo, 1)
                elif name == "expert" and k % CHUNKS == 2 and k > CHUNKS:
                    added(l, k // CHUNKS - 1)
                elif name == "expert_end":
                    added(l, UNITS - 1)
                elif name == "sums":
                    pool_power(pool, ps, l, k[0], g["power_half"])
                elif name == "spread":
                    pool.wait_ge(ps.hi_done, ps.at(l, k[0] + 1))
                    hi_lo_used(pool, l, k[0])
                    pool.tensor_tensor(LO[:], XS[:], HI[:].bitcast(F32), ALU.subtract).then_inc(ps.lo_done, 1)
                elif name == "cosines":
                    t = k
                    n = l * TILES + t
                    pool.wait_ge(rounded, 2 * n + 2)
                    pool.tensor_tensor(TURNS[:, 0:2, :], TURNS[:, 0:2, :], own(QK[:, :, 3, :]), ALU.subtract)
                    pool.tensor_tensor(TURNS[:, 2, :], TURNS[:, 2, :], own(V[:, t % 2, 3, :]),
                                       ALU.subtract).then_inc(reduced, 1)
                elif name == "fold":
                    n = l * TILES + k
                    pool.wait_ge(ham, (n + 1) * HAM)
                    pool.tensor_tensor(AM[:, 0, :], AM[:, 0, :], AM[:, 1, :], ALU.subtract).then_inc(fold_step, 1)
                    pool.tensor_tensor(AM[:, 2, :], AM[:, 2, :], AM[:, 3, :], ALU.add).then_inc(fold_step, 1)
                    pool.wait_ge(fold_step, n * FOLD + 2)
                    pool.tensor_tensor(AM[:, 0, :], AM[:, 0, :], AM[:, 2, :], ALU.subtract).then_inc(fold_step, 1)

        def added(l, u):
            pool.wait_ge(o_read, UNITS * l + u + 1)
            pool.wait_ge(x_added, UNITS * l + u)
            pool.tensor_tensor(tile(X, u % TILES), tile(X, u % TILES), CO[:], ALU.add).then_inc(x_added, 1)

        with pool.Fori(0, LAYERS) as l:
            body(l)

    @block.vector
    def _(dve):
        dve.memset(rounder[:], ROUND)
        dve.memset(unrounder[:], -ROUND)
        dve.memset(quarter[:], 0.25).then_inc(const_set, 1)
        dve.wait_ge(consts_loaded, 32)

        def unit(l, u):
            dve.wait_ge(down_done, l * STEPS + (u + 1) * CHUNKS)
            dve.wait_ge(cb_loaded[u % 2], (l * (UNITS // 2) + u // 2 + 1) * 16)
            dve.wait_ge(x_added, l * UNITS + u)
            dve.tensor_tensor(CO[:], banks[4][:], CB[:, u % 2, :], ALU.mult).then_inc(o_read, 1)

        def pair(ap, a, b):
            return ap[:, a:b + 1:b - a, :]

        def hamilton(n, t, i):
            q = own(QK[:, 0, :, :])

            def k_(j):
                return own(QK[:, 1, j, :]).unsqueeze(1).broadcast_to([P, 4, TILE])

            base = n * HAM
            ADD, SUB = ALU.add, ALU.subtract
            if i == 0:
                dve.wait_ge(cos_done, n + 1)
                dve.wait_ge(diff_done, 2 * (n + 1))
                dve.wait_ge(freq_done, n)
                ins = dve.tensor_tensor(AM[:], q, k_(0), ALU.mult)
            elif i in (1, 2, 5):
                dve.wait_ge(ham, base if i < 5 else base + 5)
                ins = dve.tensor_tensor((TB if i == 2 else TA)[:], q, k_({1: 1, 2: 2, 5: 3}[i]), ALU.mult)
            elif i in (3, 4):
                dve.wait_ge(ham, base + 2)
                (d, s, op) = ((1, 2), (0, 3), ADD) if i == 3 else ((0, 3), (1, 2), SUB)
                ins = dve.tensor_tensor(pair(AM, *d), pair(AM, *d), pair(TA, *s), op)
            elif i in (6, 7):
                dve.wait_ge(ham, base + 5 if i == 6 else base + 5)
                (d, s, op) = ((2, 3), (0, 1), ADD) if i == 6 else ((0, 1), (2, 3), SUB)
                ins = dve.tensor_tensor(pair(AM, *d), pair(AM, *d), pair(TB, *s), op)
            elif i < 12:
                d, s, op = ((3, 0, ADD), (2, 1, SUB), (1, 2, ADD), (0, 3, SUB))[i - 8]
                dve.wait_ge(ham, base + i - 1)
                ins = dve.tensor_tensor(AM[:, d, :], AM[:, d, :], TA[:, s, :], op)
            else:
                dve.wait_ge(ham, base + 12)
                ins = dve.tensor_tensor(AM[:], AM[:], own(V[:, t % 2, :, :]), ALU.mult)
            ins.then_inc(ham, 1)

        def body(l):
            for name, k in SCHEDULE:
                if name == "prep":
                    dve.wait_ge(bias_products, l + 1)
                    dve.wait_ge(attn_loaded, 64 * l + 64)
                    dve.wait_ge(gelu_done, 4 * TILES * l)
                    dve.wait_ge(z_ready, 2 * TILES * l)
                    dve.tensor_tensor(BIAS[:], banks[6][:, 0:10], LC[:, 0:10], ALU.add)
                    dve.tensor_copy(LU[:], LC[:]).then_inc(bias_done, 1)
                    dve.wait_ge(bias_done, l + 1)
                    dve.wait_ge(hi_ready, 2 * l + 1)
                    dve.scalar_tensor_tensor(WQL[:], QRAW[:], LC[:, G1:G1 + 1], WQH[:].bitcast(F32),
                                             ALU.mult, ALU.subtract).then_inc(lo_ready, 1)
                    dve.wait_ge(hi_ready, 2 * l + 2)
                    dve.scalar_tensor_tensor(FCL[:], FRAW[:], LC[:, G2:G2 + 1], FCH[:].bitcast(F32),
                                             ALU.mult, ALU.subtract).then_inc(lo_ready, 1)
                elif name == "expert":
                    dve.wait_ge(silu_done, l * STEPS + k + 1)
                    dve.wait_ge(down_done, l * STEPS + max(k - 1, 0))
                    dve.tensor_tensor(H[:, k % 2, :], S[:, k % 2, :], banks[2 + k % 2][:],
                                      ALU.mult).then_inc(h_ready, 1)
                    if k % CHUNKS == 1 and k > CHUNKS:
                        unit(l, k // CHUNKS - 1)
                elif name == "expert_end":
                    unit(l, UNITS - 1)
                elif name == "spread":
                    n = k[0]
                    dve.wait_ge(ps.spread, ps.at(l, n + 1))
                    dve.wait_ge(ps.lo_done, ps.at(l, n))
                    dve.tensor_tensor(XS[:], XC[:], LNB[:], ALU.mult).then_inc(ps.scaled, 1)
                elif name == "cosines":
                    t, n = k, l * TILES + k
                    dve.wait_ge(edge_done, n + 1)
                    dve.wait_ge(view_read, (n + 1) * VIEWS)
                    for buf, side in ((QK, slice(0, 2)), (V, slice(t % 2, t % 2 + 1))):
                        zero = buf[:, side, 0, :]
                        dve.tensor_tensor(own(buf[:, side, 1, :]), own(zero), zero[..., 0:TILE],
                                          ALU.subtract).then_inc(diff_done, 1)
                elif name == "ham":
                    hamilton(l * TILES + k[0], *k)
                elif name == "freq":
                    n = l * TILES + k
                    dve.wait_ge(freq_done, n + 1)
                    dve.wait_ge(proj_done, n)
                    s = (k % HALVES) * TILE
                    dve.tensor_tensor(XG[:], banks[6][:], GAIN[:, s:s + TILE], ALU.mult).then_inc(gained, 1)
                elif name == "proj":
                    dve.wait_ge(proj_done, l * TILES + k + 1)
                    dve.scalar_tensor_tensor(tile(Z, k), banks[7][:], LU[:, PB:PB + 1], tile(Z, k),
                                             ALU.add, ALU.add).then_inc(z_ready, 1)
                elif name == "mlp":
                    dve.wait_ge(mp_step, (l * TILES + k + 1) * 4)
                    dve.scalar_tensor_tensor(tile(Z, k), LNB[:], LU[:, MB:MB + 1], tile(Z, k),
                                             ALU.add, ALU.add).then_inc(z_ready, 1)

        with dve.Fori(0, LAYERS) as l:
            body(l)
        dve.wait_ge(x_added, UNITS * LAYERS)
        dve.wait_ge(z_ready, 2 * TILES * LAYERS)
        for t in range(TILES):
            dve.tensor_tensor(tile(X, t), tile(X, t), tile(Z, t), ALU.add).then_inc(out_ready, 1)

    @block.tensor
    def _(pe):
        pe.wait_ge(consts_loaded, 32)

        def down(l, s):
            u, c = s // CHUNKS, s % CHUNKS
            pe.wait_ge(h_ready, l * STEPS + s + 1)
            if c == 0:
                pe.wait_ge(o_read, l * UNITS + u)
                pe.wait_ge(wd_loaded, (l + 1) * 16 * PER_LAYER)
            pe.matmul(banks[4][:], WD[:, u // TILES, c, :], H[:, s % 2, :],
                      start=(c == 0), stop=(c == CHUNKS - 1)).then_inc(down_done, 1)

        def body(l):
            for name, k in SCHEDULE:
                if name == "prep":
                    pe.wait_ge(attn_loaded, 64 * l + 64)
                    pe.wait_ge(gelu_done, 4 * TILES * l)
                    pe.wait_ge(z_ready, 2 * TILES * l)
                    for i in range(VIEWS):
                        pe.matmul(banks[6][:, i:i + 1], QRAW[:, i * P:(i + 1) * P], LC[:, B1:B1 + 1], start=True, stop=True)
                    for i in range(4):
                        mm = pe.matmul(banks[6][:, VIEWS + i:VIEWS + i + 1], FRAW[:, i * P:(i + 1) * P],
                                       LC[:, B2:B2 + 1], start=True, stop=True)
                    mm.then_inc(bias_products, 1)
                    pe.matmul(banks[7][:, 0:P], hartley[:], PRAW[:], start=True, stop=True).then_inc(fold_done, 1)
                elif name == "expert":
                    u, c = k // CHUNKS, k % CHUNKS
                    e, t = u // TILES, u % TILES
                    pe.wait_ge(h_ready, l * STEPS + max(k - 1, 0))
                    if t == 0 and c == 0:
                        pe.wait_ge(egu_lo, PER_LAYER * l + e + 1)
                    for up in range(2):
                        a = up * FF + c * P
                        mm = split3(pe, banks[2 * up + k % 2][:], GUH[:, e, a:a + P], GUL[:, e, a:a + P],
                                    tile(XH, t), tile(XL, t))
                    mm.then_inc(gu_done, 1)
                    if k > 0:
                        down(l, k - 1)
                elif name == "expert_end":
                    down(l, STEPS - 1)
                elif name == "centre":
                    n, t, kind = k
                    pe.wait_ge(ps.scaled, ps.at(l, n))
                    at = SCHEDULE.index((name, k))
                    marks = [0] + [Z_MARK[x] for x in SCHEDULE[:at] if x[0] == "mlp"]
                    if kind == "C":
                        marks.append(Z_MARK["proj", t])
                    pe.wait_ge(z_ready, 2 * TILES * l + max(marks))
                    pe.matmul(LNB[:], centre[:], tile(Z, t), start=True, stop=True).then_inc(ps.source_done, 1)
                elif name == "sums":
                    pe_sums(pe, ps, l, k[0], SQ, mean_col[:])
                elif name == "turn":
                    pe_turn(pe, ps, l, k[0])
                elif name == "spread":
                    pe_spread(pe, ps, l, k[0])
                elif name == "views":
                    t = k
                    pe.wait_ge(ps.lo_done, ps.at(l, MARKS["A", t] + 1))
                    pe.wait_ge(lo_ready, 2 * l + 2)
                    pe.wait_ge(fold_copied, l + 1)
                    pe.wait_ge(bias_done, l + 1)
                    for i in range(VIEWS):
                        if i >= 2:
                            pe.wait_ge(view_read, (l * TILES + t) * VIEWS + i - 1)
                        else:
                            pe.wait_ge(view_read, (l * TILES + t) * VIEWS)
                            pe.wait_ge(gained, l * TILES + max(t - 1, 0))
                            pe.wait_ge(z_ready, 2 * TILES * l + (Z_MARK["proj", t - 2] if t > 1 else 0))
                            pe.wait_ge(gelu_done, 4 * (l * TILES + max(t - 2, 0)))
                        mm = split3(pe, banks[6 + i % 2][:], WQH[:, i * P:(i + 1) * P], WQL[:, i * P:(i + 1) * P], HI[:], LO[:])
                        mm.then_inc(view_done, 1)
                elif name == "freq":
                    n = l * TILES + k
                    pe.wait_ge(fold_step, FOLD * (n + 1))
                    pe.wait_ge(view_read, VIEWS * (l * TILES + min(k + 2, TILES)))
                    pe.wait_ge(gelu_done, 4 * n)
                    pe.matmul(banks[6][:], hartley[:], AM[:, 0, :], start=True, stop=True).then_inc(freq_done, 1)
                elif name == "proj":
                    n = l * TILES + k
                    pe.wait_ge(gained, n + 1)
                    pe.matmul(banks[7][:], WP[:], XG[:], start=True, stop=True).then_inc(proj_done, 1)
                elif name == "mlp":
                    t = k
                    pe.wait_ge(ps.lo_done, ps.at(l, MARKS["C", t] + 1))
                    pe.wait_ge(mp_loaded, (l + 1) * 16)
                    pe.wait_ge(view_read, VIEWS * (l * TILES + min(t + 3, TILES)))
                    pe.wait_ge(z_ready, 2 * TILES * l + Z_MARK["proj", t])
                    for c in range(4 + 1):
                        if c < 4:
                            pe.wait_ge(gelu_done, (l * TILES + t) * 4 + max(c - 1, 0))
                            split3(pe, banks[6 + c % 2][:], FCH[:, c * P:(c + 1) * P], FCL[:, c * P:(c + 1) * P],
                                   HI[:], LO[:]).then_inc(fc_done, 1)
                        if c > 0:
                            pe.wait_ge(gelu_done, (l * TILES + t) * 4 + c)
                            mm = pe.matmul(LNB[:], MP[:, c - 1, :], GE[:, (c - 1) % 2, :], start=(c == 1), stop=(c == 4))
                            mm.then_inc(mp_step, 1)

        with pe.Fori(0, LAYERS) as l:
            body(l)


def _constants():
    pick = np.zeros((2 * GROUPS, GROUPS, P), np.float32)
    for i in range(GROUPS):
        pick[i, i] = pick[GROUPS + i, i] = 1.0

    def cas(n):
        a = 2 * np.pi * np.outer(np.arange(n), np.arange(n)) / n
        return np.cos(a) + np.sin(a)

    heads, dims = 16, 8
    ks = np.fft.fftfreq(SEQ)[None, None, :]
    kh = np.fft.fftfreq(heads)[:, None, None]
    kd = np.fft.fftfreq(dims)[None, :, None]
    km = np.sqrt(ks ** 2 + kh ** 2 + kd ** 2 + 1e-10)
    gain = np.cos(np.arctan(np.log(km + 1e-10))).reshape(P, SEQ)
    lam = np.arange(SEQ, dtype=np.float32) / np.float32(SEQ)
    t = np.arange(SEQ, dtype=np.float32) * np.float32(0.1)
    phase = t - np.float32(2.0) * lam + np.float32(0.5) * lam ** 2
    modulation = np.sin(t + lam) * np.cos(phase)
    return {
        "c_ident": np.eye(P, dtype=np.float32),
        "c_centre": (np.eye(P) - 1.0 / P).astype(np.float32),
        "c_pick": pick,
        "c_hartley": np.kron(cas(heads), cas(dims)).astype(np.float32),
        "c_gain": (gain * (1.0 + 0.1 * modulation)).astype(np.float32),
        "c_rank": np.arange(EXPERTS, 0, -1, dtype=np.float32)[None],
    }


def _layout(i):
    a = {k: np.asarray(v) for k, v in i.items()}
    heads, dims = 16, 8
    head_before = (np.arange(heads) - 1) % heads

    def views(x):
        x = x.reshape(*x.shape[:-1], heads, 3, dims)
        parts = [x[..., j, :] for j in range(3)]
        parts += [p[..., head_before, :] for p in parts]
        return [p.reshape(*p.shape[:-2], P) for p in parts]

    cols0 = np.zeros((P, 12), np.float32)
    cols0[:, 0] = a["L0_attn_bqkv"][:P]
    for c, m in enumerate(H0_ROWS):
        cols0[:m, 1 + c] = a["L0_attn_bg"][c * P:c * P + m]
        cols0[:m, 4 + c] = a["L0_attn_bu"][c * P:c * P + m]
    for c, n in ((7, "bd"), (8, "g1"), (9, "b1"), (10, "g2"), (11, "b2")):
        cols0[:, c] = a["L0_attn_" + n]
    cols1 = np.zeros((LAYERS, P, 16), np.float32)
    for c, v in enumerate(views(a["L1_attn_attn_b"])):
        cols1[:, :, c] = v
    cols1[:, :, 6:10] = a["L1_attn_fc_b"].reshape(LAYERS, 4, P).transpose(0, 2, 1)
    for c, n in ((10, "ln1_w"), (11, "ln1_b"), (12, "ln2_w"), (13, "ln2_b"), (14, "aproj_b"), (15, "mproj_b")):
        cols1[:, :, c] = a["L1_attn_" + n]
    return {
        "xT": a["L0_attn_x"].reshape(TOK, P).T,
        "w0_attn": np.concatenate([a["L0_attn_Wqkv"], a["L0_attn_Wg"], a["L0_attn_Wu"]], 1),
        "w0_down": a["L0_attn_Wd"],
        "kv_bias": a["L0_attn_bqkv"][None, P:],
        "cols0": cols0,
        "w0_gu": np.concatenate([a["L0_ffn_Wg"], a["L0_ffn_Wu"]], 2),
        "w0_d": a["L0_ffn_Wd"].reshape(EXPERTS, CHUNKS, P, P).transpose(2, 0, 1, 3),
        "conf_w": a["L1_ffn_conf_w"].T,
        "conf_b": a["L1_ffn_conf_b"][None],
        "wealth": a["L1_ffn_wealth"][None],
        "w1_qkv": np.concatenate(views(a["L1_attn_attn_w"]), -1),
        "w1_fc": a["L1_attn_fc_w"],
        "w1_proj": a["L1_attn_aproj_w"],
        "w1_mproj": a["L1_attn_mproj_w"].reshape(LAYERS, 4, P, P).transpose(0, 2, 1, 3),
        "cols1": cols1,
        "w1_gu": np.concatenate([a["L1_ffn_gate_w"], a["L1_ffn_up_w"]], 1).transpose(0, 2, 1),
        "w1_d": a["L1_ffn_down_w"].transpose(0, 2, 1).reshape(EXPERTS, CHUNKS, P, P).transpose(0, 2, 1, 3),
    }


def kernel(**inputs):
    import concourse.bacc as _bacc
    from concourse.bass_utils import run_bass_kernel_spmd as _run

    nc = _bacc.Bacc("TRN2", target_bir_lowering=False, num_devices=1)
    arrays, A = {}, {}
    for name, a in {**_layout(inputs), **_constants()}.items():
        a = np.ascontiguousarray(a)
        arrays[f"in_{name}"] = a
        A[name] = nc.dram_tensor(f"in_{name}", a.shape, mybir.dt.from_np(a.dtype), kind="ExternalInput").ap()
    A["outT"] = nc.dram_tensor("outT", (P, TOK), F32, kind="ExternalOutput").ap()
    kernel_program(nc, A)
    got = _run(nc, [arrays], core_ids=[0]).results[0]["outT"]
    return np.ascontiguousarray(got.T).reshape(BATCHES, SEQ, P)
```

```python
from contextlib import ExitStack

import numpy as np

import concourse.bass as bass
from concourse import mybir

F32 = mybir.dt.float32
F32R = mybir.dt.float32r
ALU = mybir.AluOpType
ACT = mybir.ActivationFunctionType
AX = mybir.AxisListType

P = 128
TOK = 4096
TILE = 512
GROUPS = TILE // P
SEQ = 1024
BATCHES = TOK // SEQ
HALVES = SEQ // TILE
TILES = TOK // TILE
EXPERTS = 8
FF = 512
CHUNKS = FF // P
H0 = 341
H0_ROWS = [min(P, H0 - P * c) for c in range(3)]
LAYERS = 4
PER_LAYER = EXPERTS // LAYERS
EPS = 1e-5
ATTN_EPS = 1e-6
ROUND = 12582912.0
TURN = 6.283185


def kernel_program(nc, A):
    with ExitStack() as whole:
        def sem_of(ctx):
            return lambda name: ctx.enter_context(nc.semaphore(name))

        def sb_of(ctx):
            return lambda name, shape, dt=F32: ctx.enter_context(nc.sbuf_tensor(name, shape, dt))

        sb = sb_of(whole)
        X = sb("X", [P, TOK])
        ident = sb("ident", [P, P])
        centre = sb("centre", [P, P])
        mean_col = sb("mean_col", [P, 1])
        pick = sb("pick", [2 * GROUPS, GROUPS, P], F32R)
        power_half = sb("power_half", [P, GROUPS])
        power_one = sb("power_one", [P, GROUPS])
        ones = sb("ones", [P, GROUPS])
        eps_col = sb("eps_col", [P, 1])
        attn_eps_col = sb("attn_eps_col", [P, 1])
        banks = [whole.enter_context(nc.psum_tensor(f"bank{i}", [P, TILE], F32)) for i in range(8)]

        XC = sb("XC", [P, TILE])
        SQ = sb("SQ", [P, TILE])
        XS = sb("XS", [P, TILE])
        HI = sb("HI", [P, TILE], F32R)
        LO = sb("LO", [P, TILE], F32R)
        VAR = sb("VAR", [P, GROUPS])
        RSTD = sb("RSTD", [P, GROUPS])
        RHL = sb("RHL", [P, 2 * GROUPS])
        RT = sb("RT", [2 * GROUPS, P], F32R)
        SH = sb("SH", [P, 4, TILE])

        LNB = banks[5]

        def split3(pe, out, w_hi, w_lo, x_hi, x_lo):
            pe.matmul(out, w_hi, x_hi, start=True, stop=False)
            pe.matmul(out, w_lo, x_hi, start=False, stop=False)
            return pe.matmul(out, w_hi, x_lo, start=False, stop=True)

        class PerToken:

            def __init__(self, sem, per_pass):
                self.per = per_pass
                self.source_done = sem("source_done")
                self.copied = sem("copied")
                self.sums_done = sem("sums_done")
                self.var_copied = sem("var_copied")
                self.power_step = sem("power_step")
                self.turned = sem("turned")
                self.rows_copied = sem("rows_copied")
                self.spread = sem("spread")
                self.scaled = sem("scaled")
                self.hi_done = sem("hi_done")
                self.lo_done = sem("lo_done")

            def at(self, it, n, each=1):
                return it * (self.per * each) + n * each

        def pe_sums(pe, ps, it, n, lhs, col):
            pe.wait_ge(ps.copied, ps.at(it, n + 1))
            for g in range(GROUPS):
                mm = pe.matmul(LNB[:, g:g + 1], lhs[:, g * P:(g + 1) * P], col, start=True, stop=True)
            mm.then_inc(ps.sums_done, 1)

        def act_var(act, ps, it, n, eps_col):
            act.wait_ge(ps.sums_done, ps.at(it, n + 1))
            act.wait_ge(ps.power_step, ps.at(it, n, 3))
            act.activation(VAR[:], LNB[:, 0:GROUPS], ACT.Identity, bias=eps_col).then_inc(ps.var_copied, 1)

        def pool_power(pool, ps, it, n, power):
            pool.wait_ge(ps.var_copied, ps.at(it, n + 1))
            pool.wait_ge(ps.turned, ps.at(it, n))
            pool.wait_ge(ps.power_step, ps.at(it, n, 3))
            pool.tensor_tensor(RSTD[:], VAR[:], power[:], ALU.pow).then_inc(ps.power_step, 1)
            pool.wait_ge(ps.power_step, ps.at(it, n, 3) + 1)
            pool.tensor_tensor(RHL[:, 0:GROUPS].bitcast(F32R), RSTD[:], ones[:], ALU.mult).then_inc(ps.power_step, 1)
            pool.wait_ge(ps.power_step, ps.at(it, n, 3) + 2)
            pool.tensor_tensor(RHL[:, GROUPS:].bitcast(F32R), RSTD[:], RHL[:, 0:GROUPS],
                               ALU.subtract).then_inc(ps.power_step, 1)

        def pe_turn(pe, ps, it, n):
            pe.wait_ge(ps.power_step, ps.at(it, n + 1, 3))
            pe.transpose(LNB[0:2 * GROUPS, P:2 * P], RHL[:], ident[:]).then_inc(ps.turned, 1)

        def act_rows(act, ps, it, n):
            act.wait_ge(ps.turned, ps.at(it, n + 1))
            act.wait_ge(ps.spread, ps.at(it, n))
            act.activation(RT[:], LNB[0:2 * GROUPS, P:2 * P], ACT.Copy).then_inc(ps.rows_copied, 1)

        def pe_spread(pe, ps, it, n):
            pe.wait_ge(ps.rows_copied, ps.at(it, n + 1))
            for g in range(GROUPS):
                mm = pe.matmul(LNB[:, g * P:(g + 1) * P], pick[:, g, :], RT[:], start=True, stop=True)
            mm.then_inc(ps.spread, 1)

        def act_centred(act, ps, it, n):
            act.wait_ge(ps.source_done, ps.at(it, n + 1))
            act.wait_ge(ps.scaled, ps.at(it, n))
            act.activation(XC[:], LNB[:], ACT.Copy)
            act.wait_ge(ps.sums_done, ps.at(it, n))
            act.activation(SQ[:], LNB[:], ACT.Square).then_inc(ps.copied, 1)

        def setup(sem, pick_raw, block):
            loaded, made = sem("const_loaded"), sem("const_made")

            @block.sync
            def _(sp):
                for dst, src in ((ident, A["c_ident"]), (centre, A["c_centre"]), (pick_raw, A["c_pick"])):
                    sp.dma_start(dst[:], src).then_inc(loaded, 16)
                sp.dma_start(X[:], A["xT"]).then_inc(loaded, 16)
                sp.wait_ge(loaded, 64)

            @block.vector
            def _(dve):
                dve.memset(mean_col[:], 1.0 / P)
                dve.memset(ones[:], 1.0)
                dve.memset(eps_col[:], EPS)
                dve.memset(attn_eps_col[:], ATTN_EPS)
                dve.memset(power_half[:], -0.5)
                dve.memset(power_one[:], -1.0).then_inc(made, 1)
                dve.wait_ge(loaded, 64)
                dve.tensor_copy(pick[:], pick_raw[:]).then_inc(made, 1)
                dve.wait_ge(made, 2)

        with ExitStack() as ctx:
            setup(sem_of(ctx), sb_of(ctx)("pick_raw", [2 * GROUPS, GROUPS, P]), ctx.enter_context(nc.Block()))

        with ExitStack() as ctx:
            sem, sb = sem_of(ctx), sb_of(ctx)
            first_layer(nc, A, sem, sb, ctx, locals())

        Z = whole.enter_context(nc.sbuf_tensor("Z", [P, TOK], F32))
        XH = whole.enter_context(nc.sbuf_tensor("XH", [P, TOK], F32R))
        XL = whole.enter_context(nc.sbuf_tensor("XL", [P, TOK], F32R))
        combine = nc.dram_tensor("combine", (EXPERTS, TOK), F32, kind="Internal").ap()
        with ExitStack() as ctx:
            sem, sb = sem_of(ctx), sb_of(ctx)
            routing(nc, A, sem, sb, ctx, locals())
        with ExitStack() as ctx:
            sem, sb = sem_of(ctx), sb_of(ctx)
            second_layer(nc, A, sem, sb, ctx, locals())


def first_layer(nc, A, sem, sb, ctx, g):
    X, ident, centre, mean_col = g["X"], g["ident"], g["centre"], g["mean_col"]
    banks, LNB, XC, SQ, XS, HI, LO, SH = (g[k] for k in ("banks", "LNB", "XC", "SQ", "XS", "HI", "LO", "SH"))
    split3, PerToken = g["split3"], g["PerToken"]
    pe_sums, act_var, pool_power, pe_turn, act_rows, pe_spread, act_centred = (
        g[k] for k in ("pe_sums", "act_var", "pool_power", "pe_turn", "act_rows", "pe_spread", "act_centred"))
    power_half, power_one, eps_col, attn_eps_col = (
        g[k] for k in ("power_half", "power_one", "eps_col", "attn_eps_col"))

    GUH = sb("GUH", [P, EXPERTS, 2 * FF], F32R)
    GUL = sb("GUL", [P, EXPERTS, 2 * FF], F32R)
    WD = sb("WD", [P, EXPERTS, CHUNKS, P])
    raw = sb("raw0", [P, 2, 2 * FF])
    AW = 3 * P + 2 * H0
    attn_raw = sb("attn_raw", [P, AW])
    AH = sb("AH", [P, AW], F32R)
    AL = sb("AL", [P, AW], F32R)
    WDA = sb("WDA", [P, 3, P])
    kv_bias = sb("kv_bias", [P, 2 * P])
    cols = sb("cols0", [P, 16])
    BQ, BG, BU, BD, G1, B1, G2, B2 = 0, 1, 4, 7, 8, 9, 10, 11
    XN = sb("XN", [P, HALVES, TILE])
    NH = sb("NH", [P, HALVES, TILE], F32R)
    NL = sb("NL", [P, HALVES, TILE], F32R)
    KV = sb("KV", [P, HALVES * GROUPS, 2 * P + 2])
    KE = sb("KE", [P, GROUPS, P])
    KVS = sb("KVS", [P, P + 2])
    QB = sb("QB", [P, TILE])
    QE = sb("QE", [P, TILE])
    QP = sb("QP", [P, TILE])
    Y = sb("Y", [P, TILE])
    X1 = sb("X1", [P, TILE])
    S2 = sb("S2", [P, TILE])
    H2 = sb("H2", [P, 3, TILE])
    GX = sb("GX", [P, HALVES, TILE])

    STEPS = HALVES * EXPERTS * CHUNKS
    PT = 4 * HALVES
    ps = PerToken(sem, PT)
    small_loaded, wd_loaded = sem("small_loaded"), sem("wd_loaded")
    raw_loaded = [sem(f"raw_loaded{i}") for i in range(2)]
    hi_split, lo_split, attn_hi, attn_lo = sem("hi_split"), sem("lo_split"), sem("attn_hi"), sem("attn_lo")
    ones_set = sem("ones_set")
    gate_done, up_done, silu_done, h_ready, down_done = (
        sem(n) for n in ("gate_done", "up_done", "silu_done", "h_ready", "down_done"))
    o_added = sem("o_added")
    kv_done, kv_biased, k_min, k_exp, k_ready = (sem(n) for n in ("kv_done", "kv_biased", "k_min", "k_exp", "k_ready"))
    kvs_done, kvs_copied = sem("kvs_done"), sem("kvs_copied")
    q_done, q_copied, q_min, q_exp, q_ready = (sem(n) for n in ("q_done", "q_copied", "q_min", "q_exp", "q_ready"))
    y_ready, x1_ready = sem("y_ready"), sem("x1_ready")
    gu2_done, silu2_done, h2_ready, down2_done = (sem(n) for n in ("gu2_done", "silu2_done", "h2_ready", "down2_done"))
    x_ready, xs_kept = sem("x_ready"), sem("xs_kept")

    def schedule():
        out = []
        ffn = iter(range(STEPS))

        def f(n=1):
            for _ in range(n):
                s = next(ffn, None)
                if s is not None:
                    out.append(("expert", s))

        def scaling(n, last, gaps=(1, 2, 1)):
            out.append(("centre", n))
            f(gaps[0])
            out.append(("sums", n))
            f(gaps[1])
            out.append(("turn", n))
            f(gaps[2])
            out.append(("spread", n))
            out.append((last, n))

        n = iter(range(PT))
        for h in range(HALVES):
            scaling((next(n), h, "norm0"), "end_norm0", (1, 2, 1) if h else (0, 0, 0))
        f(1)
        for h in range(HALVES):
            out.append(("keys", h))
            f(3)
        out.append(("kv_sum", 0))
        f(2)
        for h in range(HALVES):
            out.append(("query", h))
            f(3)
            scaling((next(n), h, "attn"), "end_attn")
            f(1)
            scaling((next(n), h, "norm1"), "end_norm1")
            f(1)
            out.append(("ffn2", h))
            f(1)
            scaling((next(n), h, "norm2"), "end_norm2")
            f(1)
        f(STEPS)
        out.append(("expert_end", STEPS))
        return out

    SCHEDULE = schedule()
    MARKS = {(k[2], k[1]): k[0] for name, k in SCHEDULE if name == "centre"}

    def x_tile(b, h):
        return X[:, bass.ds(b * SEQ + h * TILE, TILE)]

    def attn_cols(part, lo):
        w = AL if lo else AH
        return w[:, part * P:(part + 1) * P]

    def ffn2_cols(up, c, lo):
        w = AL if lo else AH
        a = 3 * P + up * H0 + c * P
        return w[:, a:a + H0_ROWS[c]]

    block = ctx.enter_context(nc.Block())

    @block.sync
    def _(sp):
        loads = [(attn_raw[:], A["w0_attn"]), (kv_bias[:], A["kv_bias"].broadcast_to([P, 2 * P])),
                 (cols[:, 0:12], A["cols0"]), (WDA[:, 0:2, :], A["w0_down"][0:2 * P, :].rearrange("(c p) n -> p c n", p=P)),
                 (WDA[0:H0_ROWS[2], 2, :], A["w0_down"][2 * P:H0, :])]
        for dst, src in loads:
            sp.dma_start(dst, src).then_inc(small_loaded, 16)
        for e in range(EXPERTS):
            if e >= 2:
                sp.wait_ge(lo_split, e - 1)
            sp.dma_start(raw[:, e % 2, :], A["w0_gu"][e]).then_inc(raw_loaded[e % 2], 16)
        sp.dma_start(WD[:], A["w0_d"]).then_inc(wd_loaded, 16)
        sp.wait_ge(x_ready, BATCHES * HALVES)

    @block.scalar
    def _(act):
        act.wait_ge(small_loaded, 16 * 5)
        act.activation(AH[:], attn_raw[:], ACT.Copy).then_inc(attn_hi, 1)
        for e in range(EXPERTS):
            act.wait_ge(raw_loaded[e % 2], 16 * (e // 2 + 1))
            act.activation(GUH[:, e, :], raw[:, e % 2, :], ACT.Copy).then_inc(hi_split, 1)

        def body(b):
            for name, k in SCHEDULE:
                if name == "expert":
                    act.wait_ge(gate_done, b * STEPS + k + 1)
                    act.wait_ge(down_done, b * STEPS + max(k - 3, 0))
                    act.activation(SH[:, k % 4, :], banks[k % 2][:], ACT.Silu).then_inc(silu_done, 1)
                elif name == "centre":
                    n, h, kind = k
                    if kind == "attn":
                        act.wait_ge(ps.source_done, ps.at(b, n + 1))
                        act.wait_ge(ps.scaled, ps.at(b, n))
                        act.activation(XC[:], LNB[:], ACT.Copy).then_inc(ps.copied, 1)
                    else:
                        act_centred(act, ps, b, n)
                elif name == "sums":
                    act_var(act, ps, b, k[0], attn_eps_col[:] if k[2] == "attn" else eps_col[:])
                elif name == "turn":
                    act_rows(act, ps, b, k[0])
                elif name == "end_norm0":
                    n, h, _ = k
                    act.wait_ge(ps.scaled, ps.at(b, n + 1))
                    act.wait_ge(up_done, b * STEPS)
                    act.wait_ge(q_done, b * HALVES)
                    act.activation(NH[:, h, :], XN[:, h, :], ACT.Copy).then_inc(ps.hi_done, 1)
                elif name == "keys":
                    act.wait_ge(kv_biased, (b * HALVES + k) * 2 + 2)
                    act.wait_ge(k_ready, b * HALVES + k)
                    act.activation(KE[:], KV[:, k * GROUPS:(k + 1) * GROUPS, 0:P], ACT.Relu, scale=-1.0).then_inc(k_min, 1)
                    act.wait_ge(k_min, b * HALVES + k + 1)
                    act.activation(KE[:], KE[:], ACT.Exp, scale=-1.0).then_inc(k_exp, 1)
                elif name == "kv_sum":
                    act.wait_ge(kvs_done, b + 1)
                    act.wait_ge(ps.sums_done, ps.at(b, 0))
                    act.activation(KVS[:], banks[6][:, 0:P + 2], ACT.Copy).then_inc(kvs_copied, 1)
                elif name == "query":
                    act.wait_ge(q_done, b * HALVES + k + 1)
                    act.wait_ge(q_ready, b * HALVES + k)
                    act.activation(QB[:], banks[7][:], ACT.Identity, bias=cols[:, BQ:BQ + 1]).then_inc(q_copied, 1)
                    act.wait_ge(q_copied, b * HALVES + k + 1)
                    act.activation(QE[:], QB[:], ACT.Relu, scale=-1.0).then_inc(q_min, 1)
                    act.wait_ge(q_min, b * HALVES + k + 1)
                    act.activation(QE[:], QE[:], ACT.Exp, scale=-1.0).then_inc(q_exp, 1)
                elif name == "end_norm1":
                    n, h, _ = k
                    act.wait_ge(ps.scaled, ps.at(b, n + 1))
                    act.wait_ge(y_ready, b * 2 * HALVES + 2 * h)
                    act.activation(X1[:], XS[:], ACT.Identity, bias=cols[:, B1:B1 + 1],
                                   scale=cols[:, G1:G1 + 1]).then_inc(x1_ready, 1)
                    act.wait_ge(x1_ready, b * HALVES + h + 1)
                    act.wait_ge(gu2_done, (b * HALVES + h) * 3)
                    act.activation(HI[:], X1[:], ACT.Copy).then_inc(ps.hi_done, 1)
                elif name == "ffn2":
                    for c in range(3):
                        m = H0_ROWS[c]
                        act.wait_ge(gu2_done, (b * HALVES + k) * 3 + c + 1)
                        act.wait_ge(h2_ready, (b * HALVES + k) * 3 + c)
                        act.activation(S2[0:m, :], banks[6][0:m, :], ACT.Silu,
                                       bias=cols[0:m, BG + c:BG + c + 1]).then_inc(silu2_done, 1)

        with act.Fori(0, BATCHES) as b:
            body(b)

    @block.gpsimd
    def _(pool):
        pool.memset(KV[:, :, 2 * P:], 1.0).then_inc(ones_set, 1)

        def body(b):
            for name, k in SCHEDULE:
                if name == "sums":
                    pool_power(pool, ps, b, k[0], power_one if k[2] == "attn" else power_half)
                elif name == "end_norm0":
                    n, h, _ = k
                    pool.wait_ge(ps.hi_done, 2 * HALVES * b + h + 1)
                    pool.tensor_tensor(NL[:, h, :], XN[:, h, :], NH[:, h, :].bitcast(F32),
                                       ALU.subtract).then_inc(ps.lo_done, 1)
                elif name == "end_norm1":
                    n, h, _ = k
                    pool.wait_ge(ps.hi_done, 2 * HALVES * b + HALVES + h + 1)
                    pool.wait_ge(gu2_done, (b * HALVES + h) * 3)
                    pool.tensor_tensor(LO[:], X1[:], HI[:].bitcast(F32), ALU.subtract).then_inc(ps.lo_done, 1)

        with pool.Fori(0, BATCHES) as b:
            body(b)

    @block.vector
    def _(dve):
        dve.wait_ge(attn_hi, 1)
        dve.tensor_tensor(AL[:], attn_raw[:], AH[:].bitcast(F32), ALU.subtract).then_inc(attn_lo, 1)
        for e in range(EXPERTS):
            dve.wait_ge(hi_split, e + 1)
            dve.tensor_tensor(GUL[:, e, :], raw[:, e % 2, :], GUH[:, e, :].bitcast(F32),
                              ALU.subtract).then_inc(lo_split, 1)

        def add_experts(b, h):
            dve.wait_ge(down_done, b * STEPS + (h + 1) * EXPERTS * CHUNKS)
            dve.scalar_tensor_tensor(x_tile(b, h), banks[4][:], cols[:, B2:B2 + 1], x_tile(b, h),
                                     ALU.add, ALU.add).then_inc(o_added, 1)

        def body(b):
            for name, k in SCHEDULE:
                if name == "expert":
                    dve.wait_ge(silu_done, b * STEPS + k + 1)
                    dve.wait_ge(up_done, b * STEPS + k + 1)
                    dve.tensor_tensor(SH[:, k % 4, :], SH[:, k % 4, :], banks[2 + k % 2][:],
                                      ALU.mult).then_inc(h_ready, 1)
                    if k > EXPERTS * CHUNKS and k % (EXPERTS * CHUNKS) == 1:
                        add_experts(b, k // (EXPERTS * CHUNKS) - 1)
                elif name == "expert_end":
                    add_experts(b, HALVES - 1)
                    for h in range(HALVES):
                        dve.wait_ge(o_added, b * HALVES + h + 1)
                        dve.wait_ge(ps.scaled, ps.at(b, MARKS["norm2", h] + 1))
                        dve.tensor_tensor(x_tile(b, h), x_tile(b, h), GX[:, h, :], ALU.add).then_inc(x_ready, 1)
                elif name == "spread":
                    n, h, kind = k
                    dve.wait_ge(ps.spread, ps.at(b, n + 1))
                    if kind == "norm0":
                        dve.wait_ge(y_ready, b * 2 * HALVES)
                        dve.wait_ge(ps.lo_done, 2 * HALVES * b)
                        dve.tensor_tensor(XN[:, h, :], XC[:], LNB[:], ALU.mult).then_inc(ps.scaled, 1)
                    else:
                        dve.wait_ge(x1_ready, b * HALVES + (h if kind != "norm2" else h + 1))
                        dve.wait_ge(y_ready, b * 2 * HALVES + 2 * h + (0 if kind == "attn" else 1 if kind == "norm1" else 2))
                        dve.wait_ge(xs_kept, b * HALVES + h)
                        dve.tensor_tensor(XS[:], XC[:], LNB[:], ALU.mult).then_inc(ps.scaled, 1)
                elif name == "keys":
                    for half in range(2):
                        dve.wait_ge(kv_done, (b * HALVES + k) * 2 + half + 1)
                        if half == 0 and k == 0:
                            dve.wait_ge(kvs_done, b)
                            dve.wait_ge(small_loaded, 16 * 5)
                        i = k * GROUPS + 2 * half
                        dve.tensor_tensor(KV[:, i:i + 2, 0:2 * P],
                                          banks[6 + half][:].rearrange("p (a n) -> p a n", a=2),
                                          kv_bias[:].unsqueeze(1).broadcast_to([P, 2, 2 * P]),
                                          ALU.add).then_inc(kv_biased, 1)
                    dve.wait_ge(k_exp, b * HALVES + k + 1)
                    kk = KV[:, k * GROUPS:(k + 1) * GROUPS, 0:P]
                    dve.scalar_tensor_tensor(kk, kk, 0.0, KE[:], ALU.max, ALU.add).then_inc(k_ready, 1)
                elif name == "query":
                    dve.wait_ge(q_exp, b * HALVES + k + 1)
                    if k == 0:
                        dve.wait_ge(ps.sums_done, ps.at(b, 0))
                    else:
                        dve.wait_ge(ps.sums_done, ps.at(b, MARKS["attn", k - 1] + 1))
                    dve.scalar_tensor_tensor(QP[:], QB[:], 0.0, QE[:], ALU.max, ALU.add).then_inc(q_ready, 1)
                elif name == "end_attn":
                    n, h, _ = k
                    dve.wait_ge(ps.scaled, ps.at(b, n + 1))
                    dve.wait_ge(ps.source_done, ps.at(b, n))
                    dve.tensor_tensor(Y[:], XS[:], XN[:, h, :], ALU.add).then_inc(y_ready, 1)
                elif name == "ffn2":
                    for c in range(3):
                        m = H0_ROWS[c]
                        dve.wait_ge(silu2_done, (b * HALVES + k) * 3 + c + 1)
                        dve.wait_ge(down2_done, b * HALVES + k)
                        dve.scalar_tensor_tensor(H2[0:m, c, :], banks[7][0:m, :], cols[0:m, BU + c:BU + c + 1],
                                                 S2[0:m, :], ALU.add, ALU.mult).then_inc(h2_ready, 1)
                    dve.wait_ge(down2_done, b * HALVES + k + 1)
                    dve.scalar_tensor_tensor(Y[:], LNB[:], cols[:, BD:BD + 1], X1[:],
                                             ALU.add, ALU.add).then_inc(y_ready, 1)
                elif name == "end_norm2":
                    n, h, _ = k
                    dve.wait_ge(ps.scaled, ps.at(b, n + 1))
                    dve.wait_ge(x_ready, b * HALVES)
                    dve.tensor_scalar(GX[:, h, :], XS[:], cols[:, G2:G2 + 1], None, ALU.mult).then_inc(xs_kept, 1)

        with dve.Fori(0, BATCHES) as b:
            body(b)

    @block.tensor
    def _(pe):
        pe.wait_ge(attn_lo, 1)
        pe.wait_ge(lo_split, EXPERTS)
        pe.wait_ge(wd_loaded, 16)
        pe.wait_ge(small_loaded, 16 * 5)
        pe.wait_ge(ones_set, 1)

        def down(b, s):
            e, c = s // CHUNKS % EXPERTS, s % CHUNKS
            first, last = s % (EXPERTS * CHUNKS) == 0, s % (EXPERTS * CHUNKS) == EXPERTS * CHUNKS - 1
            pe.wait_ge(h_ready, b * STEPS + s + 1)
            if first:
                pe.wait_ge(o_added, b * HALVES + s // (EXPERTS * CHUNKS))
            mm = pe.matmul(banks[4][:], WD[:, e, c, :], SH[:, s % 4, :], start=first, stop=last)
            mm.then_inc(down_done, 1)

        def body(b):
            for name, k in SCHEDULE:
                if name == "expert":
                    e, c, h = k // CHUNKS % EXPERTS, k % CHUNKS, k // (CHUNKS * EXPERTS)
                    if k % (EXPERTS * CHUNKS) == 0:
                        pe.wait_ge(ps.lo_done, 2 * HALVES * b + h + 1)
                    a = c * P
                    pe.wait_ge(silu_done, b * STEPS + max(k - 1, 0))
                    split3(pe, banks[k % 2][:], GUH[:, e, a:a + P], GUL[:, e, a:a + P],
                           NH[:, h, :], NL[:, h, :]).then_inc(gate_done, 1)
                    pe.wait_ge(h_ready, b * STEPS + max(k - 1, 0))
                    a += FF
                    split3(pe, banks[2 + k % 2][:], GUH[:, e, a:a + P], GUL[:, e, a:a + P],
                           NH[:, h, :], NL[:, h, :]).then_inc(up_done, 1)
                    if k > 1:
                        down(b, k - 2)
                elif name == "expert_end":
                    down(b, STEPS - 2)
                    down(b, STEPS - 1)
                elif name == "centre":
                    n, h, kind = k
                    pe.wait_ge(ps.scaled, ps.at(b, n))
                    pe.wait_ge(y_ready, b * 2 * HALVES + (0 if kind == "norm0" else 2 * h + (0 if kind == "attn" else 1 if kind == "norm1" else 2)))
                    if kind == "attn":
                        pe.wait_ge(q_ready, b * HALVES + h + 1)
                        pe.matmul(LNB[:], KVS[:, 0:P], QP[:], start=True, stop=True).then_inc(ps.source_done, 1)
                    elif kind == "norm0":
                        pe.matmul(LNB[:], centre[:], x_tile(b, h), start=True, stop=True).then_inc(ps.source_done, 1)
                    else:
                        pe.matmul(LNB[:], centre[:], Y[:], start=True, stop=True).then_inc(ps.source_done, 1)
                elif name == "sums":
                    if k[2] == "attn":
                        pe_sums(pe, ps, b, k[0], QP, KVS[:, P:P + 1])
                    else:
                        pe_sums(pe, ps, b, k[0], SQ, mean_col[:])
                elif name == "turn":
                    pe_turn(pe, ps, b, k[0])
                elif name == "spread":
                    pe_spread(pe, ps, b, k[0])
                elif name == "keys":
                    h = k
                    pe.wait_ge(ps.lo_done, 2 * HALVES * b + h + 1)
                    for half in range(2):
                        if h > 0:
                            pe.wait_ge(kv_biased, (b * HALVES + h) * 2 - 1 + half)
                        else:
                            pe.wait_ge(kv_biased, b * HALVES * 2)
                            pe.wait_ge(h2_ready, b * HALVES * 3)
                        for i in range(2):
                            t = slice((2 * half + i) * P, (2 * half + i + 1) * P)
                            mm = split3(pe, banks[6 + half][:, i * 2 * P:(i + 1) * 2 * P],
                                        NH[:, h, t], NL[:, h, t], AH[:, P:3 * P], AL[:, P:3 * P])
                        mm.then_inc(kv_done, 1)
                elif name == "kv_sum":
                    pe.wait_ge(k_ready, (b + 1) * HALVES)
                    n = HALVES * GROUPS
                    for i in range(n):
                        mm = pe.matmul(banks[6][:, 0:P + 2], KV[:, i, 0:P], KV[:, i, P:2 * P + 2],
                                       start=(i == 0), stop=(i == n - 1))
                    mm.then_inc(kvs_done, 1)
                elif name == "query":
                    if k > 0:
                        pe.wait_ge(h2_ready, (b * HALVES + k) * 3)
                    pe.wait_ge(kv_biased, (b + 1) * 2 * HALVES)
                    split3(pe, banks[7][:], attn_cols(0, 0), attn_cols(0, 1), NH[:, k, :], NL[:, k, :]).then_inc(q_done, 1)
                    pe.wait_ge(kvs_copied, b + 1)
                elif name == "ffn2":
                    pe.wait_ge(ps.lo_done, 2 * HALVES * b + HALVES + k + 1)
                    pe.wait_ge(ps.scaled, ps.at(b, MARKS["norm1", k] + 1))
                    for c in range(3):
                        m = H0_ROWS[c]
                        pe.wait_ge(h2_ready, (b * HALVES + k) * 3 + c)
                        for up in range(2):
                            mm = split3(pe, banks[6 + up][0:m, :], ffn2_cols(up, c, 0), ffn2_cols(up, c, 1), HI[:], LO[:])
                        mm.then_inc(gu2_done, 1)
                    for c in range(3):
                        m = H0_ROWS[c]
                        pe.wait_ge(h2_ready, (b * HALVES + k) * 3 + c + 1)
                        mm = pe.matmul(LNB[:], WDA[0:m, c, :], H2[0:m, c, :], start=(c == 0), stop=(c == 2))
                    mm.then_inc(down2_done, 1)

        with pe.Fori(0, BATCHES) as b:
            body(b)


def routing(nc, A, sem, sb, ctx, g):
    X, Z, XH, XL, combine, ident, centre, mean_col = (
        g[k] for k in ("X", "Z", "XH", "XL", "combine", "ident", "centre", "mean_col"))
    banks, LNB, XC, SQ, XS = (g[k] for k in ("banks", "LNB", "XC", "SQ", "XS"))
    pe_sums, act_var, pool_power, pe_turn, act_rows, pe_spread, act_centred = (
        g[k] for k in ("pe_sums", "act_var", "pool_power", "pe_turn", "act_rows", "pe_spread", "act_centred"))
    ps = g["PerToken"](sem, 1)
    NG = TOK // P
    WIDE = [P, NG, EXPERTS]

    conf = sb("conf", [P, EXPERTS])
    rows = sb("rows", [P, 3, EXPERTS])
    LG = sb("LG", WIDE)
    TH = sb("TH", WIDE)
    BID = sb("BID", WIDE)
    LEFT = sb("LEFT", WIDE)
    EQ = sb("EQ", WIDE)
    ONE1 = sb("ONE1", WIDE)
    ONE2 = sb("ONE2", WIDE)
    CW = sb("CW", [P, EXPERTS, NG])
    M1, M2, F1, F2, DIF, EX, SUM, W1, W2 = (sb(n, [P, NG]) for n in ("M1", "M2", "F1", "F2", "DIF", "EX", "SUM", "W1", "W2"))
    CT = sb("CT", [P, 2, P])

    rows_loaded = sem("rows_loaded")
    logits_done, logits_copied, z_done, xh_done, xl_done = (
        sem(n) for n in ("logits_done", "logits_copied", "z_done", "xh_done", "xl_done"))
    biased, tanh_done, dif_done, exp_done, cw_done, cw_turned, ct_copied, stored, chain = (
        sem(n) for n in ("biased", "tanh_done", "dif_done", "exp_done", "cw_done", "cw_turned", "ct_copied", "stored", "chain"))

    block = ctx.enter_context(nc.Block())

    @block.sync
    def _(sp):
        sp.dma_start(conf[:], A["conf_w"]).then_inc(rows_loaded, 16)
        for i, name in enumerate(("conf_b", "wealth", "c_rank")):
            sp.dma_start(rows[:, i, :], A[name].broadcast_to([P, EXPERTS])).then_inc(rows_loaded, 16)
        sp.wait_ge(ct_copied, 2)
        sp.dma_start(combine.rearrange("e (j k) -> (e j) k", k=P).rearrange("(a r) k -> r a k", a=2),
                     CT[:]).then_inc(stored, 16)
        sp.wait_ge(stored, 16)

    @block.scalar
    def _(act):
        with act.Fori(0, TILES) as t:
            act_centred(act, ps, t, 0)
            act_var(act, ps, t, 0, g["eps_col"][:])
            act_rows(act, ps, t, 0)
            act.wait_ge(ps.scaled, t + 1)
            act.activation(Z[:, bass.ds(t * TILE, TILE)], XS[:], ACT.Copy).then_inc(z_done, 1)
            act.activation(XH[:, bass.ds(t * TILE, TILE)], XS[:], ACT.Copy).then_inc(xh_done, 1)
            act.wait_ge(logits_done, t + 1)
            act.activation(LG[:, bass.ds(t * GROUPS, GROUPS), :],
                           banks[6][:, 0:GROUPS * EXPERTS].rearrange("p (g e) -> p g e", e=EXPERTS),
                           ACT.Copy).then_inc(logits_copied, 1)
        act.wait_ge(biased, 1)
        act.activation(TH[:], LG[:], ACT.Tanh, scale=0.5).then_inc(tanh_done, 1)
        act.wait_ge(dif_done, 1)
        act.activation(EX[:], DIF[:], ACT.Exp).then_inc(exp_done, 1)
        for i in range(2):
            act.wait_ge(cw_turned, i + 1)
            act.activation(CT[:, i, :], banks[6 + i][:, 0:P], ACT.Copy).then_inc(ct_copied, 1)

    @block.gpsimd
    def _(pool):
        with pool.Fori(0, TILES) as t:
            pool_power(pool, ps, t, 0, g["power_half"])

    @block.vector
    def _(dve):
        with dve.Fori(0, TILES) as t:
            dve.wait_ge(ps.spread, t + 1)
            dve.wait_ge(logits_done, t)
            dve.wait_ge(xl_done, t)
            dve.tensor_tensor(XS[:], XC[:], LNB[:], ALU.mult).then_inc(ps.scaled, 1)
            dve.wait_ge(xh_done, t + 1)
            dve.tensor_tensor(XL[:, bass.ds(t * TILE, TILE)], XS[:], XH[:, bass.ds(t * TILE, TILE)].bitcast(F32),
                              ALU.subtract).then_inc(xl_done, 1)

        count = [0]

        def link(ins):
            count[0] += 1
            ins.then_inc(chain, 1)
            dve.wait_ge(chain, count[0])

        def wide(ap):
            return ap.unsqueeze(1).broadcast_to(WIDE)

        def deep(ap):
            return ap.unsqueeze(2).broadcast_to(WIDE)

        dve.wait_ge(logits_copied, TILES)
        dve.wait_ge(rows_loaded, 64)
        dve.tensor_tensor(LG[:], LG[:], wide(rows[:, 0, :]), ALU.add).then_inc(biased, 1)
        dve.wait_ge(tanh_done, 1)
        link(dve.tensor_scalar(TH[:], TH[:], 0.5, 0.5, ALU.mult, ALU.add))
        link(dve.tensor_tensor(BID[:], TH[:], wide(rows[:, 1, :]), ALU.mult))
        link(dve.tensor_reduce(M1[:], BID[:], AX.X, ALU.max))
        link(dve.tensor_tensor(EQ[:], BID[:], deep(M1[:]), ALU.is_equal))
        link(dve.tensor_tensor(EQ[:], EQ[:], wide(rows[:, 2, :]), ALU.mult))
        link(dve.tensor_reduce(F1[:], EQ[:], AX.X, ALU.max))
        link(dve.tensor_tensor(ONE1[:], deep(F1[:]), wide(rows[:, 2, :]), ALU.is_equal))
        link(dve.scalar_tensor_tensor(LEFT[:], ONE1[:], -3.0e38, BID[:], ALU.mult, ALU.add))
        link(dve.tensor_reduce(M2[:], LEFT[:], AX.X, ALU.max))
        link(dve.tensor_tensor(EQ[:], LEFT[:], deep(M2[:]), ALU.is_equal))
        link(dve.tensor_tensor(EQ[:], EQ[:], wide(rows[:, 2, :]), ALU.mult))
        link(dve.tensor_reduce(F2[:], EQ[:], AX.X, ALU.max))
        link(dve.tensor_tensor(ONE2[:], deep(F2[:]), wide(rows[:, 2, :]), ALU.is_equal))
        dve.tensor_tensor(DIF[:], M2[:], M1[:], ALU.subtract).then_inc(dif_done, 1)
        dve.wait_ge(exp_done, 1)
        link(dve.tensor_scalar(SUM[:], EX[:], 1.0, None, ALU.add))
        link(dve.reciprocal(W1[:], SUM[:]))
        link(dve.tensor_tensor(W2[:], EX[:], W1[:], ALU.mult))
        link(dve.tensor_tensor(ONE1[:], ONE1[:], deep(W1[:]), ALU.mult))
        link(dve.tensor_tensor(ONE2[:], ONE2[:], deep(W2[:]), ALU.mult))
        dve.tensor_tensor(CW[:].rearrange("p e j -> p j e"), ONE1[:], ONE2[:], ALU.add).then_inc(cw_done, 1)

    @block.tensor
    def _(pe):
        pe.wait_ge(rows_loaded, 64)
        with pe.Fori(0, TILES) as t:
            pe.wait_ge(ps.scaled, t)
            pe.matmul(LNB[:], centre[:], X[:, bass.ds(t * TILE, TILE)], start=True, stop=True).then_inc(ps.source_done, 1)
            pe_sums(pe, ps, t, 0, SQ, mean_col[:])
            pe_turn(pe, ps, t, 0)
            pe_spread(pe, ps, t, 0)
            pe.wait_ge(ps.scaled, t + 1)
            pe.wait_ge(logits_copied, t)
            for j in range(GROUPS):
                mm = pe.matmul(banks[6][:, j * EXPERTS:(j + 1) * EXPERTS], XS[:, j * P:(j + 1) * P], conf[:],
                               start=True, stop=True)
            mm.then_inc(logits_done, 1)
        pe.wait_ge(cw_done, 1)
        pe.wait_ge(logits_copied, TILES)
        for i in range(2):
            pe.transpose(banks[6 + i][:, 0:P], CW[:].rearrange("p e j -> p (e j)")[:, i * P:(i + 1) * P],
                         ident[:]).then_inc(cw_turned, 1)


class Pipeline:

    STEP = 8
    EARLY = 6
    VIEWS = (-4.25, -3.69, -3.07)
    HAM = (0.78, 1.32, 1.34, 1.7, 1.93, 2.01, 2.45, 2.51, 3.49, 4.57, 5.74, 6.25, 6.9)
    SCALINGS = {"A": {"centre": -11.36, "sums": -10.38, "turn": -9.04, "spread": -8.99, "halves": -5.41},
                "C": {"centre": 16.82, "sums": 17.15, "turn": 18.17, "spread": 19.21, "halves": 24.0}}
    TILE = {"turns": -2.53, "round": -1.69, "cosines": 0.49, "fold": 8.79, "freq": 14.27, "gain": 14.33,
            "proj": 15.15, "proj_add": 15.92, "fc_a": 25.43, "fc_b": 25.83, "mproj": 26.03,
            "mlp_add": 26.27}

    def __init__(self):
        span, out = TILES * self.STEP, []
        STEPS = PER_LAYER * TILES * CHUNKS
        cut = -self.EARLY - 0.5
        for l in range(LAYERS):
            def put(place, name, k=0):
                out.append((l * span + place, len(out), name, l, k))

            for s in range(STEPS):
                put(s * (1.3 if l == LAYERS - 1 else 1) - self.EARLY, "expert", s)
            for e, (load, split, down) in enumerate(((-46, -22, -34.8), (-18, 10, -2.8))):
                put(load, "load_up", e)
                put(split, "split_expert", e)
                put(down, "load_down", e)
            put(-24, "load_attn")
            put(-10, "prep_views")
            put(10.5, "prep_proj")
            put(18.4, "load_mproj")
            put(18.6, "prep_fc")
            for t in range(TILES):
                a = t * self.STEP
                for j, place in enumerate(self.VIEWS):
                    put(a + place, "views", (t, j))
                for i, place in enumerate(self.HAM):
                    put(a + place, "ham", (t, i))
                for name, place in self.TILE.items():
                    put(a + place, name, t)
                for kind, places in self.SCALINGS.items():
                    for name, place in places.items():
                        put(a + place, name, (t, kind))
                if l == LAYERS - 1:
                    put(max(a + self.TILE["mlp_add"] + 1, 1.3 * (STEPS // 2 + CHUNKS * t + 8) - self.EARLY), "out", t)
        out.sort()
        names = sorted({x[2] for x in out})
        self.per_layer = {n: sum(1 for x in out if x[2] == n and x[3] == 0) for n in names}
        self.windows = [[] for _ in range(LAYERS)]
        users = (("freq", "gain"), ("proj", "proj_add"), ("mproj", "mlp_add"), ("fc_a", "fc_b"))
        seen = dict.fromkeys(names, 0)
        for place, _, name, l, k in out:
            w = min(max(int((place - cut) // span), 0), LAYERS - 1)
            self.windows[w].append((name, l - w, k, dict(seen)))
            if name in ("freq", "proj", "mproj", "fc_a", "views", "prep_views", "prep_fc", "prep_proj"):
                assert all(seen[a] == seen[b] for a, b in users if a != "freq" or name not in ("proj", "mproj"))
            seen[name] += 1
        same = [[x[:3] for x in w] for w in self.windows[1:-1]]
        assert all(x == same[0] for x in same)

    def steps(self, w, layer):
        for name, off, k, seen in self.windows[w]:
            def before(other, seen=seen):
                return seen[other] if isinstance(layer, int) else (layer - w) * self.per_layer[other] + seen[other]
            yield name, layer + off, k, before

    def run(self, engine, body):
        body(0, 0)
        with engine.Fori(1, LAYERS - 1) as l:
            body(1, l)
        body(LAYERS - 1, LAYERS - 1)


def second_layer(nc, A, sem, sb, ctx, g):
    X, Z, XH, XL, combine, ident, centre, mean_col = (
        g[k] for k in ("X", "Z", "XH", "XL", "combine", "ident", "centre", "mean_col"))
    banks, LNB, XC, SQ, XS, HI, LO, SH = (g[k] for k in ("banks", "LNB", "XC", "SQ", "XS", "HI", "LO", "SH"))
    split3 = g["split3"]
    pe_sums, act_var, pool_power, pe_turn, act_rows, pe_spread, act_centred = (
        g[k] for k in ("pe_sums", "act_var", "pool_power", "pe_turn", "act_rows", "pe_spread", "act_centred"))

    W = TILE + 2
    VIEWS = 6
    GUH = sb("GUH2", [P, PER_LAYER, 2 * FF], F32R)
    GUL = sb("GUL2", [P, PER_LAYER, 2 * FF], F32R)
    WD = sb("WD2", [P, PER_LAYER, CHUNKS, P])
    raw = sb("raw2", [P, 2 * FF])
    QRAW = sb("QRAW", [P, VIEWS * P])
    FRAW = sb("FRAW", [P, 4 * P])
    PRAW = sb("PRAW", [P, P])
    LC = sb("LC", [P, LAYERS, 16])
    LQ = sb("LQ", [P, 16])
    LP = sb("LP", [P, 16])
    LF = sb("LF", [P, 16])
    BIAS = sb("BIAS", [P, 10])
    PB, MB, G1, B1, G2, B2 = 14, 15, 10, 11, 12, 13
    WQH = sb("WQH", [P, VIEWS * P], F32R)
    WQL = sb("WQL", [P, VIEWS * P], F32R)
    FCH = sb("FCH", [P, 4 * P], F32R)
    FCL = sb("FCL", [P, 4 * P], F32R)
    WP = sb("WP", [P, P])
    MP = sb("MP", [P, 4, P])
    hartley = sb("hartley", [P, P])
    GAIN = sb("GAIN", [P, SEQ])
    quarter = sb("quarter", [P, 1])
    rounder = sb("rounder", [P, 1])
    unrounder = sb("unrounder", [P, 1])
    QK = sb("QK", [P, 2, 4, W])
    V = sb("V", [P, 2, 4, W])
    TURNS = sb("TURNS", [P, 3, TILE])
    AM = sb("AM", [P, 4, TILE])
    TA = sb("TA", [P, 4, TILE])
    XG = sb("XG", [P, TILE])
    GE = sb("GE", [P, 4, TILE])
    CB = sb("CB", [P, 2, TILE])
    CO = sb("CO", [P, TILE])

    STEPS = PER_LAYER * TILES * CHUNKS
    UNITS = PER_LAYER * TILES
    ps = g["PerToken"](sem, 0)
    consts_loaded, const_set = sem("consts_loaded"), sem("const_set")
    attn_loaded, mp_loaded, gu_loaded = sem("attn_loaded"), sem("mp_loaded"), sem("gu_loaded")
    wd_loaded = [sem(f"wd2_loaded{e}") for e in range(PER_LAYER)]
    cb_loaded = [sem(f"cb_loaded{i}") for i in range(2)]
    q_cols, q_products, q_bias, q_hi, q_lo = (sem(n) for n in ("q_cols", "q_products", "q_bias", "q_hi", "q_lo"))
    f_cols, f_products, f_bias, f_hi, f_lo = (sem(n) for n in ("f_cols", "f_products", "f_bias", "f_hi", "f_lo"))
    p_cols, fold_product, fold_copied = sem("p_cols"), sem("fold_product"), sem("fold_copied")
    egu_hi, egu_lo = sem("egu_hi"), sem("egu_lo")
    proj_added, mlp_added = sem("proj_added"), sem("mlp_added")
    gate_done, up_done, silu_done, h_ready, down_done = (
        sem(n) for n in ("gate_done2", "up_done2", "silu_done2", "h_ready2", "down_done2"))
    o_read, x_added = sem("o_read"), sem("x_added")
    out_ready, out_stored = sem("out_ready"), sem("out_stored")
    view_done, view_read, edge_done, turns_done, rounded, reduced, cos_done, diff_done = (
        sem(n) for n in ("view_done", "view_read", "edge_done", "turns_done", "rounded", "reduced", "cos_done", "diff_done"))
    ham, fold_step = sem("ham"), sem("fold_step")
    freq_done, gained, proj_done = sem("freq_done"), sem("gained"), sem("proj_done")
    fc_done, gelu_done, mp_done = sem("fc_done"), sem("gelu_done"), sem("mp_done")
    HAM, FOLD = 13, 3
    FREE_QK = 8

    pipeline = Pipeline()

    def tile(ap, t):
        return ap[:, t * TILE:(t + 1) * TILE]

    def own(ap):
        return ap[..., 1:TILE + 1]

    def one(l):
        return bass.ds(l, 1)

    def less(n, by):
        return max(n - by, 0) if isinstance(n, int) else n - by

    def hi_lo_used(engine, before):
        engine.wait_ge(view_done, 2 * before("views"))
        engine.wait_ge(fc_done, 2 * before("fc_a") + 2 * before("fc_b"))

    block = ctx.enter_context(nc.Block())

    @block.sync
    def _(sp):
        sp.dma_start(LC[:], A["cols1"]).then_inc(consts_loaded, 16)
        sp.dma_start(hartley[:], A["c_hartley"]).then_inc(consts_loaded, 16)
        sp.dma_start(GAIN[:], A["c_gain"]).then_inc(consts_loaded, 16)

        def body(w, layer):
            for name, l, k, before in pipeline.steps(w, layer):
                if name == "load_attn":
                    sp.wait_ge(q_lo, l)
                    sp.wait_ge(q_products, l)
                    sp.wait_ge(f_lo, l)
                    sp.wait_ge(f_products, l)
                    sp.wait_ge(fold_product, l)
                    for dst, src in ((QRAW, "w1_qkv"), (FRAW, "w1_fc"), (PRAW, "w1_proj")):
                        sp.dma_start(dst[:], A[src][one(l)].rearrange("a p n -> p (a n)")).then_inc(attn_loaded, 16)
                elif name == "load_up":
                    sp.wait_ge(egu_lo, PER_LAYER * l + k)
                    sp.dma_start(raw[:], A["w1_gu"][one(l * PER_LAYER + k)].rearrange("a p n -> p (a n)")).then_inc(gu_loaded, 16)
                elif name == "load_down":
                    if k:
                        sp.wait_ge(down_done, l * STEPS)
                    elif w or l:
                        sp.wait_ge(down_done, (l - 1) * STEPS + STEPS // 2)
                    sp.dma_start(WD[:, k, :, :], A["w1_d"][one(l * PER_LAYER + k)].rearrange("a p c n -> p (a c) n")
                                 ).then_inc(wd_loaded[k], 16)
                elif name == "load_mproj":
                    sp.wait_ge(mp_done, TILES * l)
                    sp.dma_start(MP[:], A["w1_mproj"][one(l)].rearrange("a p c n -> p (a c) n")).then_inc(mp_loaded, 16)
                elif name == "expert" and k % CHUNKS == 0:
                    u = k // CHUNKS
                    e, t = u // TILES, u % TILES
                    sp.wait_ge(o_read, less(UNITS * l + u, 1))
                    sp.dma_start(CB[:, u % 2, :],
                                 combine[one(l * PER_LAYER + e),
                                         t * TILE:(t + 1) * TILE].broadcast_to([P, TILE])).then_inc(cb_loaded[u % 2], 16)
                elif name == "out":
                    sp.wait_ge(out_ready, k + 1)
                    sp.dma_start(A["outT"][:, k * TILE:(k + 1) * TILE], tile(X, k)).then_inc(out_stored, 16)

        pipeline.run(sp, body)
        sp.wait_ge(out_stored, 16 * TILES)

    @block.scalar
    def _(act):
        act.wait_ge(const_set, 1)

        def body(w, layer):
            for name, l, k, before in pipeline.steps(w, layer):
                n = before(name)
                if name == "prep_views":
                    act.wait_ge(attn_loaded, 48 * l + 48)
                    act.wait_ge(q_cols, l + 1)
                    act.wait_ge(view_done, VIEWS * TILES * l)
                    act.activation(WQH[:], QRAW[:], ACT.Copy, scale=LQ[:, G1:G1 + 1]).then_inc(q_hi, 1)
                elif name == "prep_proj":
                    act.wait_ge(fold_product, l + 1)
                    act.wait_ge(proj_done, TILES * l)
                    act.activation(WP[:], banks[7][:, 0:P], ACT.Copy, scale=1.0 / P).then_inc(fold_copied, 1)
                elif name == "prep_fc":
                    act.wait_ge(attn_loaded, 48 * l + 48)
                    act.wait_ge(f_cols, l + 1)
                    act.wait_ge(fc_done, 4 * TILES * l)
                    act.activation(FCH[:], FRAW[:], ACT.Copy, scale=LF[:, G2:G2 + 1]).then_inc(f_hi, 1)
                elif name == "split_expert":
                    act.wait_ge(gu_loaded, (n + 1) * 16)
                    if k:
                        act.wait_ge(up_done, l * STEPS)
                    elif w or l:
                        act.wait_ge(up_done, (l - 1) * STEPS + STEPS // 2)
                    act.activation(GUH[:, k, :], raw[:], ACT.Copy).then_inc(egu_hi, 1)
                elif name == "expert":
                    act.wait_ge(gate_done, n + 1)
                    act.wait_ge(down_done, less(n, 3))
                    act.activation(SH[:, k % 4, :], banks[k % 2][:], ACT.Silu).then_inc(silu_done, 1)
                elif name == "centre":
                    act_centred(act, ps, 0, n)
                elif name == "sums":
                    act_var(act, ps, 0, n, g["eps_col"][:])
                elif name == "turn":
                    act_rows(act, ps, 0, n)
                elif name == "halves":
                    act.wait_ge(ps.scaled, n + 1)
                    hi_lo_used(act, before)
                    act.activation(HI[:], XS[:], ACT.Copy).then_inc(ps.hi_done, 1)
                elif name == "views":
                    t, j = k
                    views_of = l * TILES + t
                    if j == 0:
                        act.wait_ge(ham, before("ham"))
                        if t % HALVES:
                            act.wait_ge(view_read, 2 * n)
                            act.activation(QK[:, :, 0, 0:1], QK[:, :, 0, TILE:TILE + 1], ACT.Copy)
                            act.activation(V[:, t % 2, 0, 0:1], V[:, (t - 1) % 2, 0, TILE:TILE + 1], ACT.Copy).then_inc(edge_done, 1)
                            act.wait_ge(edge_done, views_of + 1)
                        act.wait_ge(q_bias, l + 1)
                    outs = [QK[:, 0, 0, :], QK[:, 1, 0, :], V[:, t % 2, 0, :],
                            QK[:, 0, 2, :], QK[:, 1, 2, :], V[:, t % 2, 2, :]]
                    for i in range(2):
                        act.wait_ge(view_done, 2 * n + i + 1)
                        act.activation(own(outs[2 * j + i]), banks[6 + i][:], ACT.Identity,
                                       bias=BIAS[:, 2 * j + i:2 * j + i + 1]).then_inc(view_read, 1)
                    if j == 2 and t % HALVES == 0:
                        act.wait_ge(view_read, 2 * n + 2)
                        act.activation(QK[:, :, 0, 0:1], QK[:, :, 0, 1:2], ACT.Copy)
                        act.activation(V[:, t % 2, 0, 0:1], V[:, t % 2, 0, 1:2], ACT.Copy).then_inc(edge_done, 1)
                elif name == "turns":
                    act.wait_ge(view_read, VIEWS * (n + 1))
                    act.activation(own(QK[:, :, 3, :]), own(QK[:, :, 0, :]), ACT.Identity, bias=quarter[:],
                                   scale=1.0 / (2 * np.pi))
                    act.activation(own(V[:, k % 2, 3, :]), own(V[:, k % 2, 0, :]), ACT.Identity, bias=quarter[:],
                                   scale=1.0 / (2 * np.pi)).then_inc(turns_done, 1)
                elif name == "round":
                    act.wait_ge(turns_done, n + 1)
                    act.wait_ge(cos_done, n)
                    act.activation(TURNS[:, 0:2, :], own(QK[:, :, 3, :]), ACT.Identity, bias=rounder[:])
                    act.activation(TURNS[:, 2, :], own(V[:, k % 2, 3, :]), ACT.Identity, bias=rounder[:]).then_inc(rounded, 1)
                    act.wait_ge(rounded, 2 * n + 1)
                    act.activation(TURNS[:], TURNS[:], ACT.Identity, bias=unrounder[:]).then_inc(rounded, 1)
                elif name == "cosines":
                    act.wait_ge(reduced, n + 1)
                    act.activation(own(QK[:, :, 3, :]), TURNS[:, 0:2, :], ACT.Sin, scale=-TURN)
                    act.activation(own(V[:, k % 2, 3, :]), TURNS[:, 2, :], ACT.Sin, scale=-TURN).then_inc(cos_done, 1)
                elif name == "fc_b":
                    act.wait_ge(mp_done, n)
                    act.wait_ge(f_bias, l + 1)
                    for c in range(4):
                        act.wait_ge(fc_done, 4 * n + c + 1)
                        act.activation(GE[:, c, :], banks[6 + c % 2][:], ACT.Gelu,
                                       bias=BIAS[:, VIEWS + c:VIEWS + c + 1]).then_inc(gelu_done, 1)

        pipeline.run(act, body)

    @block.gpsimd
    def _(pool):
        def added(n, u):
            pool.wait_ge(o_read, n + 1)
            pool.wait_ge(x_added, n)
            pool.tensor_tensor(tile(X, u % TILES), tile(X, u % TILES), CO[:], ALU.add).then_inc(x_added, 1)

        def body(w, layer):
            for name, l, k, before in pipeline.steps(w, layer):
                n = before(name)
                if name == "split_expert":
                    pool.wait_ge(egu_hi, n + 1)
                    pool.tensor_tensor(GUL[:, k, :], raw[:], GUH[:, k, :].bitcast(F32),
                                       ALU.subtract).then_inc(egu_lo, 1)
                elif name == "expert" and k % CHUNKS == 2 and (k > CHUNKS or w):
                    added(l * UNITS + k // CHUNKS - 1, k // CHUNKS - 1)
                elif name == "sums":
                    pool_power(pool, ps, 0, n, g["power_half"])
                elif name == "halves":
                    pool.wait_ge(ps.hi_done, n + 1)
                    hi_lo_used(pool, before)
                    pool.tensor_tensor(LO[:], XS[:], HI[:].bitcast(F32), ALU.subtract).then_inc(ps.lo_done, 1)
                elif name == "round":
                    pool.wait_ge(rounded, 2 * n + 2)
                    pool.tensor_tensor(TURNS[:, 0:2, :], TURNS[:, 0:2, :], own(QK[:, :, 3, :]), ALU.subtract)
                    pool.tensor_tensor(TURNS[:, 2, :], TURNS[:, 2, :], own(V[:, k % 2, 3, :]),
                                       ALU.subtract).then_inc(reduced, 1)
                elif name == "fold":
                    pool.wait_ge(ham, (n + 1) * HAM)
                    pool.tensor_tensor(TA[:, 0, :], TA[:, 0, :], TA[:, 1, :], ALU.subtract).then_inc(fold_step, 1)
                    pool.tensor_tensor(TA[:, 2, :], TA[:, 2, :], TA[:, 3, :], ALU.add).then_inc(fold_step, 1)
                    pool.wait_ge(fold_step, n * FOLD + 2)
                    pool.wait_ge(proj_done, n)
                    pool.tensor_tensor(XG[:], TA[:, 0, :], TA[:, 2, :], ALU.subtract).then_inc(fold_step, 1)
                elif name == "expert" and w == LAYERS - 1 and k == STEPS - 1:
                    added(LAYERS * UNITS - 1, UNITS - 1)

        pipeline.run(pool, body)

    @block.vector
    def _(dve):
        dve.memset(rounder[:], ROUND)
        dve.memset(unrounder[:], -ROUND)
        dve.memset(quarter[:], 0.25).then_inc(const_set, 1)
        dve.wait_ge(consts_loaded, 48)

        def unit(n, u):
            dve.wait_ge(down_done, (n + 1) * CHUNKS)
            dve.wait_ge(cb_loaded[u % 2], (n - u % 2) * 8 + 16)
            dve.wait_ge(x_added, n)
            dve.tensor_tensor(CO[:], banks[4][:], CB[:, u % 2, :], ALU.mult).then_inc(o_read, 1)

        def pair(ap, a, b):
            return ap[:, a:b + 1:b - a, :]

        def hamilton(n, t, i):
            q = own(QK[:, 0, :, :])

            def k_(j):
                return own(QK[:, 1, j, :]).unsqueeze(1).broadcast_to([P, 4, TILE])

            base = n * HAM
            ADD, SUB = ALU.add, ALU.subtract
            sums = {2: ((1, 2), (0, 3), ADD), 3: ((0, 3), (1, 2), SUB),
                    5: ((2, 3), (0, 1), ADD), 6: ((0, 1), (2, 3), SUB)}
            if i == 0:
                dve.wait_ge(cos_done, n + 1)
                dve.wait_ge(diff_done, 2 * (n + 1))
                dve.wait_ge(ham, base)
                ins = dve.tensor_tensor(AM[:], q, k_(0), ALU.mult)
            elif i in (1, 4, 7):
                if i == 1:
                    dve.wait_ge(fold_step, n * FOLD)
                else:
                    dve.wait_ge(ham, base + i)
                ins = dve.tensor_tensor(TA[:], q, k_(1 + i // 3), ALU.mult)
            elif i in sums:
                dve.wait_ge(ham, base + (2 if i < 4 else 5))
                d, s, op = sums[i]
                ins = dve.tensor_tensor(pair(AM, *d), pair(AM, *d), pair(TA, *s), op)
            elif i < 12:
                dve.wait_ge(ham, base + 8)
                d, s, op = ((3, 0, ADD), (2, 1, SUB), (1, 2, ADD), (0, 3, SUB))[i - 8]
                ins = dve.tensor_tensor(AM[:, d, :], AM[:, d, :], TA[:, s, :], op)
            else:
                dve.wait_ge(ham, base + 12)
                ins = dve.tensor_tensor(TA[:], AM[:], own(V[:, t % 2, :, :]), ALU.mult)
            ins.then_inc(ham, 1)

        def keep_columns(dve, out, l):
            columns = LC[:, one(l), :].rearrange("p a c -> p (a c)")
            return dve.tensor_tensor(out[:], columns, columns, ALU.max)

        def body(w, layer):
            for name, l, k, before in pipeline.steps(w, layer):
                n = before(name)
                if name == "prep_views":
                    dve.wait_ge(view_read, VIEWS * TILES * l)
                    dve.wait_ge(q_products, l)
                    keep_columns(dve, LQ, l).then_inc(q_cols, 1)
                    dve.wait_ge(q_cols, l + 1)
                    dve.wait_ge(q_products, l + 1)
                    dve.tensor_tensor(BIAS[:, 0:VIEWS], banks[6][:, 0:VIEWS], LQ[:, 0:VIEWS], ALU.add).then_inc(q_bias, 1)
                    dve.wait_ge(q_hi, l + 1)
                    dve.scalar_tensor_tensor(WQL[:], QRAW[:], LQ[:, G1:G1 + 1], WQH[:].bitcast(F32),
                                             ALU.mult, ALU.subtract).then_inc(q_lo, 1)
                elif name == "prep_proj":
                    dve.wait_ge(proj_added, TILES * l)
                    keep_columns(dve, LP, l).then_inc(p_cols, 1)
                elif name == "prep_fc":
                    dve.wait_ge(gelu_done, 4 * TILES * l)
                    dve.wait_ge(mlp_added, TILES * l)
                    dve.wait_ge(f_products, l)
                    keep_columns(dve, LF, l).then_inc(f_cols, 1)
                    dve.wait_ge(f_cols, l + 1)
                    dve.wait_ge(f_products, l + 1)
                    dve.tensor_tensor(BIAS[:, VIEWS:], banks[6][:, 0:4], LF[:, VIEWS:VIEWS + 4], ALU.add).then_inc(f_bias, 1)
                    dve.wait_ge(f_hi, l + 1)
                    dve.scalar_tensor_tensor(FCL[:], FRAW[:], LF[:, G2:G2 + 1], FCH[:].bitcast(F32),
                                             ALU.mult, ALU.subtract).then_inc(f_lo, 1)
                elif name == "expert":
                    dve.wait_ge(silu_done, n + 1)
                    dve.wait_ge(up_done, n + 1)
                    dve.tensor_tensor(SH[:, k % 4, :], SH[:, k % 4, :], banks[2 + k % 2][:],
                                      ALU.mult).then_inc(h_ready, 1)
                    if k % CHUNKS == 1 and (k > CHUNKS or w):
                        unit(l * UNITS + k // CHUNKS - 1, k // CHUNKS - 1)
                    if w == LAYERS - 1 and k == STEPS - 1:
                        unit(LAYERS * UNITS - 1, UNITS - 1)
                elif name == "spread":
                    dve.wait_ge(ps.spread, n + 1)
                    dve.wait_ge(ps.lo_done, n)
                    dve.tensor_tensor(XS[:], XC[:], LNB[:], ALU.mult).then_inc(ps.scaled, 1)
                elif name == "turns":
                    dve.wait_ge(edge_done, n + 1)
                    dve.wait_ge(view_read, (n + 1) * VIEWS)
                    for buf, side in ((QK, slice(0, 2)), (V, slice(k % 2, k % 2 + 1))):
                        zero = buf[:, side, 0, :]
                        dve.tensor_tensor(own(buf[:, side, 1, :]), own(zero), zero[..., 0:TILE],
                                          ALU.subtract).then_inc(diff_done, 1)
                elif name == "ham":
                    hamilton(l * TILES + k[0], *k)
                elif name == "gain":
                    dve.wait_ge(freq_done, n + 1)
                    s = (k % HALVES) * TILE
                    dve.tensor_tensor(XG[:], banks[6][:], GAIN[:, s:s + TILE], ALU.mult).then_inc(gained, 1)
                elif name == "proj_add":
                    dve.wait_ge(proj_done, n + 1)
                    dve.wait_ge(p_cols, l + 1)
                    dve.scalar_tensor_tensor(tile(Z, k), banks[7][:], LP[:, PB:PB + 1], tile(Z, k),
                                             ALU.add, ALU.add).then_inc(proj_added, 1)
                elif name == "mlp_add":
                    dve.wait_ge(mp_done, n + 1)
                    dve.wait_ge(f_cols, l + 1)
                    dve.scalar_tensor_tensor(tile(Z, k), banks[7][:], LF[:, MB:MB + 1], tile(Z, k),
                                             ALU.add, ALU.add).then_inc(mlp_added, 1)
                elif name == "out":
                    dve.wait_ge(x_added, UNITS * LAYERS - TILES + k + 1)
                    dve.wait_ge(mlp_added, TILES * (LAYERS - 1) + k + 1)
                    dve.tensor_tensor(tile(X, k), tile(X, k), tile(Z, k), ALU.add).then_inc(out_ready, 1)

        pipeline.run(dve, body)

    @block.tensor
    def _(pe):
        pe.wait_ge(consts_loaded, 48)

        def down(n, l, k):
            if k < 0:
                l, k = l - 1, k + STEPS
            u, c = k // CHUNKS, k % CHUNKS
            pe.wait_ge(h_ready, n + 1)
            if c == 0:
                pe.wait_ge(o_read, l * UNITS + u)
                if u % TILES == 0:
                    pe.wait_ge(wd_loaded[u // TILES], (l + 1) * 16)
            pe.matmul(banks[4][:], WD[:, u // TILES, c, :], SH[:, k % 4, :],
                      start=(c == 0), stop=(c == CHUNKS - 1)).then_inc(down_done, 1)

        def banks_free(before):
            pe.wait_ge(view_read, 2 * before("views"))
            pe.wait_ge(gained, before("gain"))
            pe.wait_ge(proj_added, before("proj_add"))
            pe.wait_ge(mlp_added, before("mlp_add"))
            pe.wait_ge(gelu_done, 4 * before("fc_b"))
            pe.wait_ge(q_bias, before("prep_views"))
            pe.wait_ge(f_bias, before("prep_fc"))
            pe.wait_ge(fold_copied, before("prep_proj"))

        def body(w, layer):
            for name, l, k, before in pipeline.steps(w, layer):
                n = before(name)
                if name == "prep_views":
                    pe.wait_ge(attn_loaded, 48 * l + 48)
                    pe.wait_ge(q_cols, l + 1)
                    banks_free(before)
                    for i in range(VIEWS):
                        mm = pe.matmul(banks[6][:, i:i + 1], QRAW[:, i * P:(i + 1) * P], LQ[:, B1:B1 + 1], start=True, stop=True)
                    mm.then_inc(q_products, 1)
                elif name == "prep_fc":
                    pe.wait_ge(attn_loaded, 48 * l + 48)
                    pe.wait_ge(f_cols, l + 1)
                    banks_free(before)
                    for i in range(4):
                        mm = pe.matmul(banks[6][:, i:i + 1], FRAW[:, i * P:(i + 1) * P],
                                       LF[:, B2:B2 + 1], start=True, stop=True)
                    mm.then_inc(f_products, 1)
                elif name == "prep_proj":
                    pe.wait_ge(attn_loaded, 48 * l + 48)
                    banks_free(before)
                    pe.matmul(banks[7][:, 0:P], hartley[:], PRAW[:], start=True, stop=True).then_inc(fold_product, 1)
                elif name == "expert":
                    u, c = k // CHUNKS, k % CHUNKS
                    e, t = u // TILES, u % TILES
                    if t == 0 and c == 0:
                        pe.wait_ge(egu_lo, PER_LAYER * l + e + 1)
                    a = c * P
                    pe.wait_ge(silu_done, less(n, 1))
                    split3(pe, banks[k % 2][:], GUH[:, e, a:a + P], GUL[:, e, a:a + P],
                           tile(XH, t), tile(XL, t)).then_inc(gate_done, 1)
                    pe.wait_ge(h_ready, less(n, 1))
                    a += FF
                    split3(pe, banks[2 + k % 2][:], GUH[:, e, a:a + P], GUL[:, e, a:a + P],
                           tile(XH, t), tile(XL, t)).then_inc(up_done, 1)
                    if k > 1 or w:
                        down(n - 2, l, k - 2)
                    if w == LAYERS - 1 and k == STEPS - 1:
                        down(n - 1, l, k - 1)
                        down(n, l, k)
                elif name == "centre":
                    t, kind = k
                    pe.wait_ge(ps.scaled, n)
                    if kind == "C":
                        pe.wait_ge(proj_added, TILES * l + t + 1)
                    elif w or l:
                        pe.wait_ge(mlp_added, TILES * (l - 1) + t + 1)
                    pe.matmul(LNB[:], centre[:], tile(Z, t), start=True, stop=True).then_inc(ps.source_done, 1)
                elif name == "sums":
                    pe_sums(pe, ps, 0, n, SQ, mean_col[:])
                elif name == "turn":
                    pe_turn(pe, ps, 0, n)
                elif name == "spread":
                    pe_spread(pe, ps, 0, n)
                elif name == "views":
                    t, j = k
                    pe.wait_ge(ps.lo_done, before("halves"))
                    pe.wait_ge(q_lo, l + 1)
                    banks_free(before)
                    for i in range(2):
                        a = (2 * j + i) * P
                        split3(pe, banks[6 + i][:], WQH[:, a:a + P], WQL[:, a:a + P], HI[:], LO[:]).then_inc(view_done, 1)
                elif name == "freq":
                    pe.wait_ge(fold_step, FOLD * (n + 1))
                    banks_free(before)
                    pe.matmul(banks[6][:], hartley[:], XG[:], start=True, stop=True).then_inc(freq_done, 1)
                elif name == "proj":
                    pe.wait_ge(gained, n + 1)
                    pe.wait_ge(fold_copied, l + 1)
                    banks_free(before)
                    pe.matmul(banks[7][:], WP[:], XG[:], start=True, stop=True).then_inc(proj_done, 1)
                elif name in ("fc_a", "fc_b"):
                    pe.wait_ge(ps.lo_done, before("halves"))
                    pe.wait_ge(f_lo, l + 1)
                    banks_free(before)
                    for i in range(2):
                        c = i
                        if name == "fc_b":
                            c = i + 2
                            pe.wait_ge(gelu_done, 4 * n + i + 1)
                        split3(pe, banks[6 + i][:], FCH[:, c * P:(c + 1) * P], FCL[:, c * P:(c + 1) * P],
                               HI[:], LO[:]).then_inc(fc_done, 1)
                elif name == "mproj":
                    pe.wait_ge(mp_loaded, (l + 1) * 16)
                    banks_free(before)
                    for c in range(4):
                        mm = pe.matmul(banks[7][:], MP[:, c, :], GE[:, c, :], start=(c == 0), stop=(c == 3))
                    mm.then_inc(mp_done, 1)

        pipeline.run(pe, body)


def _constants():
    pick = np.zeros((2 * GROUPS, GROUPS, P), np.float32)
    for i in range(GROUPS):
        pick[i, i] = pick[GROUPS + i, i] = 1.0

    def cas(n):
        a = 2 * np.pi * np.outer(np.arange(n), np.arange(n)) / n
        return np.cos(a) + np.sin(a)

    heads, dims = 16, 8
    ks = np.fft.fftfreq(SEQ)[None, None, :]
    kh = np.fft.fftfreq(heads)[:, None, None]
    kd = np.fft.fftfreq(dims)[None, :, None]
    km = np.sqrt(ks ** 2 + kh ** 2 + kd ** 2 + 1e-10)
    gain = np.cos(np.arctan(np.log(km + 1e-10))).reshape(P, SEQ)
    lam = np.arange(SEQ, dtype=np.float32) / np.float32(SEQ)
    t = np.arange(SEQ, dtype=np.float32) * np.float32(0.1)
    phase = t - np.float32(2.0) * lam + np.float32(0.5) * lam ** 2
    modulation = np.sin(t + lam) * np.cos(phase)
    return {
        "c_ident": np.eye(P, dtype=np.float32),
        "c_centre": (np.eye(P) - 1.0 / P).astype(np.float32),
        "c_pick": pick,
        "c_hartley": np.kron(cas(heads), cas(dims)).astype(np.float32),
        "c_gain": (gain * (1.0 + 0.1 * modulation)).astype(np.float32),
        "c_rank": np.arange(EXPERTS, 0, -1, dtype=np.float32)[None],
    }


def _layout(i):
    a = {k: np.asarray(v) for k, v in i.items()}
    heads, dims = 16, 8
    head_before = (np.arange(heads) - 1) % heads

    def views(x):
        x = x.reshape(*x.shape[:-1], heads, 3, dims)
        parts = [x[..., j, :] for j in range(3)]
        parts += [p[..., head_before, :] for p in parts]
        return [p.reshape(*p.shape[:-2], P) for p in parts]

    cols0 = np.zeros((P, 12), np.float32)
    cols0[:, 0] = a["L0_attn_bqkv"][:P]
    for c, m in enumerate(H0_ROWS):
        cols0[:m, 1 + c] = a["L0_attn_bg"][c * P:c * P + m]
        cols0[:m, 4 + c] = a["L0_attn_bu"][c * P:c * P + m]
    for c, n in ((7, "bd"), (8, "g1"), (9, "b1"), (10, "g2"), (11, "b2")):
        cols0[:, c] = a["L0_attn_" + n]
    cols1 = np.zeros((P, LAYERS, 16), np.float32)
    for c, v in enumerate(views(a["L1_attn_attn_b"])):
        cols1[:, :, c] = v.T
    cols1[:, :, 6:10] = a["L1_attn_fc_b"].reshape(LAYERS, 4, P).transpose(2, 0, 1)
    for c, n in ((10, "ln1_w"), (11, "ln1_b"), (12, "ln2_w"), (13, "ln2_b"), (14, "aproj_b"), (15, "mproj_b")):
        cols1[:, :, c] = a["L1_attn_" + n].T
    return {
        "xT": a["L0_attn_x"].reshape(TOK, P).T,
        "w0_attn": np.concatenate([a["L0_attn_Wqkv"], a["L0_attn_Wg"], a["L0_attn_Wu"]], 1),
        "w0_down": a["L0_attn_Wd"],
        "kv_bias": a["L0_attn_bqkv"][None, P:],
        "cols0": cols0,
        "w0_gu": np.concatenate([a["L0_ffn_Wg"], a["L0_ffn_Wu"]], 2),
        "w0_d": a["L0_ffn_Wd"].reshape(EXPERTS, CHUNKS, P, P).transpose(2, 0, 1, 3),
        "conf_w": a["L1_ffn_conf_w"].T,
        "conf_b": a["L1_ffn_conf_b"][None],
        "wealth": a["L1_ffn_wealth"][None],
        "w1_qkv": np.concatenate(views(a["L1_attn_attn_w"]), -1),
        "w1_fc": a["L1_attn_fc_w"],
        "w1_proj": a["L1_attn_aproj_w"],
        "w1_mproj": a["L1_attn_mproj_w"].reshape(LAYERS, 4, P, P).transpose(0, 2, 1, 3),
        "cols1": cols1,
        "w1_gu": np.concatenate([a["L1_ffn_gate_w"], a["L1_ffn_up_w"]], 1).transpose(0, 2, 1),
        "w1_d": a["L1_ffn_down_w"].transpose(0, 2, 1).reshape(EXPERTS, CHUNKS, P, P).transpose(0, 2, 1, 3),
    }


def kernel(**inputs):
    import concourse.bacc as _bacc
    from concourse.bass_utils import run_bass_kernel_spmd as _run

    nc = _bacc.Bacc("TRN2", target_bir_lowering=False, num_devices=1)
    arrays, A = {}, {}
    for name, a in {**_layout(inputs), **_constants()}.items():
        a = np.ascontiguousarray(a)
        arrays[f"in_{name}"] = a
        A[name] = nc.dram_tensor(f"in_{name}", a.shape, mybir.dt.from_np(a.dtype), kind="ExternalInput").ap()
    A["outT"] = nc.dram_tensor("outT", (P, TOK), F32, kind="ExternalOutput").ap()
    kernel_program(nc, A)
    got = _run(nc, [arrays], core_ids=[0]).results[0]["outT"]
    return np.ascontiguousarray(got.T).reshape(BATCHES, SEQ, P)
```

```python
from contextlib import ExitStack

import numpy as np

import concourse.bass as bass
from concourse import mybir

F32 = mybir.dt.float32
F32R = mybir.dt.float32r
ALU = mybir.AluOpType
ACT = mybir.ActivationFunctionType
AX = mybir.AxisListType

P = 128
TOK = 4096
TILE = 512
GROUPS = TILE // P
SEQ = 1024
BATCHES = TOK // SEQ
HALVES = SEQ // TILE
TILES = TOK // TILE
EXPERTS = 8
FF = 512
CHUNKS = FF // P
H0 = 341
H0_ROWS = [min(P, H0 - P * c) for c in range(3)]
LAYERS = 4
PER_LAYER = EXPERTS // LAYERS
EPS = 1e-5
ATTN_EPS = 1e-6
ROUND = 12582912.0
TURN = 6.283185


def kernel_program(nc, A):
    with ExitStack() as whole:
        def sem_of(ctx):
            return lambda name: ctx.enter_context(nc.semaphore(name))

        def sb_of(ctx):
            return lambda name, shape, dt=F32: ctx.enter_context(nc.sbuf_tensor(name, shape, dt))

        sb = sb_of(whole)
        X = sb("X", [P, TOK])
        ident = sb("ident", [P, P])
        centre = sb("centre", [P, P])
        mean_col = sb("mean_col", [P, 1])
        pick = sb("pick", [2 * GROUPS, GROUPS, P], F32R)
        power_half = sb("power_half", [P, GROUPS])
        power_one = sb("power_one", [P, GROUPS])
        ones = sb("ones", [P, GROUPS])
        eps_col = sb("eps_col", [P, 1])
        attn_eps_col = sb("attn_eps_col", [P, 1])
        banks = [whole.enter_context(nc.psum_tensor(f"bank{i}", [P, TILE], F32)) for i in range(8)]

        XC = sb("XC", [P, TILE])
        SQ = sb("SQ", [P, TILE])
        XS = sb("XS", [P, TILE])
        HI = sb("HI", [P, TILE], F32R)
        LO = sb("LO", [P, TILE], F32R)
        VAR = sb("VAR", [P, GROUPS])
        RSTD = sb("RSTD", [P, GROUPS])
        RHL = sb("RHL", [P, 2 * GROUPS])
        RT = sb("RT", [2 * GROUPS, P], F32R)
        SH = sb("SH", [P, 4, TILE])

        LNB = banks[5]
        x_first_loaded = sem_of(whole)("x_first_loaded")
        Z = sb("Z", [P, TOK])
        LG = sb("LG", [P, TOK // P, EXPERTS])
        later_loaded = sem_of(whole)("later_loaded")
        LATER = 5
        rows = sb("rows", [P, 3, EXPERTS])
        LC = sb("LC", [P, LAYERS, 16])
        hartley = sb("hartley", [P, P])

        def split3(pe, out, w_hi, w_lo, x_hi, x_lo):
            pe.matmul(out, w_hi, x_hi, start=True, stop=False)
            pe.matmul(out, w_lo, x_hi, start=False, stop=False)
            return pe.matmul(out, w_hi, x_lo, start=False, stop=True)

        class PerToken:

            def __init__(self, sem, per_pass):
                self.per = per_pass
                self.source_done = sem("source_done")
                self.copied = sem("copied")
                self.sums_done = sem("sums_done")
                self.var_copied = sem("var_copied")
                self.power_step = sem("power_step")
                self.turned = sem("turned")
                self.rows_copied = sem("rows_copied")
                self.spread = sem("spread")
                self.scaled = sem("scaled")
                self.hi_done = sem("hi_done")
                self.lo_done = sem("lo_done")

            def at(self, it, n, each=1):
                return it * (self.per * each) + n * each

        def pe_sums(pe, ps, it, n, lhs, col):
            pe.wait_ge(ps.copied, ps.at(it, n + 1))
            for g in range(GROUPS):
                mm = pe.matmul(LNB[:, g:g + 1], lhs[:, g * P:(g + 1) * P], col, start=True, stop=True)
            mm.then_inc(ps.sums_done, 1)

        def act_var(act, ps, it, n, eps_col):
            act.wait_ge(ps.sums_done, ps.at(it, n + 1))
            act.wait_ge(ps.power_step, ps.at(it, n, 3))
            act.activation(VAR[:], LNB[:, 0:GROUPS], ACT.Identity, bias=eps_col).then_inc(ps.var_copied, 1)

        def pool_power(pool, ps, it, n, power):
            pool.wait_ge(ps.var_copied, ps.at(it, n + 1))
            pool.wait_ge(ps.turned, ps.at(it, n))
            pool.wait_ge(ps.power_step, ps.at(it, n, 3))
            pool.tensor_tensor(RSTD[:], VAR[:], power[:], ALU.pow).then_inc(ps.power_step, 1)
            pool.wait_ge(ps.power_step, ps.at(it, n, 3) + 1)
            pool.tensor_tensor(RHL[:, 0:GROUPS].bitcast(F32R), RSTD[:], ones[:], ALU.mult).then_inc(ps.power_step, 1)
            pool.wait_ge(ps.power_step, ps.at(it, n, 3) + 2)
            pool.tensor_tensor(RHL[:, GROUPS:].bitcast(F32R), RSTD[:], RHL[:, 0:GROUPS],
                               ALU.subtract).then_inc(ps.power_step, 1)

        def pe_turn(pe, ps, it, n):
            pe.wait_ge(ps.power_step, ps.at(it, n + 1, 3))
            pe.transpose(LNB[0:2 * GROUPS, P:2 * P], RHL[:], ident[:]).then_inc(ps.turned, 1)

        def act_rows(act, ps, it, n):
            act.wait_ge(ps.turned, ps.at(it, n + 1))
            act.wait_ge(ps.spread, ps.at(it, n))
            act.activation(RT[:], LNB[0:2 * GROUPS, P:2 * P], ACT.Copy).then_inc(ps.rows_copied, 1)

        def pe_spread(pe, ps, it, n):
            pe.wait_ge(ps.rows_copied, ps.at(it, n + 1))
            for g in range(GROUPS):
                mm = pe.matmul(LNB[:, g * P:(g + 1) * P], pick[:, g, :], RT[:], start=True, stop=True)
            mm.then_inc(ps.spread, 1)

        def act_centred(act, ps, it, n):
            act.wait_ge(ps.source_done, ps.at(it, n + 1))
            act.wait_ge(ps.scaled, ps.at(it, n))
            act.activation(XC[:], LNB[:], ACT.Copy)
            act.wait_ge(ps.sums_done, ps.at(it, n))
            act.activation(SQ[:], LNB[:], ACT.Square).then_inc(ps.copied, 1)

        def setup(sem, pick_raw, block):
            loaded, made = sem("const_loaded"), sem("const_made")

            @block.sync
            def _(sp):
                for dst, src in ((ident, A["c_ident"]), (centre, A["c_centre"]), (pick_raw, A["c_pick"])):
                    sp.dma_start(dst[:], src).then_inc(loaded, 16)
                sp.dma_start(X[:, 0:SEQ], A["xT"][:, 0:SEQ]).then_inc(x_first_loaded, 16)
                sp.wait_ge(loaded, 48)

            @block.vector
            def _(dve):
                dve.memset(mean_col[:], 1.0 / P)
                dve.memset(ones[:], 1.0)
                dve.memset(eps_col[:], EPS)
                dve.memset(attn_eps_col[:], ATTN_EPS)
                dve.memset(power_half[:], -0.5)
                dve.memset(power_one[:], -1.0).then_inc(made, 1)
                dve.wait_ge(loaded, 48)
                dve.tensor_copy(pick[:], pick_raw[:]).then_inc(made, 1)
                dve.wait_ge(made, 2)

        with ExitStack() as ctx:
            setup(sem_of(ctx), sb_of(ctx)("pick_raw", [2 * GROUPS, GROUPS, P]), ctx.enter_context(nc.Block()))

        with ExitStack() as ctx:
            sem, sb = sem_of(ctx), sb_of(ctx)
            first_layer(nc, A, sem, sb, ctx, locals())

        XH = whole.enter_context(nc.sbuf_tensor("XH", [P, TOK], F32R))
        XL = whole.enter_context(nc.sbuf_tensor("XL", [P, TOK], F32R))
        combine = nc.dram_tensor("combine", (EXPERTS, TOK), F32, kind="Internal").ap()
        with ExitStack() as ctx:
            sem, sb = sem_of(ctx), sb_of(ctx)
            routing(nc, A, sem, sb, ctx, locals())
        with ExitStack() as ctx:
            sem, sb = sem_of(ctx), sb_of(ctx)
            second_layer(nc, A, sem, sb, ctx, locals())


class Pipeline:

    def __init__(self, steps, layers, span, cut):
        steps = sorted(steps, key=lambda x: x[0])
        names = {x[1] for x in steps}
        self.layers = layers
        self.per_layer = {n: sum(1 for x in steps if x[1] == n and x[2] == 1) for n in names}
        self.windows = [[] for _ in range(layers)]
        seen = dict.fromkeys(names, 0)
        for place, name, l, k in steps:
            w = min(max(int((place - cut) // span), 0), layers - 1)
            assert name != "centre" or seen["centre"] == seen["spread"]
            self.windows[w].append((name, l - w, k, dict(seen)))
            seen[name] += 1
        inner = [[x[:3] for x in w] for w in self.windows[1:-1]]
        assert all(x == inner[0] for x in inner)

    def steps(self, w, layer):
        for name, off, k, seen in self.windows[w]:
            def before(other, seen=seen):
                return seen[other] if isinstance(layer, int) else (layer - w) * self.per_layer[other] + seen[other]
            yield name, layer + off, k, before

    def run(self, engine, body):
        body(0, 0)
        with engine.Fori(1, self.layers - 1) as l:
            body(1, l)
        body(self.layers - 1, self.layers - 1)


def less(n, by):
    return max(n - by, 0) if isinstance(n, int) else n - by


def first_layer_steps():
    span, out = HALVES * EXPERTS * CHUNKS, []
    for b in range(BATCHES):
        def put(place, name, k=0):
            out.append((b * span + place, name, b, k))

        for s in range(span):
            put(s, "expert", s)
        if b == 0:
            put(-0.5, "split_attn")
            for e in range(EXPERTS):
                put(max(4 * e - 6, e - 12), "split", e)

        def scaling(place, kind, h):
            for gap, name in ((0, "centre"), (1.1, "sums"), (2.7, "turn"), (3.7, "spread")):
                put(place + gap, name, (h, kind))
            put(place + 4.3, "end_" + kind, h)

        scaling(-14, "norm0", 0)
        scaling(4, "norm0", 1)
        put(2.5, "keys", 0)
        put(9.4, "keys", 1)
        put(13.5, "kv_sum")
        for h, (query, attn, norm1, ffn, norm2, finish, norm3) in enumerate((
                (15, 18, 23.2, 31.4, 37, 42, 46.1), (28.3, 31.3, 41.5, 48.2, 55.6, span + 3, span + 9.2))):
            put(query, "query", h)
            scaling(attn, "attn", h)
            scaling(norm1, "norm1", h)
            for c in range(3):
                put(ffn + 1.1 * c, "ffn2", (h, c))
            put(ffn + 4, "ffn2_down", h)
            put(ffn + 4.8, "ffn2_add", h)
            scaling(norm2, "norm2", h)
            put(finish, "finish", h)
            scaling(norm3, "norm3", h)
            put(norm3 + 5.4, "logits", h)
    return out


def first_layer(nc, A, sem, sb, ctx, g):
    X, Z, LG, ident, centre, mean_col, pick = (g[k] for k in ("X", "Z", "LG", "ident", "centre", "mean_col", "pick"))
    banks, LNB, XC, SQ, XS, HI, LO, SH = (g[k] for k in ("banks", "LNB", "XC", "SQ", "XS", "HI", "LO", "SH"))
    split3, PerToken = g["split3"], g["PerToken"]
    pe_sums, act_var, pool_power, pe_turn, act_rows, pe_spread, act_centred = (
        g[k] for k in ("pe_sums", "act_var", "pool_power", "pe_turn", "act_rows", "pe_spread", "act_centred"))
    power_half, power_one, eps_col, attn_eps_col = (
        g[k] for k in ("power_half", "power_one", "eps_col", "attn_eps_col"))

    GUH = sb("GUH", [P, EXPERTS, 2 * FF], F32R)
    GUL = sb("GUL", [P, EXPERTS, 2 * FF], F32R)
    WDH = sb("WDH", [P, EXPERTS, CHUNKS * P], F32R)
    WDL = sb("WDL", [P, EXPERTS, CHUNKS * P], F32R)
    raw = sb("raw0", [P, 2, 3 * FF])
    AW = 3 * P + 2 * H0
    attn_raw = sb("attn_raw", [P, AW])
    AH = sb("AH", [P, AW], F32R)
    AL = sb("AL", [P, AW], F32R)
    WDA = sb("WDA", [P, 3, P])
    kv_bias = sb("kv_bias", [P, 2 * P])
    conf = sb("conf", [P, EXPERTS])
    cols = sb("cols0", [P, 16])
    BQ, BG, BU, BD, G1, B1, G2, B2 = 0, 1, 4, 7, 8, 9, 10, 11
    NH = sb("NH", [P, HALVES, TILE], F32R)
    NL = sb("NL", [P, HALVES, TILE], F32R)
    KV = sb("KV", [P, HALVES * GROUPS, 2 * P + 2])
    KVS = sb("KVS", [P, P + 2])
    QP = sb("QP", [P, TILE])
    QE = sb("QE", [P, TILE])
    KE = QE[:].rearrange("p (g d) -> p g d", g=GROUPS)
    YA = attn_raw[:, 0:TILE]
    YF = attn_raw[:, TILE:2 * TILE]
    rest = raw[:].rearrange("p a n -> p (a n)")
    H2 = rest[:, 0:3 * TILE].rearrange("p (c n) -> p c n", c=3)
    X1 = rest[:, 3 * TILE:4 * TILE]
    GX = rest[:, 4 * TILE:6 * TILE].rearrange("p (h n) -> p h n", h=HALVES)
    HH = sb("HH", [P, 2, TILE], F32R)
    HL = sb("HL", [P, 2, TILE], F32R)

    STEPS = HALVES * EXPERTS * CHUNKS
    HALF = EXPERTS * CHUNKS
    SMALL = 6
    ps = PerToken(sem, 0)
    small_loaded, x_rest_loaded = sem("small_loaded"), sem("x_rest_loaded")
    raw_loaded = [sem(f"raw_loaded{i}") for i in range(2)]
    hi_split, lo_split, attn_hi, attn_lo = sem("hi_split"), sem("lo_split"), sem("attn_hi"), sem("attn_lo")
    ones_set = sem("ones_set")
    gate_done, up_done, silu_done, h_ready, hh_done, hl_done, down_done = (
        sem(n) for n in ("gate_done", "up_done", "silu_done", "h_ready", "hh_done", "hl_done", "down_done"))
    o_added = sem("o_added")
    nh_done, nl_done, hi_done, lo_done = (sem(n) for n in ("nh_done", "nl_done", "hi1_done", "lo1_done"))
    kv_done, kv_biased, k_min, k_exp, k_ready = (sem(n) for n in ("kv_done", "kv_biased", "k_min", "k_exp", "k_ready"))
    kvs_done, kvs_copied = sem("kvs_done"), sem("kvs_copied")
    q_done, q_copied, q_min, q_exp, q_ready = (sem(n) for n in ("q_done", "q_copied", "q_min", "q_exp", "q_ready"))
    ya_step, ya_ready, yf_ready, x1_ready = sem("ya_step"), sem("ya_ready"), sem("yf_ready"), sem("x1_ready")
    gu2_done, silu2_done, h2_ready, down2_done = (sem(n) for n in ("gu2_done", "silu2_done", "h2_ready", "down2_done"))
    x_ready, gx_ready = sem("x_ready"), sem("gx_ready")
    z_copied, logits_done, logits_copied = sem("z_copied"), sem("logits_done"), sem("logits_copied")

    pipeline = Pipeline(first_layer_steps(), BATCHES, STEPS, cut=-0.5)

    def x_tile(ap, b, h):
        return ap[:, bass.ds(b * SEQ + h * TILE, TILE)]

    def attn_cols(part, lo):
        w = AL if lo else AH
        return w[:, part * P:(part + 1) * P]

    def ffn2_cols(up, c, lo):
        w = AL if lo else AH
        a = 3 * P + up * H0 + c * P
        return w[:, a:a + H0_ROWS[c]]

    block = ctx.enter_context(nc.Block())

    @block.sync
    def _(sp):
        def expert(e):
            if e >= 2:
                sp.wait_ge(lo_split, e - 1)
            sp.dma_start(raw[:, e % 2, :], A["w0_gud"][e]).then_inc(raw_loaded[e % 2], 16)

        expert(0)
        expert(1)
        loads = [(attn_raw[:], A["w0_attn"]), (kv_bias[:], A["kv_bias"].broadcast_to([P, 2 * P])),
                 (cols[:, 0:12], A["cols0"]), (WDA[:, 0:2, :], A["w0_down"][0:2 * P, :].rearrange("(c p) n -> p c n", p=P)),
                 (WDA[0:H0_ROWS[2], 2, :], A["w0_down"][2 * P:H0, :]), (conf[:], A["conf_w"])]
        assert len(loads) == SMALL
        for dst, src in loads:
            sp.dma_start(dst, src).then_inc(small_loaded, 16)
        for e in range(2, EXPERTS):
            expert(e)
        sp.dma_start(X[:, SEQ:], A["xT"][:, SEQ:]).then_inc(x_rest_loaded, 16)
        for dst, src in ((g["LC"], "cols1"), (g["hartley"], "c_hartley")):
            sp.dma_start(dst[:], A[src]).then_inc(g["later_loaded"], 16)
        for i, name in enumerate(("conf_b", "wealth", "c_rank")):
            sp.dma_start(g["rows"][:, i, :], A[name].broadcast_to([P, EXPERTS])).then_inc(g["later_loaded"], 16)

    @block.scalar
    def _(act):
        def product_hi(n, k):
            act.wait_ge(h_ready, n + 1)
            act.wait_ge(down_done, less(n, 1))
            act.activation(HH[:, k % 2, :], SH[:, k % 4, :], ACT.Copy).then_inc(hh_done, 1)

        def body(w, layer):
            for name, b, k, before in pipeline.steps(w, layer):
                n = before(name)
                if name == "split":
                    act.wait_ge(raw_loaded[k % 2], 16 * (k // 2 + 1))
                    act.activation(GUH[:, k, :], raw[:, k % 2, 0:2 * FF], ACT.Copy)
                    act.activation(WDH[:, k, :], raw[:, k % 2, 2 * FF:], ACT.Copy).then_inc(hi_split, 1)
                elif name == "split_attn":
                    act.wait_ge(small_loaded, 16 * SMALL)
                    act.activation(AH[:], attn_raw[:], ACT.Copy).then_inc(attn_hi, 1)
                elif name == "expert":
                    if k or w:
                        product_hi(n - 1, k - 1)
                    act.wait_ge(gate_done, n + 1)
                    act.wait_ge(hl_done, less(n, 3))
                    act.activation(SH[:, k % 4, :], banks[k % 2][:], ACT.Silu).then_inc(silu_done, 1)
                    if w == BATCHES - 1 and k == STEPS - 1:
                        product_hi(n, k)
                elif name == "centre":
                    if k[1] == "attn":
                        act.wait_ge(ps.source_done, n + 1)
                        act.wait_ge(ps.scaled, n)
                        act.activation(XC[:], LNB[:], ACT.Copy).then_inc(ps.copied, 1)
                    else:
                        act_centred(act, ps, 0, n)
                elif name == "sums":
                    act_var(act, ps, 0, n, attn_eps_col[:] if k[1] == "attn" else eps_col[:])
                elif name == "turn":
                    act_rows(act, ps, 0, n)
                elif name == "end_norm0":
                    act.wait_ge(ps.scaled, before("spread"))
                    act.wait_ge(ya_ready, before("end_attn"))
                    act.wait_ge(kv_done, 2 * before("keys"))
                    act.wait_ge(q_done, before("query"))
                    if k:
                        act.wait_ge(up_done, b * STEPS)
                    elif w or b:
                        act.wait_ge(up_done, b * STEPS - HALF)
                    act.activation(NH[:, k, :], XS[:], ACT.Copy).then_inc(nh_done, 1)
                elif name == "keys":
                    act.wait_ge(kv_biased, 2 * n + 2)
                    act.wait_ge(k_ready, n)
                    act.wait_ge(q_ready, before("query"))
                    act.activation(KE, KV[:, k * GROUPS:(k + 1) * GROUPS, 0:P], ACT.Relu, scale=-1.0).then_inc(k_min, 1)
                    act.wait_ge(k_min, n + 1)
                    act.activation(KE, KE, ACT.Exp, scale=-1.0).then_inc(k_exp, 1)
                elif name == "kv_sum":
                    act.wait_ge(kvs_done, n + 1)
                    act.wait_ge(ps.sums_done, before("sums"))
                    act.activation(KVS[:], banks[6][:, 0:P + 2], ACT.Copy).then_inc(kvs_copied, 1)
                elif name == "query":
                    act.wait_ge(q_done, n + 1)
                    act.wait_ge(ps.sums_done, before("sums"))
                    act.wait_ge(k_ready, before("keys"))
                    act.wait_ge(q_ready, n)
                    act.activation(QP[:], banks[7][:], ACT.Identity, bias=cols[:, BQ:BQ + 1]).then_inc(q_copied, 1)
                    act.wait_ge(q_copied, n + 1)
                    act.activation(QE[:], QP[:], ACT.Relu, scale=-1.0).then_inc(q_min, 1)
                    act.wait_ge(q_min, n + 1)
                    act.activation(QE[:], QE[:], ACT.Exp, scale=-1.0).then_inc(q_exp, 1)
                elif name == "end_norm1":
                    act.wait_ge(ps.scaled, before("spread"))
                    act.wait_ge(yf_ready, n)
                    act.wait_ge(lo_split, EXPERTS)
                    act.activation(X1, XS[:], ACT.Identity, bias=cols[:, B1:B1 + 1],
                                   scale=cols[:, G1:G1 + 1]).then_inc(x1_ready, 1)
                    act.wait_ge(x1_ready, n + 1)
                    act.wait_ge(gu2_done, 3 * n)
                    act.activation(HI[:], X1, ACT.Copy).then_inc(hi_done, 1)
                elif name == "ffn2":
                    c = k[1]
                    m = H0_ROWS[c]
                    act.wait_ge(gu2_done, n + 1)
                    act.wait_ge(down2_done, before("ffn2_down"))
                    act.wait_ge(lo_split, EXPERTS)
                    act.activation(H2[0:m, c, :], banks[6][0:m, :], ACT.Silu,
                                   bias=cols[0:m, BG + c:BG + c + 1]).then_inc(silu2_done, 1)
                elif name == "end_norm3":
                    act.wait_ge(ps.scaled, before("spread"))
                    act.activation(x_tile(Z, b, k), XS[:], ACT.Copy).then_inc(z_copied, 1)
                elif name == "logits":
                    act.wait_ge(logits_done, n + 1)
                    act.activation(LG[:, bass.ds(b * HALVES * GROUPS + k * GROUPS, GROUPS), :],
                                   banks[6][:, 0:GROUPS * EXPERTS].rearrange("p (g e) -> p g e", e=EXPERTS),
                                   ACT.Copy).then_inc(logits_copied, 1)

        pipeline.run(act, body)

    @block.gpsimd
    def _(pool):
        pool.memset(KV[:, :, 2 * P:], 1.0).then_inc(ones_set, 1)

        def body(w, layer):
            for name, b, k, before in pipeline.steps(w, layer):
                n = before(name)
                if name == "sums":
                    pool_power(pool, ps, 0, n, power_one if k[1] == "attn" else power_half)
                elif name == "end_norm0":
                    pool.wait_ge(nh_done, n + 1)
                    pool.tensor_tensor(NL[:, k, :], XS[:], NH[:, k, :].bitcast(F32),
                                       ALU.subtract).then_inc(nl_done, 1)
                elif name == "end_norm1":
                    pool.wait_ge(hi_done, n + 1)
                    pool.wait_ge(gu2_done, 3 * n)
                    pool.tensor_tensor(LO[:], X1, HI[:].bitcast(F32), ALU.subtract).then_inc(lo_done, 1)

        pipeline.run(pool, body)

    @block.vector
    def _(dve):
        def product_lo(n, k):
            dve.wait_ge(hh_done, n + 1)
            dve.wait_ge(down_done, less(n, 1))
            dve.tensor_tensor(HL[:, k % 2, :], SH[:, k % 4, :], HH[:, k % 2, :].bitcast(F32),
                              ALU.subtract).then_inc(hl_done, 1)

        def add_experts(n, b, h):
            dve.wait_ge(down_done, (n + 1) * HALF)
            dve.scalar_tensor_tensor(x_tile(X, b, h), banks[4][:], cols[:, B2:B2 + 1], x_tile(X, b, h),
                                     ALU.add, ALU.add).then_inc(o_added, 1)

        def body(w, layer):
            for name, b, k, before in pipeline.steps(w, layer):
                n = before(name)
                if name == "split":
                    dve.wait_ge(hi_split, k + 1)
                    dve.tensor_tensor(GUL[:, k, :], raw[:, k % 2, 0:2 * FF], GUH[:, k, :].bitcast(F32), ALU.subtract)
                    dve.tensor_tensor(WDL[:, k, :], raw[:, k % 2, 2 * FF:], WDH[:, k, :].bitcast(F32),
                                      ALU.subtract).then_inc(lo_split, 1)
                elif name == "split_attn":
                    dve.wait_ge(attn_hi, 1)
                    dve.tensor_tensor(AL[:], attn_raw[:], AH[:].bitcast(F32), ALU.subtract).then_inc(attn_lo, 1)
                elif name == "expert":
                    if k or w:
                        product_lo(n - 1, k - 1)
                    dve.wait_ge(silu_done, n + 1)
                    dve.wait_ge(up_done, n + 1)
                    dve.tensor_tensor(SH[:, k % 4, :], SH[:, k % 4, :], banks[2 + k % 2][:],
                                      ALU.mult).then_inc(h_ready, 1)
                    if w == BATCHES - 1 and k == STEPS - 1:
                        product_lo(n, k)
                    if k == HALF + 1:
                        add_experts(b * HALVES, b, 0)
                    elif k == 1 and w:
                        add_experts(b * HALVES - 1, b - 1, 1)
                    elif k == STEPS - 1 and w == BATCHES - 1:
                        add_experts(b * HALVES + 1, b, 1)
                elif name == "finish":
                    tiles = b * HALVES + k + 1
                    dve.wait_ge(o_added, tiles)
                    dve.wait_ge(gx_ready, tiles)
                    dve.tensor_tensor(x_tile(X, b, k), x_tile(X, b, k), GX[:, k, :], ALU.add).then_inc(x_ready, 1)
                elif name == "spread":
                    dve.wait_ge(ps.spread, n + 1)
                    dve.wait_ge(nl_done, before("end_norm0"))
                    dve.wait_ge(x1_ready, before("end_norm1"))
                    dve.wait_ge(ya_ready, before("end_attn"))
                    dve.wait_ge(gx_ready, before("end_norm2"))
                    dve.wait_ge(z_copied, before("end_norm3"))
                    dve.wait_ge(logits_done, before("logits"))
                    dve.tensor_tensor(XS[:], XC[:], LNB[:], ALU.mult).then_inc(ps.scaled, 1)
                elif name == "keys":
                    for half in range(2):
                        dve.wait_ge(kv_done, 2 * n + half + 1)
                        dve.wait_ge(kvs_done, before("kv_sum"))
                        i = k * GROUPS + 2 * half
                        dve.tensor_tensor(KV[:, i:i + 2, 0:2 * P],
                                          banks[6 + half][:].rearrange("p (a n) -> p a n", a=2),
                                          kv_bias[:].unsqueeze(1).broadcast_to([P, 2, 2 * P]),
                                          ALU.add).then_inc(kv_biased, 1)
                    dve.wait_ge(k_exp, n + 1)
                    kk = KV[:, k * GROUPS:(k + 1) * GROUPS, 0:P]
                    dve.scalar_tensor_tensor(kk, kk, 0.0, KE, ALU.max, ALU.add).then_inc(k_ready, 1)
                elif name == "query":
                    dve.wait_ge(q_exp, n + 1)
                    dve.scalar_tensor_tensor(QP[:], QP[:], 0.0, QE[:], ALU.max, ALU.add).then_inc(q_ready, 1)
                elif name == "end_attn":
                    dve.wait_ge(attn_lo, 1)
                    dve.wait_ge(ps.scaled, before("spread"))
                    dve.wait_ge(ps.source_done, before("centre"))
                    dve.wait_ge(nl_done, before("end_norm0"))
                    dve.tensor_tensor(YA, NH[:, k, :].bitcast(F32), NL[:, k, :].bitcast(F32), ALU.add).then_inc(ya_step, 1)
                    dve.wait_ge(ya_step, n + 1)
                    dve.tensor_tensor(YA, YA, XS[:], ALU.add).then_inc(ya_ready, 1)
                elif name == "ffn2":
                    c = k[1]
                    m = H0_ROWS[c]
                    dve.wait_ge(silu2_done, n + 1)
                    dve.scalar_tensor_tensor(H2[0:m, c, :], banks[7][0:m, :], cols[0:m, BU + c:BU + c + 1],
                                             H2[0:m, c, :], ALU.add, ALU.mult).then_inc(h2_ready, 1)
                elif name == "ffn2_add":
                    dve.wait_ge(down2_done, n + 1)
                    dve.wait_ge(ps.source_done, before("centre"))
                    dve.scalar_tensor_tensor(YF, banks[6][:], cols[:, BD:BD + 1], X1,
                                             ALU.add, ALU.add).then_inc(yf_ready, 1)
                elif name == "end_norm2":
                    dve.wait_ge(ps.scaled, before("spread"))
                    dve.wait_ge(x_ready, before("finish"))
                    dve.wait_ge(lo_split, EXPERTS)
                    dve.tensor_scalar(GX[:, k, :], XS[:], cols[:, G2:G2 + 1], None, ALU.mult).then_inc(gx_ready, 1)

        pipeline.run(dve, body)

    @block.tensor
    def _(pe):
        pe.wait_ge(ones_set, 1)

        def down(n, b, k):
            if k < 0:
                b, k = b - 1, k + STEPS
            e, c = k // CHUNKS % EXPERTS, k % CHUNKS
            first, last = k % HALF == 0, k % HALF == HALF - 1
            pe.wait_ge(hl_done, n + 1)
            if first:
                pe.wait_ge(o_added, b * HALVES + k // HALF)
            w_hi, w_lo = (w[:, e, c * P:(c + 1) * P] for w in (WDH, WDL))
            pe.matmul(banks[4][:], w_hi, HH[:, k % 2, :], start=first, stop=False)
            pe.matmul(banks[4][:], w_lo, HH[:, k % 2, :], start=False, stop=False)
            pe.matmul(banks[4][:], w_hi, HL[:, k % 2, :], start=False, stop=last).then_inc(down_done, 1)

        def banks_free(before):
            pe.wait_ge(kv_biased, 2 * before("keys"))
            pe.wait_ge(kvs_copied, before("kv_sum"))
            pe.wait_ge(q_copied, before("query"))
            pe.wait_ge(h2_ready, before("ffn2"))
            pe.wait_ge(yf_ready, before("ffn2_add"))
            pe.wait_ge(logits_copied, before("logits"))

        def body(w, layer):
            for name, b, k, before in pipeline.steps(w, layer):
                n = before(name)
                if name == "expert":
                    e, c, h = k // CHUNKS % EXPERTS, k % CHUNKS, k // HALF
                    if k % HALF == 0:
                        pe.wait_ge(nl_done, b * HALVES + h + 1)
                    if c == 0:
                        pe.wait_ge(lo_split, e + 1)
                    a = c * P
                    pe.wait_ge(silu_done, less(n, 1))
                    split3(pe, banks[k % 2][:], GUH[:, e, a:a + P], GUL[:, e, a:a + P],
                           NH[:, h, :], NL[:, h, :]).then_inc(gate_done, 1)
                    pe.wait_ge(h_ready, less(n, 1))
                    a += FF
                    split3(pe, banks[2 + k % 2][:], GUH[:, e, a:a + P], GUL[:, e, a:a + P],
                           NH[:, h, :], NL[:, h, :]).then_inc(up_done, 1)
                    if k > 1 or w:
                        down(n - 2, b, k - 2)
                    if w == BATCHES - 1 and k == STEPS - 1:
                        down(n - 1, b, k - 1)
                        down(n, b, k)
                elif name == "centre":
                    h, kind = k
                    tiles = b * HALVES + h + 1
                    pe.wait_ge(ps.scaled, n)
                    if kind == "attn":
                        pe.wait_ge(q_ready, tiles)
                        pe.wait_ge(kvs_copied, b + 1)
                        pe.matmul(LNB[:], KVS[:, 0:P], QP[:], start=True, stop=True).then_inc(ps.source_done, 1)
                    elif kind in ("norm0", "norm3"):
                        if kind == "norm3":
                            pe.wait_ge(x_ready, tiles)
                        elif w or b:
                            pe.wait_ge(x_rest_loaded, 16)
                        else:
                            pe.wait_ge(g["x_first_loaded"], 16)
                        pe.matmul(LNB[:], centre[:], x_tile(X, b, h), start=True, stop=True).then_inc(ps.source_done, 1)
                    else:
                        pe.wait_ge(ya_ready if kind == "norm1" else yf_ready, tiles)
                        pe.matmul(LNB[:], centre[:], YA if kind == "norm1" else YF,
                                  start=True, stop=True).then_inc(ps.source_done, 1)
                elif name == "sums":
                    if k[1] == "attn":
                        pe_sums(pe, ps, 0, n, QP, KVS[:, P:P + 1])
                    else:
                        pe_sums(pe, ps, 0, n, SQ, mean_col[:])
                elif name == "turn":
                    pe_turn(pe, ps, 0, n)
                elif name == "spread":
                    pe_spread(pe, ps, 0, n)
                elif name == "keys":
                    h = k
                    pe.wait_ge(nl_done, b * HALVES + h + 1)
                    pe.wait_ge(attn_lo, 1)
                    banks_free(before)
                    for half in range(2):
                        for i in range(2):
                            t = slice((2 * half + i) * P, (2 * half + i + 1) * P)
                            mm = split3(pe, banks[6 + half][:, i * 2 * P:(i + 1) * 2 * P],
                                        NH[:, h, t], NL[:, h, t], AH[:, P:3 * P], AL[:, P:3 * P])
                        mm.then_inc(kv_done, 1)
                elif name == "kv_sum":
                    pe.wait_ge(k_ready, HALVES * (n + 1))
                    banks_free(before)
                    m = HALVES * GROUPS
                    for i in range(m):
                        mm = pe.matmul(banks[6][:, 0:P + 2], KV[:, i, 0:P], KV[:, i, P:2 * P + 2],
                                       start=(i == 0), stop=(i == m - 1))
                    mm.then_inc(kvs_done, 1)
                elif name == "query":
                    banks_free(before)
                    split3(pe, banks[7][:], attn_cols(0, 0), attn_cols(0, 1), NH[:, k, :], NL[:, k, :]).then_inc(q_done, 1)
                elif name == "ffn2":
                    h, c = k
                    m = H0_ROWS[c]
                    pe.wait_ge(lo_done, b * HALVES + h + 1)
                    banks_free(before)
                    for up in range(2):
                        mm = split3(pe, banks[6 + up][0:m, :], ffn2_cols(up, c, 0), ffn2_cols(up, c, 1), HI[:], LO[:])
                    mm.then_inc(gu2_done, 1)
                elif name == "ffn2_down":
                    banks_free(before)
                    for c in range(3):
                        m = H0_ROWS[c]
                        mm = pe.matmul(banks[6][:], WDA[0:m, c, :], H2[0:m, c, :], start=(c == 0), stop=(c == 2))
                    mm.then_inc(down2_done, 1)
                elif name == "logits":
                    banks_free(before)
                    pe.wait_ge(ps.scaled, before("spread"))
                    for j in range(GROUPS):
                        mm = pe.matmul(banks[6][:, j * EXPERTS:(j + 1) * EXPERTS], XS[:, j * P:(j + 1) * P], conf[:],
                                       start=True, stop=True)
                    mm.then_inc(logits_done, 1)

        pipeline.run(pe, body)


def routing(nc, A, sem, sb, ctx, g):
    Z, LG, XH, XL, combine, ident, banks, rows = (
        g[k] for k in ("Z", "LG", "XH", "XL", "combine", "ident", "banks", "rows"))
    NG = TOK // P
    WIDE = [P, NG, EXPERTS]

    TH = sb("TH", WIDE)
    BID = sb("BID", WIDE)
    LEFT = sb("LEFT", WIDE)
    EQ = sb("EQ", WIDE)
    ONE1 = sb("ONE1", WIDE)
    ONE2 = sb("ONE2", WIDE)
    CW = sb("CW", [P, EXPERTS, NG])
    M1, M2, F1, F2, DIF, EX, SUM, W1, W2 = (sb(n, [P, NG]) for n in ("M1", "M2", "F1", "F2", "DIF", "EX", "SUM", "W1", "W2"))
    CT = sb("CT", [P, 2, P])

    xh_done, xl_done = sem("xh_done"), sem("xl_done")
    biased, tanh_done, dif_done, exp_done, cw_done, cw_turned, ct_copied, stored, chain = (
        sem(n) for n in ("biased", "tanh_done", "dif_done", "exp_done", "cw_done", "cw_turned", "ct_copied", "stored", "chain"))

    block = ctx.enter_context(nc.Block())

    @block.sync
    def _(sp):
        sp.wait_ge(ct_copied, 2)
        sp.dma_start(combine.rearrange("e (j k) -> (e j) k", k=P).rearrange("(a r) k -> r a k", a=2),
                     CT[:]).then_inc(stored, 16)
        sp.wait_ge(stored, 16)

    @block.scalar
    def _(act):
        for i in range(BATCHES):
            act.activation(XH[:, i * SEQ:(i + 1) * SEQ], Z[:, i * SEQ:(i + 1) * SEQ], ACT.Copy).then_inc(xh_done, 1)
        act.wait_ge(biased, 1)
        act.activation(TH[:], LG[:], ACT.Tanh, scale=0.5).then_inc(tanh_done, 1)
        act.wait_ge(dif_done, 1)
        act.activation(EX[:], DIF[:], ACT.Exp).then_inc(exp_done, 1)
        for i in range(2):
            act.wait_ge(cw_turned, i + 1)
            act.activation(CT[:, i, :], banks[6 + i][:, 0:P], ACT.Copy).then_inc(ct_copied, 1)

    @block.gpsimd
    def _(pool):
        for i in range(BATCHES):
            pool.wait_ge(xh_done, i + 1)
            pool.tensor_tensor(XL[:, i * SEQ:(i + 1) * SEQ], Z[:, i * SEQ:(i + 1) * SEQ],
                               XH[:, i * SEQ:(i + 1) * SEQ].bitcast(F32), ALU.subtract).then_inc(xl_done, 1)

    @block.vector
    def _(dve):
        count = [0]

        def link(ins):
            count[0] += 1
            ins.then_inc(chain, 1)
            dve.wait_ge(chain, count[0])

        def wide(ap):
            return ap.unsqueeze(1).broadcast_to(WIDE)

        def deep(ap):
            return ap.unsqueeze(2).broadcast_to(WIDE)

        dve.wait_ge(g["later_loaded"], 16 * g["LATER"])
        dve.tensor_tensor(LG[:], LG[:], wide(rows[:, 0, :]), ALU.add).then_inc(biased, 1)
        dve.wait_ge(tanh_done, 1)
        link(dve.tensor_scalar(TH[:], TH[:], 0.5, 0.5, ALU.mult, ALU.add))
        link(dve.tensor_tensor(BID[:], TH[:], wide(rows[:, 1, :]), ALU.mult))
        link(dve.tensor_reduce(M1[:], BID[:], AX.X, ALU.max))
        link(dve.tensor_tensor(EQ[:], BID[:], deep(M1[:]), ALU.is_equal))
        link(dve.tensor_tensor(EQ[:], EQ[:], wide(rows[:, 2, :]), ALU.mult))
        link(dve.tensor_reduce(F1[:], EQ[:], AX.X, ALU.max))
        link(dve.tensor_tensor(ONE1[:], deep(F1[:]), wide(rows[:, 2, :]), ALU.is_equal))
        link(dve.scalar_tensor_tensor(LEFT[:], ONE1[:], -3.0e38, BID[:], ALU.mult, ALU.add))
        link(dve.tensor_reduce(M2[:], LEFT[:], AX.X, ALU.max))
        link(dve.tensor_tensor(EQ[:], LEFT[:], deep(M2[:]), ALU.is_equal))
        link(dve.tensor_tensor(EQ[:], EQ[:], wide(rows[:, 2, :]), ALU.mult))
        link(dve.tensor_reduce(F2[:], EQ[:], AX.X, ALU.max))
        link(dve.tensor_tensor(ONE2[:], deep(F2[:]), wide(rows[:, 2, :]), ALU.is_equal))
        dve.tensor_tensor(DIF[:], M2[:], M1[:], ALU.subtract).then_inc(dif_done, 1)
        dve.wait_ge(exp_done, 1)
        link(dve.tensor_scalar(SUM[:], EX[:], 1.0, None, ALU.add))
        link(dve.reciprocal(W1[:], SUM[:]))
        link(dve.tensor_tensor(W2[:], EX[:], W1[:], ALU.mult))
        link(dve.tensor_tensor(ONE1[:], ONE1[:], deep(W1[:]), ALU.mult))
        link(dve.tensor_tensor(ONE2[:], ONE2[:], deep(W2[:]), ALU.mult))
        dve.tensor_tensor(CW[:].rearrange("p e j -> p j e"), ONE1[:], ONE2[:], ALU.add).then_inc(cw_done, 1)

    @block.tensor
    def _(pe):
        pe.wait_ge(cw_done, 1)
        for i in range(2):
            pe.transpose(banks[6 + i][:, 0:P], CW[:].rearrange("p e j -> p (e j)")[:, i * P:(i + 1) * P],
                         ident[:]).then_inc(cw_turned, 1)


def second_layer_steps():
    STEP, EARLY = 8, 8
    EXPERT = {"expert": (-0.7815, 0.9691, 1.779, 3.2652, 3.812, 4.1715, 5.3975, 6.3719),
              "silu": (0.973, 2.189, 2.6671, 3.6978, 4.2202, 4.4767, 5.7484, 6.3721),
              "mult": (1.0505, 2.7098, 2.8568, 3.7867, 5.0731, 6.3155, 6.5471, 8.2899),
              "down": (3.7994, 4.1171, 4.9086, 5.3588, 6.406, 7.8886, 8.1299, 9.1349)}
    UNIT = {"unit": (6.3725, 10.8734), "added": (7.1077, 13.1334)}
    VIEWS = (-1.6983, -1.625, -0.9155)
    HAM = (3.6234, 4.1871, 4.2026, 4.3683, 5.1938, 6.1387, 6.1877, 6.288, 6.7929, 6.8537, 6.951, 7.3637, 7.5361)
    SCALINGS = {"A": {"centre": -6.9192, "sums": -5.3124, "turn": -4.1731, "spread": -3.7891, "halves": -3.0417},
                "C": {"centre": 20.5159, "sums": 21.073, "turn": 22.3861, "spread": 24.3288, "halves": 25.1889}}
    SINGLE = {"turns": 0.3093, "round": 0.9653, "cosines": 2.8401, "fold": 8.8998, "freq": 9.1708,
              "gain": 10.7082, "proj": 11.1879, "proj_add": 11.5491, "fc_a": 28.1135, "fc_b": 28.2295,
              "mproj": 28.9335, "mlp_add": 30.2162}
    ENDINGS = {5: 59.2, 6: 61.2, 7: 66.1}
    ENDING = {"centre": 0, "sums": 0.6, "turn": 1.4, "spread": 1.8, "halves": 2.2, "fc_a": 3.1, "fc_b": 3.4,
              "mproj": 3.9, "mlp_add": 4.4}
    LAST = {"freq": 64.95, "gain": 65.05, "proj": 65.7, "proj_add": 65.9}
    span, out = TILES * STEP, []
    chunks = PER_LAYER * TILES * CHUNKS
    for l in range(LAYERS):
        def put(place, name, k=0):
            out.append((l * span + place, name, l, k))

        for s in range(chunks):
            for name, places in EXPERT.items():
                put(s // STEP * STEP + places[s % STEP] - EARLY, name, s)
        for u in range(chunks // CHUNKS):
            for name, places in UNIT.items():
                put(u // 2 * STEP + places[u % 2] - EARLY, name, u)
        for e, (load, split, down) in enumerate(((-40, -16, -28.8), (-12, 16, 3.2))):
            put(load - EARLY, "load_up", e)
            put(split - EARLY, "split_expert", e)
            put(down - EARLY, "load_down", e)
        put(-24, "load_attn")
        if l == 0:
            put(0, "load_gain")
        for place, name in ((-5.27, "views"), (25.12, "fc")):
            put(place - 1, "keep_" + name)
            put(place, "prep_" + name)
            put(place + 0.8, "low_" + name)
        put(8.2, "prep_proj")
        put(22.28, "load_mproj")
        for t in range(TILES):
            a = t * STEP
            for j, place in enumerate(VIEWS):
                put(a + place, "views", (t, j))
            for i, place in enumerate(HAM):
                put(a + place, "ham", (t, i))
            single, scalings = dict(SINGLE), {kind: dict(places) for kind, places in SCALINGS.items()}
            if l == LAYERS - 1 and t in ENDINGS:
                for name, place in ENDING.items():
                    (scalings["C"] if name in scalings["C"] else single)[name] = ENDINGS[t] + place - a
                if t == TILES - 1:
                    single.update({name: place - a for name, place in LAST.items()})
            for name, place in single.items():
                put(a + place, name, t)
            for kind, places in scalings.items():
                for name, place in places.items():
                    put(a + place, name, (t, kind))
            if l == LAYERS - 1:
                u = TILES + t
                put(max(a + single["mlp_add"], u // 2 * STEP + UNIT["added"][u % 2] - EARLY) + 0.1, "out", t)
    return out


def second_layer(nc, A, sem, sb, ctx, g):
    X, Z, XH, XL, combine, ident, centre, mean_col, LC, hartley = (
        g[k] for k in ("X", "Z", "XH", "XL", "combine", "ident", "centre", "mean_col", "LC", "hartley"))
    banks, LNB, XC, SQ, XS, HI, LO, SH = (g[k] for k in ("banks", "LNB", "XC", "SQ", "XS", "HI", "LO", "SH"))
    split3 = g["split3"]
    pe_sums, act_var, pool_power, pe_turn, act_rows, pe_spread, act_centred = (
        g[k] for k in ("pe_sums", "act_var", "pool_power", "pe_turn", "act_rows", "pe_spread", "act_centred"))

    W = TILE + 2
    VIEWS = 6
    GUH = sb("GUH2", [P, PER_LAYER, 2 * FF], F32R)
    GUL = sb("GUL2", [P, PER_LAYER, 2 * FF], F32R)
    WD = sb("WD2", [P, PER_LAYER, CHUNKS, P])
    raw = sb("raw2", [P, 2 * FF])
    QRAW = sb("QRAW", [P, VIEWS * P])
    FRAW = sb("FRAW", [P, 4 * P])
    PRAW = sb("PRAW", [P, P])
    LQ = sb("LQ", [P, 16])
    LP = sb("LP", [P, 16])
    LF = sb("LF", [P, 16])
    BIAS = sb("BIAS", [P, 10])
    PB, MB, G1, B1, G2, B2 = 14, 15, 10, 11, 12, 13
    WQH = sb("WQH", [P, VIEWS * P], F32R)
    WQL = sb("WQL", [P, VIEWS * P], F32R)
    FCH = sb("FCH", [P, 4 * P], F32R)
    FCL = sb("FCL", [P, 4 * P], F32R)
    WP = sb("WP", [P, P])
    MP = sb("MP", [P, 4, P])
    GAIN = sb("GAIN", [P, SEQ])
    quarter = sb("quarter", [P, 1])
    rounder = sb("rounder", [P, 1])
    unrounder = sb("unrounder", [P, 1])
    QK = sb("QK", [P, 2, 4, W])
    V = sb("V", [P, 2, 4, W])
    TURNS = sb("TURNS", [P, 3, TILE])
    AM = sb("AM", [P, 4, TILE])
    TA = sb("TA", [P, 4, TILE])
    XG = sb("XG", [P, TILE])
    GE = sb("GE", [P, 4, TILE])
    CB = sb("CB", [P, 2, TILE])
    CO = sb("CO", [P, TILE])

    STEPS = PER_LAYER * TILES * CHUNKS
    UNITS = PER_LAYER * TILES
    ps = g["PerToken"](sem, 0)
    const_set, gain_loaded = sem("const_set"), sem("gain_loaded")
    attn_loaded, mp_loaded, gu_loaded = sem("attn_loaded"), sem("mp_loaded"), sem("gu_loaded")
    wd_loaded = [sem(f"wd2_loaded{e}") for e in range(PER_LAYER)]
    cb_loaded = [sem(f"cb_loaded{i}") for i in range(2)]
    q_cols, q_products, q_bias, q_hi, q_lo = (sem(n) for n in ("q_cols", "q_products", "q_bias", "q_hi", "q_lo"))
    f_cols, f_products, f_bias, f_hi, f_lo = (sem(n) for n in ("f_cols", "f_products", "f_bias", "f_hi", "f_lo"))
    p_cols, fold_product, fold_copied = sem("p_cols"), sem("fold_product"), sem("fold_copied")
    egu_hi, egu_lo = sem("egu_hi"), sem("egu_lo")
    proj_added, mlp_added = sem("proj_added"), sem("mlp_added")
    gate_done, up_done, silu_done, h_ready, down_done = (
        sem(n) for n in ("gate_done2", "up_done2", "silu_done2", "h_ready2", "down_done2"))
    o_read, x_added = sem("o_read"), sem("x_added")
    out_ready, out_stored = sem("out_ready"), sem("out_stored")
    view_done, view_read, edge_done, turns_done, rounded, reduced, cos_done, diff_done = (
        sem(n) for n in ("view_done", "view_read", "edge_done", "turns_done", "rounded", "reduced", "cos_done", "diff_done"))
    ham, fold_step = sem("ham"), sem("fold_step")
    freq_done, gained, proj_done = sem("freq_done"), sem("gained"), sem("proj_done")
    fc_done, gelu_done, mp_done = sem("fc_done"), sem("gelu_done"), sem("mp_done")
    HAM, FOLD = 13, 3
    FREE_QK = 8

    pipeline = Pipeline(second_layer_steps(), LAYERS, STEPS, cut=-8.787)

    def tile(ap, t):
        return ap[:, t * TILE:(t + 1) * TILE]

    def own(ap):
        return ap[..., 1:TILE + 1]

    def one(l):
        return bass.ds(l, 1)

    def hi_lo_used(engine, before):
        engine.wait_ge(view_done, 2 * before("views"))
        engine.wait_ge(fc_done, 2 * before("fc_a") + 2 * before("fc_b"))

    block = ctx.enter_context(nc.Block())

    @block.sync
    def _(sp):
        def body(w, layer):
            for name, l, k, before in pipeline.steps(w, layer):
                if name == "load_gain":
                    sp.dma_start(GAIN[:], A["c_gain"]).then_inc(gain_loaded, 16)
                elif name == "load_attn":
                    sp.wait_ge(q_lo, l)
                    sp.wait_ge(q_products, l)
                    sp.wait_ge(f_lo, l)
                    sp.wait_ge(f_products, l)
                    sp.wait_ge(fold_product, l)
                    for dst, src in ((QRAW, "w1_qkv"), (FRAW, "w1_fc"), (PRAW, "w1_proj")):
                        sp.dma_start(dst[:], A[src][one(l)].rearrange("a p n -> p (a n)")).then_inc(attn_loaded, 16)
                elif name == "load_up":
                    sp.wait_ge(egu_lo, PER_LAYER * l + k)
                    sp.dma_start(raw[:], A["w1_gu"][one(l * PER_LAYER + k)].rearrange("a p n -> p (a n)")).then_inc(gu_loaded, 16)
                elif name == "load_down":
                    if k:
                        sp.wait_ge(down_done, l * STEPS)
                    elif w or l:
                        sp.wait_ge(down_done, (l - 1) * STEPS + STEPS // 2)
                    sp.dma_start(WD[:, k, :, :], A["w1_d"][one(l * PER_LAYER + k)].rearrange("a p c n -> p (a c) n")
                                 ).then_inc(wd_loaded[k], 16)
                elif name == "load_mproj":
                    sp.wait_ge(mp_done, TILES * l)
                    sp.dma_start(MP[:], A["w1_mproj"][one(l)].rearrange("a p c n -> p (a c) n")).then_inc(mp_loaded, 16)
                elif name == "expert" and k % CHUNKS == 0:
                    u = k // CHUNKS
                    e, t = u // TILES, u % TILES
                    sp.wait_ge(o_read, less(UNITS * l + u, 1))
                    sp.dma_start(CB[:, u % 2, :],
                                 combine[one(l * PER_LAYER + e),
                                         t * TILE:(t + 1) * TILE].broadcast_to([P, TILE])).then_inc(cb_loaded[u % 2], 16)
                elif name == "out":
                    sp.wait_ge(out_ready, k + 1)
                    sp.dma_start(A["outT"][:, k * TILE:(k + 1) * TILE], tile(X, k)).then_inc(out_stored, 16)

        pipeline.run(sp, body)
        sp.wait_ge(out_stored, 16 * TILES)

    @block.scalar
    def _(act):
        act.wait_ge(const_set, 1)

        def body(w, layer):
            for name, l, k, before in pipeline.steps(w, layer):
                n = before(name)
                if name == "prep_views":
                    act.wait_ge(attn_loaded, 48 * l + 48)
                    act.wait_ge(q_cols, l + 1)
                    act.wait_ge(view_done, VIEWS * TILES * l)
                    act.activation(WQH[:], QRAW[:], ACT.Copy, scale=LQ[:, G1:G1 + 1]).then_inc(q_hi, 1)
                elif name == "prep_proj":
                    act.wait_ge(fold_product, l + 1)
                    act.wait_ge(proj_done, TILES * l)
                    act.activation(WP[:], banks[7][:, 0:P], ACT.Copy, scale=1.0 / P).then_inc(fold_copied, 1)
                elif name == "prep_fc":
                    act.wait_ge(attn_loaded, 48 * l + 48)
                    act.wait_ge(f_cols, l + 1)
                    act.wait_ge(fc_done, 4 * TILES * l)
                    act.activation(FCH[:], FRAW[:], ACT.Copy, scale=LF[:, G2:G2 + 1]).then_inc(f_hi, 1)
                elif name == "split_expert":
                    act.wait_ge(gu_loaded, (n + 1) * 16)
                    if k:
                        act.wait_ge(up_done, l * STEPS)
                    elif w or l:
                        act.wait_ge(up_done, (l - 1) * STEPS + STEPS // 2)
                    act.activation(GUH[:, k, :], raw[:], ACT.Copy).then_inc(egu_hi, 1)
                elif name == "silu":
                    act.wait_ge(gate_done, n + 1)
                    act.wait_ge(down_done, less(n, 3))
                    act.activation(SH[:, k % 4, :], banks[k % 2][:], ACT.Silu).then_inc(silu_done, 1)
                elif name == "centre":
                    act_centred(act, ps, 0, n)
                elif name == "sums":
                    act_var(act, ps, 0, n, g["eps_col"][:])
                elif name == "turn":
                    act_rows(act, ps, 0, n)
                elif name == "halves":
                    act.wait_ge(ps.scaled, n + 1)
                    hi_lo_used(act, before)
                    act.activation(HI[:], XS[:], ACT.Copy).then_inc(ps.hi_done, 1)
                elif name == "views":
                    t, j = k
                    views_of = l * TILES + t
                    if j == 0:
                        if t or w or l:
                            act.wait_ge(ham, (views_of - 1) * HAM + FREE_QK)
                        if t % HALVES:
                            act.wait_ge(view_read, 2 * n)
                            act.activation(QK[:, :, 0, 0:1], QK[:, :, 0, TILE:TILE + 1], ACT.Copy)
                            act.activation(V[:, t % 2, 0, 0:1], V[:, (t - 1) % 2, 0, TILE:TILE + 1], ACT.Copy).then_inc(edge_done, 1)
                            act.wait_ge(edge_done, views_of + 1)
                        act.wait_ge(q_bias, l + 1)
                    outs = [QK[:, 0, 0, :], QK[:, 1, 0, :], V[:, t % 2, 0, :],
                            QK[:, 0, 2, :], QK[:, 1, 2, :], V[:, t % 2, 2, :]]
                    for i in range(2):
                        act.wait_ge(view_done, 2 * n + i + 1)
                        act.activation(own(outs[2 * j + i]), banks[6 + i][:], ACT.Identity,
                                       bias=BIAS[:, 2 * j + i:2 * j + i + 1]).then_inc(view_read, 1)
                    if j == 2 and t % HALVES == 0:
                        act.wait_ge(view_read, 2 * n + 2)
                        act.activation(QK[:, :, 0, 0:1], QK[:, :, 0, 1:2], ACT.Copy)
                        act.activation(V[:, t % 2, 0, 0:1], V[:, t % 2, 0, 1:2], ACT.Copy).then_inc(edge_done, 1)
                elif name == "turns":
                    act.wait_ge(view_read, VIEWS * (n + 1))
                    act.activation(own(QK[:, :, 3, :]), own(QK[:, :, 0, :]), ACT.Identity, bias=quarter[:],
                                   scale=1.0 / (2 * np.pi))
                    act.activation(own(V[:, k % 2, 3, :]), own(V[:, k % 2, 0, :]), ACT.Identity, bias=quarter[:],
                                   scale=1.0 / (2 * np.pi)).then_inc(turns_done, 1)
                elif name == "round":
                    act.wait_ge(turns_done, n + 1)
                    act.wait_ge(cos_done, n)
                    act.activation(TURNS[:, 0:2, :], own(QK[:, :, 3, :]), ACT.Identity, bias=rounder[:])
                    act.activation(TURNS[:, 2, :], own(V[:, k % 2, 3, :]), ACT.Identity, bias=rounder[:]).then_inc(rounded, 1)
                    act.wait_ge(rounded, 2 * n + 1)
                    act.activation(TURNS[:], TURNS[:], ACT.Identity, bias=unrounder[:]).then_inc(rounded, 1)
                elif name == "cosines":
                    act.wait_ge(reduced, n + 1)
                    act.activation(own(QK[:, :, 3, :]), TURNS[:, 0:2, :], ACT.Sin, scale=-TURN)
                    act.activation(own(V[:, k % 2, 3, :]), TURNS[:, 2, :], ACT.Sin, scale=-TURN).then_inc(cos_done, 1)
                elif name == "fc_b":
                    act.wait_ge(mp_done, n)
                    act.wait_ge(f_bias, l + 1)
                    for c in range(4):
                        act.wait_ge(fc_done, 4 * n + c + 1)
                        act.activation(GE[:, c, :], banks[6 + c % 2][:], ACT.Gelu,
                                       bias=BIAS[:, VIEWS + c:VIEWS + c + 1]).then_inc(gelu_done, 1)

        pipeline.run(act, body)

    @block.gpsimd
    def _(pool):
        def body(w, layer):
            for name, l, k, before in pipeline.steps(w, layer):
                n = before(name)
                if name == "split_expert":
                    pool.wait_ge(egu_hi, n + 1)
                    pool.tensor_tensor(GUL[:, k, :], raw[:], GUH[:, k, :].bitcast(F32),
                                       ALU.subtract).then_inc(egu_lo, 1)
                elif name == "added":
                    pool.wait_ge(o_read, n + 1)
                    pool.wait_ge(x_added, n)
                    t = k % TILES
                    pool.tensor_tensor(tile(X, t), tile(X, t), CO[:], ALU.add).then_inc(x_added, 1)
                elif name == "sums":
                    pool_power(pool, ps, 0, n, g["power_half"])
                elif name == "halves":
                    pool.wait_ge(ps.hi_done, n + 1)
                    hi_lo_used(pool, before)
                    pool.tensor_tensor(LO[:], XS[:], HI[:].bitcast(F32), ALU.subtract).then_inc(ps.lo_done, 1)
                elif name == "round":
                    pool.wait_ge(rounded, 2 * n + 2)
                    pool.tensor_tensor(TURNS[:, 0:2, :], TURNS[:, 0:2, :], own(QK[:, :, 3, :]), ALU.subtract)
                    pool.tensor_tensor(TURNS[:, 2, :], TURNS[:, 2, :], own(V[:, k % 2, 3, :]),
                                       ALU.subtract).then_inc(reduced, 1)
                elif name == "fold":
                    pool.wait_ge(ham, (n + 1) * HAM)
                    pool.tensor_tensor(TA[:, 0, :], TA[:, 0, :], TA[:, 1, :], ALU.subtract).then_inc(fold_step, 1)
                    pool.tensor_tensor(TA[:, 2, :], TA[:, 2, :], TA[:, 3, :], ALU.add).then_inc(fold_step, 1)
                    pool.wait_ge(fold_step, n * FOLD + 2)
                    pool.wait_ge(proj_done, n)
                    pool.tensor_tensor(XG[:], TA[:, 0, :], TA[:, 2, :], ALU.subtract).then_inc(fold_step, 1)

        pipeline.run(pool, body)

    @block.vector
    def _(dve):
        dve.memset(rounder[:], ROUND)
        dve.memset(unrounder[:], -ROUND)
        dve.memset(quarter[:], 0.25).then_inc(const_set, 1)

        def pair(ap, a, b):
            return ap[:, a:b + 1:b - a, :]

        def hamilton(n, t, i):
            q = own(QK[:, 0, :, :])

            def k_(j):
                return own(QK[:, 1, j, :]).unsqueeze(1).broadcast_to([P, 4, TILE])

            base = n * HAM
            ADD, SUB = ALU.add, ALU.subtract
            sums = {2: ((1, 2), (0, 3), ADD), 3: ((0, 3), (1, 2), SUB),
                    5: ((2, 3), (0, 1), ADD), 6: ((0, 1), (2, 3), SUB)}
            if i == 0:
                dve.wait_ge(cos_done, n + 1)
                dve.wait_ge(diff_done, 2 * (n + 1))
                dve.wait_ge(ham, base)
                ins = dve.tensor_tensor(AM[:], q, k_(0), ALU.mult)
            elif i in (1, 4, 7):
                if i == 1:
                    dve.wait_ge(fold_step, n * FOLD)
                else:
                    dve.wait_ge(ham, base + i)
                ins = dve.tensor_tensor(TA[:], q, k_(1 + i // 3), ALU.mult)
            elif i in sums:
                dve.wait_ge(ham, base + (2 if i < 4 else 5))
                d, s, op = sums[i]
                ins = dve.tensor_tensor(pair(AM, *d), pair(AM, *d), pair(TA, *s), op)
            elif i < 12:
                dve.wait_ge(ham, base + 8)
                d, s, op = ((3, 0, ADD), (2, 1, SUB), (1, 2, ADD), (0, 3, SUB))[i - 8]
                ins = dve.tensor_tensor(AM[:, d, :], AM[:, d, :], TA[:, s, :], op)
            else:
                dve.wait_ge(ham, base + 12)
                ins = dve.tensor_tensor(TA[:], AM[:], own(V[:, t % 2, :, :]), ALU.mult)
            ins.then_inc(ham, 1)

        def keep_columns(dve, out, l):
            columns = LC[:, one(l), :].rearrange("p a c -> p (a c)")
            return dve.tensor_tensor(out[:], columns, columns, ALU.max)

        def body(w, layer):
            for name, l, k, before in pipeline.steps(w, layer):
                n = before(name)
                if name == "keep_views":
                    dve.wait_ge(q_products, l)
                    dve.wait_ge(q_hi, l)
                    keep_columns(dve, LQ, l).then_inc(q_cols, 1)
                elif name == "prep_views":
                    dve.wait_ge(view_read, VIEWS * TILES * l)
                    dve.wait_ge(q_cols, l + 1)
                    dve.wait_ge(q_products, l + 1)
                    dve.tensor_tensor(BIAS[:, 0:VIEWS], banks[6][:, 0:VIEWS], LQ[:, 0:VIEWS], ALU.add).then_inc(q_bias, 1)
                elif name == "low_views":
                    dve.wait_ge(q_hi, l + 1)
                    dve.scalar_tensor_tensor(WQL[:], QRAW[:], LQ[:, G1:G1 + 1], WQH[:].bitcast(F32),
                                             ALU.mult, ALU.subtract).then_inc(q_lo, 1)
                elif name == "prep_proj":
                    dve.wait_ge(proj_added, TILES * l)
                    keep_columns(dve, LP, l).then_inc(p_cols, 1)
                elif name == "keep_fc":
                    dve.wait_ge(mlp_added, TILES * l)
                    dve.wait_ge(f_products, l)
                    dve.wait_ge(f_hi, l)
                    keep_columns(dve, LF, l).then_inc(f_cols, 1)
                elif name == "prep_fc":
                    dve.wait_ge(gelu_done, 4 * TILES * l)
                    dve.wait_ge(f_cols, l + 1)
                    dve.wait_ge(f_products, l + 1)
                    dve.tensor_tensor(BIAS[:, VIEWS:], banks[6][:, 0:4], LF[:, VIEWS:VIEWS + 4], ALU.add).then_inc(f_bias, 1)
                elif name == "low_fc":
                    dve.wait_ge(f_hi, l + 1)
                    dve.scalar_tensor_tensor(FCL[:], FRAW[:], LF[:, G2:G2 + 1], FCH[:].bitcast(F32),
                                             ALU.mult, ALU.subtract).then_inc(f_lo, 1)
                elif name == "mult":
                    dve.wait_ge(silu_done, n + 1)
                    dve.wait_ge(up_done, n + 1)
                    dve.tensor_tensor(SH[:, k % 4, :], SH[:, k % 4, :], banks[2 + k % 2][:],
                                      ALU.mult).then_inc(h_ready, 1)
                elif name == "unit":
                    dve.wait_ge(down_done, (n + 1) * CHUNKS)
                    dve.wait_ge(cb_loaded[k % 2], (n - k % 2) * 8 + 16)
                    dve.wait_ge(x_added, n)
                    dve.tensor_tensor(CO[:], banks[4][:], CB[:, k % 2, :], ALU.mult).then_inc(o_read, 1)
                elif name == "spread":
                    dve.wait_ge(ps.spread, n + 1)
                    dve.wait_ge(ps.lo_done, n)
                    dve.tensor_tensor(XS[:], XC[:], LNB[:], ALU.mult).then_inc(ps.scaled, 1)
                elif name == "turns":
                    dve.wait_ge(edge_done, n + 1)
                    dve.wait_ge(view_read, (n + 1) * VIEWS)
                    for buf, side in ((QK, slice(0, 2)), (V, slice(k % 2, k % 2 + 1))):
                        zero = buf[:, side, 0, :]
                        dve.tensor_tensor(own(buf[:, side, 1, :]), own(zero), zero[..., 0:TILE],
                                          ALU.subtract).then_inc(diff_done, 1)
                elif name == "ham":
                    hamilton(l * TILES + k[0], *k)
                elif name == "gain":
                    dve.wait_ge(gain_loaded, 16)
                    dve.wait_ge(freq_done, n + 1)
                    s = (k % HALVES) * TILE
                    dve.tensor_tensor(XG[:], banks[6][:], GAIN[:, s:s + TILE], ALU.mult).then_inc(gained, 1)
                elif name == "proj_add":
                    dve.wait_ge(proj_done, n + 1)
                    dve.wait_ge(p_cols, l + 1)
                    dve.scalar_tensor_tensor(tile(Z, k), banks[7][:], LP[:, PB:PB + 1], tile(Z, k),
                                             ALU.add, ALU.add).then_inc(proj_added, 1)
                elif name == "mlp_add":
                    dve.wait_ge(mp_done, n + 1)
                    dve.wait_ge(f_cols, l + 1)
                    dve.scalar_tensor_tensor(tile(Z, k), banks[7][:], LF[:, MB:MB + 1], tile(Z, k),
                                             ALU.add, ALU.add).then_inc(mlp_added, 1)
                elif name == "out":
                    dve.wait_ge(x_added, UNITS * LAYERS - TILES + k + 1)
                    dve.wait_ge(mlp_added, TILES * (LAYERS - 1) + k + 1)
                    dve.tensor_tensor(tile(X, k), tile(X, k), tile(Z, k), ALU.add).then_inc(out_ready, 1)

        pipeline.run(dve, body)

    @block.tensor
    def _(pe):
        def banks_free(before):
            pe.wait_ge(view_read, 2 * before("views"))
            pe.wait_ge(gained, before("gain"))
            pe.wait_ge(proj_added, before("proj_add"))
            pe.wait_ge(mlp_added, before("mlp_add"))
            pe.wait_ge(gelu_done, 4 * before("fc_b"))
            pe.wait_ge(q_bias, before("prep_views"))
            pe.wait_ge(f_bias, before("prep_fc"))
            pe.wait_ge(fold_copied, before("prep_proj"))

        def body(w, layer):
            for name, l, k, before in pipeline.steps(w, layer):
                n = before(name)
                if name == "prep_views":
                    pe.wait_ge(attn_loaded, 48 * l + 48)
                    pe.wait_ge(q_cols, l + 1)
                    banks_free(before)
                    for i in range(VIEWS):
                        mm = pe.matmul(banks[6][:, i:i + 1], QRAW[:, i * P:(i + 1) * P], LQ[:, B1:B1 + 1], start=True, stop=True)
                    mm.then_inc(q_products, 1)
                elif name == "prep_fc":
                    pe.wait_ge(attn_loaded, 48 * l + 48)
                    pe.wait_ge(f_cols, l + 1)
                    banks_free(before)
                    for i in range(4):
                        mm = pe.matmul(banks[6][:, i:i + 1], FRAW[:, i * P:(i + 1) * P],
                                       LF[:, B2:B2 + 1], start=True, stop=True)
                    mm.then_inc(f_products, 1)
                elif name == "prep_proj":
                    pe.wait_ge(attn_loaded, 48 * l + 48)
                    banks_free(before)
                    pe.matmul(banks[7][:, 0:P], hartley[:], PRAW[:], start=True, stop=True).then_inc(fold_product, 1)
                elif name == "expert":
                    u, c = k // CHUNKS, k % CHUNKS
                    e, t = u // TILES, u % TILES
                    if t == 0 and c == 0:
                        pe.wait_ge(egu_lo, PER_LAYER * l + e + 1)
                    a = c * P
                    pe.wait_ge(silu_done, less(n, 1))
                    split3(pe, banks[k % 2][:], GUH[:, e, a:a + P], GUL[:, e, a:a + P],
                           tile(XH, t), tile(XL, t)).then_inc(gate_done, 1)
                    pe.wait_ge(h_ready, less(n, 1))
                    a += FF
                    split3(pe, banks[2 + k % 2][:], GUH[:, e, a:a + P], GUL[:, e, a:a + P],
                           tile(XH, t), tile(XL, t)).then_inc(up_done, 1)
                elif name == "down":
                    u, c = k // CHUNKS, k % CHUNKS
                    pe.wait_ge(h_ready, n + 1)
                    if c == 0:
                        pe.wait_ge(o_read, l * UNITS + u)
                        if u % TILES == 0:
                            pe.wait_ge(wd_loaded[u // TILES], (l + 1) * 16)
                    pe.matmul(banks[4][:], WD[:, u // TILES, c, :], SH[:, k % 4, :],
                              start=(c == 0), stop=(c == CHUNKS - 1)).then_inc(down_done, 1)
                elif name == "centre":
                    t, kind = k
                    pe.wait_ge(ps.scaled, n)
                    if kind == "C":
                        pe.wait_ge(proj_added, TILES * l + t + 1)
                    elif w or l:
                        pe.wait_ge(mlp_added, TILES * (l - 1) + t + 1)
                    pe.matmul(LNB[:], centre[:], tile(Z, t), start=True, stop=True).then_inc(ps.source_done, 1)
                elif name == "sums":
                    pe_sums(pe, ps, 0, n, SQ, mean_col[:])
                elif name == "turn":
                    pe_turn(pe, ps, 0, n)
                elif name == "spread":
                    pe_spread(pe, ps, 0, n)
                elif name == "views":
                    t, j = k
                    pe.wait_ge(ps.lo_done, before("halves"))
                    pe.wait_ge(q_lo, l + 1)
                    banks_free(before)
                    for i in range(2):
                        a = (2 * j + i) * P
                        split3(pe, banks[6 + i][:], WQH[:, a:a + P], WQL[:, a:a + P], HI[:], LO[:]).then_inc(view_done, 1)
                elif name == "freq":
                    pe.wait_ge(fold_step, FOLD * (n + 1))
                    banks_free(before)
                    pe.matmul(banks[6][:], hartley[:], XG[:], start=True, stop=True).then_inc(freq_done, 1)
                elif name == "proj":
                    pe.wait_ge(gained, n + 1)
                    pe.wait_ge(fold_copied, l + 1)
                    banks_free(before)
                    pe.matmul(banks[7][:], WP[:], XG[:], start=True, stop=True).then_inc(proj_done, 1)
                elif name in ("fc_a", "fc_b"):
                    pe.wait_ge(ps.lo_done, before("halves"))
                    pe.wait_ge(f_lo, l + 1)
                    banks_free(before)
                    for i in range(2):
                        c = i
                        if name == "fc_b":
                            c = i + 2
                            pe.wait_ge(gelu_done, 4 * n + i + 1)
                        split3(pe, banks[6 + i][:], FCH[:, c * P:(c + 1) * P], FCL[:, c * P:(c + 1) * P],
                               HI[:], LO[:]).then_inc(fc_done, 1)
                elif name == "mproj":
                    pe.wait_ge(mp_loaded, (l + 1) * 16)
                    banks_free(before)
                    for c in range(4):
                        mm = pe.matmul(banks[7][:], MP[:, c, :], GE[:, c, :], start=(c == 0), stop=(c == 3))
                    mm.then_inc(mp_done, 1)

        pipeline.run(pe, body)


def _constants():
    pick = np.zeros((2 * GROUPS, GROUPS, P), np.float32)
    for i in range(GROUPS):
        pick[i, i] = pick[GROUPS + i, i] = 1.0

    def cas(n):
        a = 2 * np.pi * np.outer(np.arange(n), np.arange(n)) / n
        return np.cos(a) + np.sin(a)

    heads, dims = 16, 8
    ks = np.fft.fftfreq(SEQ)[None, None, :]
    kh = np.fft.fftfreq(heads)[:, None, None]
    kd = np.fft.fftfreq(dims)[None, :, None]
    km = np.sqrt(ks ** 2 + kh ** 2 + kd ** 2 + 1e-10)
    gain = np.cos(np.arctan(np.log(km + 1e-10))).reshape(P, SEQ)
    lam = np.arange(SEQ, dtype=np.float32) / np.float32(SEQ)
    t = np.arange(SEQ, dtype=np.float32) * np.float32(0.1)
    phase = t - np.float32(2.0) * lam + np.float32(0.5) * lam ** 2
    modulation = np.sin(t + lam) * np.cos(phase)
    return {
        "c_ident": np.eye(P, dtype=np.float32),
        "c_centre": (np.eye(P) - 1.0 / P).astype(np.float32),
        "c_pick": pick,
        "c_hartley": np.kron(cas(heads), cas(dims)).astype(np.float32),
        "c_gain": (gain * (1.0 + 0.1 * modulation)).astype(np.float32),
        "c_rank": np.arange(EXPERTS, 0, -1, dtype=np.float32)[None],
    }


def _layout(i):
    a = {k: np.asarray(v) for k, v in i.items()}
    heads, dims = 16, 8
    head_before = (np.arange(heads) - 1) % heads

    def views(x):
        x = x.reshape(*x.shape[:-1], heads, 3, dims)
        parts = [x[..., j, :] for j in range(3)]
        parts += [p[..., head_before, :] for p in parts]
        return [p.reshape(*p.shape[:-2], P) for p in parts]

    cols0 = np.zeros((P, 12), np.float32)
    cols0[:, 0] = a["L0_attn_bqkv"][:P]
    for c, m in enumerate(H0_ROWS):
        cols0[:m, 1 + c] = a["L0_attn_bg"][c * P:c * P + m]
        cols0[:m, 4 + c] = a["L0_attn_bu"][c * P:c * P + m]
    for c, n in ((7, "bd"), (8, "g1"), (9, "b1"), (10, "g2"), (11, "b2")):
        cols0[:, c] = a["L0_attn_" + n]
    cols1 = np.zeros((P, LAYERS, 16), np.float32)
    for c, v in enumerate(views(a["L1_attn_attn_b"])):
        cols1[:, :, c] = v.T
    cols1[:, :, 6:10] = a["L1_attn_fc_b"].reshape(LAYERS, 4, P).transpose(2, 0, 1)
    for c, n in ((10, "ln1_w"), (11, "ln1_b"), (12, "ln2_w"), (13, "ln2_b"), (14, "aproj_b"), (15, "mproj_b")):
        cols1[:, :, c] = a["L1_attn_" + n].T
    return {
        "xT": a["L0_attn_x"].reshape(TOK, P).T,
        "w0_attn": np.concatenate([a["L0_attn_Wqkv"], a["L0_attn_Wg"], a["L0_attn_Wu"]], 1),
        "w0_down": a["L0_attn_Wd"],
        "kv_bias": a["L0_attn_bqkv"][None, P:],
        "cols0": cols0,
        "w0_gud": np.concatenate([a["L0_ffn_Wg"], a["L0_ffn_Wu"], a["L0_ffn_Wd"].reshape(EXPERTS, CHUNKS, P, P)
                                  .transpose(0, 2, 1, 3).reshape(EXPERTS, P, CHUNKS * P)], 2),
        "conf_w": a["L1_ffn_conf_w"].T,
        "conf_b": a["L1_ffn_conf_b"][None],
        "wealth": a["L1_ffn_wealth"][None],
        "w1_qkv": np.concatenate(views(a["L1_attn_attn_w"]), -1),
        "w1_fc": a["L1_attn_fc_w"],
        "w1_proj": a["L1_attn_aproj_w"],
        "w1_mproj": a["L1_attn_mproj_w"].reshape(LAYERS, 4, P, P).transpose(0, 2, 1, 3),
        "cols1": cols1,
        "w1_gu": np.concatenate([a["L1_ffn_gate_w"], a["L1_ffn_up_w"]], 1).transpose(0, 2, 1),
        "w1_d": a["L1_ffn_down_w"].transpose(0, 2, 1).reshape(EXPERTS, CHUNKS, P, P).transpose(0, 2, 1, 3),
    }


def kernel(**inputs):
    import concourse.bacc as _bacc
    from concourse.bass_utils import run_bass_kernel_spmd as _run

    nc = _bacc.Bacc("TRN2", target_bir_lowering=False, num_devices=1)
    arrays, A = {}, {}
    for name, a in {**_layout(inputs), **_constants()}.items():
        a = np.ascontiguousarray(a)
        arrays[f"in_{name}"] = a
        A[name] = nc.dram_tensor(f"in_{name}", a.shape, mybir.dt.from_np(a.dtype), kind="ExternalInput").ap()
    A["outT"] = nc.dram_tensor("outT", (P, TOK), F32, kind="ExternalOutput").ap()
    kernel_program(nc, A)
    got = _run(nc, [arrays], core_ids=[0]).results[0]["outT"]
    return np.ascontiguousarray(got.T).reshape(BATCHES, SEQ, P)
```
